# Optimizing a Trainium2 kernel written in Bass

```python
import numpy as np
import jax
import jax.numpy as jnp

def _softmax(x, axis=-1):
    return jax.nn.softmax(x, axis=axis)

def _gelu(x):
    return jax.nn.gelu(x, approximate=True)

def _silu(x):
    return jax.nn.silu(x)

def _sigmoid(x):
    return jax.nn.sigmoid(x)

def _layernorm(x, axis=-1, eps=1e-05):
    m = jnp.mean(x, axis=axis, keepdims=True)
    v = jnp.var(x, axis=axis, keepdims=True)
    return (x - m) / jnp.sqrt(v + eps)

def _scatter_add(tgt, idx, src, axis=0):
    return tgt.at[idx].add(src)

def _segment_sum(src, seg, n):
    return jax.ops.segment_sum(src, seg, n)
kernel_name = 'mk_cond_resid_d4_seqx_r4_b0f486'

def setup_inputs(seed: int=0):
    np.random.seed(seed)
    _w = jnp.asarray

    def _rec_inputs():
        import jax
        import jax.numpy as jnp
        _rk = jax.random.key(seed)
        x = -5.13e-06 + 0.01765 * jax.random.normal(jax.random.fold_in(_rk, 1), (4, 512, 256), jnp.float32)
        _lenS = 512 - jax.random.randint(jax.random.fold_in(_rk, 7), (4,), 0, max(1, 512 // 4) + 1, jnp.int32)
        _lenS2 = 512 - jax.random.randint(jax.random.fold_in(_rk, 8), (4,), 0, max(1, 512 // 4) + 1, jnp.int32)
        cond_1024 = 0.0061147 + 1.02565 * jax.random.normal(jax.random.fold_in(_rk, 11), (4, 256), jnp.float32)
        return (x, cond_1024)
    x, cond_1024 = _rec_inputs()

    def _L0_cond_setup():
        import math
        import jax, jax.numpy as jnp
        import numpy as np
        EPS = 1e-07
        MAX_TANH_ARG = 1.0 - 1e-05

        def _norm(x):
            return jnp.sqrt(jnp.sum(x * x, axis=-1, keepdims=True)).clip(EPS)

        def logmap0(x):
            n = _norm(x)
            return jnp.arctanh(jnp.clip(n, EPS, MAX_TANH_ARG)) * x / n

        def expmap0(v):
            n = _norm(v)
            return jnp.tanh(n) * v / n

        def mobius_add(x, y):
            x2 = jnp.sum(x * x, -1, keepdims=True)
            y2 = jnp.sum(y * y, -1, keepdims=True)
            xy = jnp.sum(x * y, -1, keepdims=True)
            num = (1 + 2 * xy + y2) * x + (1 - x2) * y
            den = (1 + 2 * xy + x2 * y2).clip(EPS)
            return num / den

        def plin(x, w, b):
            return expmap0(logmap0(x) @ w + b)

        def layer_norm(x, eps=1e-06):
            m = x.mean(-1, keepdims=True)
            v = ((x - m) ** 2).mean(-1, keepdims=True)
            return (x - m) / jnp.sqrt(v + eps)

        def _beta(a, b):
            return math.exp(math.lgamma(a) + math.lgamma(b) - math.lgamma(a + b))
        D, H, FF = (256, 16, 1024)
        HD = D // H
        BETA_N = _beta(D / 2, 0.5)
        BETA_H = _beta(HD / 2, 0.5)

        def _to_heads(p):
            B, S, _ = p.shape
            t = logmap0(p).reshape(B, S, H, HD) * (BETA_H / BETA_N)
            return expmap0(jnp.transpose(t, (0, 2, 1, 3)))

        def _from_heads(ph):
            B, _, S, _ = ph.shape
            t = logmap0(ph) * (BETA_N / BETA_H)
            t = jnp.transpose(t, (0, 2, 1, 3)).reshape(B, S, D)
            return expmap0(t)
        key = jax.random.key(seed)
        ks = jax.random.split(key, 20)
        B, S = (4, 256)
        x = expmap0(0.02 * jax.random.normal(ks[0], (B, S, D), jnp.float32))
        t_emb = jax.random.normal(ks[1], (B, 1, D), jnp.float32)
        g = lambda k, sh: 0.02 * jax.random.normal(k, sh, jnp.float32)
        return {'x': x, 't_emb': t_emb, 'w_q': g(ks[2], (D, D)), 'b_q': jnp.zeros((D,), jnp.float32), 'w_k': g(ks[3], (D, D)), 'b_k': jnp.zeros((D,), jnp.float32), 'w_v': g(ks[4], (D, D)), 'b_v': jnp.zeros((D,), jnp.float32), 'w_o': g(ks[5], (D, D)), 'b_o': jnp.zeros((D,), jnp.float32), 'w_f1': g(ks[6], (D, FF)), 'b_f1': jnp.zeros((FF,), jnp.float32), 'w_f2': g(ks[7], (FF, D)), 'b_f2': jnp.zeros((D,), jnp.float32), 'w_ada': g(ks[8], (D, 6 * D)), 'b_ada': jnp.zeros((6 * D,), jnp.float32)}
    _L0_cond_all = _L0_cond_setup()
    _L0_cond_in = {k: v for k, v in _L0_cond_all.items() if k in ('w_q', 'b_q', 'w_k', 'b_k', 'w_v', 'b_v', 'w_o', 'b_o', 'w_f1', 'b_f1', 'w_f2', 'b_f2', 'w_ada', 'b_ada')}
    del _L0_cond_all

    def _L1_cond_setup():
        import jax, jax.numpy as jnp
        import numpy as np
        B, T, D_IN, V_IN, E = (64, 128, 256, 256, 256)
        key = jax.random.key(seed)
        ks = jax.random.split(key, 16)
        s = 0.01
        return {'video': jax.random.normal(ks[0], (B, V_IN), jnp.float32), 'seq': jax.random.normal(ks[1], (B, T, D_IN), jnp.float32), 'W_z': jax.random.normal(ks[2], (D_IN, E), jnp.float32) * s, 'U_z': jax.random.normal(ks[3], (E, E), jnp.float32) * s, 'C_z': jax.random.normal(ks[4], (V_IN, E), jnp.float32) * s, 'b_z': jnp.zeros((E,), jnp.float32), 'W_r': jax.random.normal(ks[5], (D_IN, E), jnp.float32) * s, 'U_r': jax.random.normal(ks[6], (E, E), jnp.float32) * s, 'C_r': jax.random.normal(ks[7], (V_IN, E), jnp.float32) * s, 'b_r': jnp.zeros((E,), jnp.float32), 'W': jax.random.normal(ks[8], (D_IN, E), jnp.float32) * s, 'U': jax.random.normal(ks[9], (E, E), jnp.float32) * s, 'C': jax.random.normal(ks[10], (V_IN, E), jnp.float32) * s, 'b': jnp.zeros((E,), jnp.float32)}
    _L1_cond_all = _L1_cond_setup()
    _L1_cond_in = {k: v for k, v in _L1_cond_all.items() if k in ('W_z', 'U_z', 'C_z', 'b_z', 'W_r', 'U_r', 'C_r', 'b_r', 'W', 'U', 'C', 'b')}
    del _L1_cond_all

    def _L2_cond_setup():
        import jax, jax.numpy as jnp
        import numpy as np
        D_MODEL = 256
        D_FF = 1024
        N_EXPERTS = 8
        TOP_K = 2
        N_SHARED = 2
        B, T = (4, 512)
        key = jax.random.key(seed)
        ks = jax.random.split(key, 9)
        Hs = D_FF // 2
        Hr = D_FF // 4
        inp = {'x': jax.random.normal(ks[0], (B, T, D_MODEL), dtype=jnp.float32), 't_emb': jax.random.normal(ks[1], (B, D_MODEL), dtype=jnp.float32), 'W_router': 0.01 * jax.random.normal(ks[2], (N_EXPERTS, 2 * D_MODEL), dtype=jnp.float32), 'router_bias': jnp.zeros((N_EXPERTS,), dtype=jnp.float32), 's_w1': 0.02 * jax.random.normal(ks[3], (N_SHARED, Hs, D_MODEL), dtype=jnp.float32), 's_w3': 0.02 * jax.random.normal(ks[4], (N_SHARED, Hs, D_MODEL), dtype=jnp.float32), 's_w2': 0.02 * jax.random.normal(ks[5], (N_SHARED, D_MODEL, Hs), dtype=jnp.float32), 'r_w1': 0.02 * jax.random.normal(ks[6], (N_EXPERTS, Hr, D_MODEL), dtype=jnp.float32), 'r_w2': 0.02 * jax.random.normal(ks[7], (N_EXPERTS, D_MODEL, Hr), dtype=jnp.float32)}
        return inp
    _L2_cond_all = _L2_cond_setup()
    _L2_cond_in = {k: v for k, v in _L2_cond_all.items() if k in ('W_router', 'router_bias', 's_w1', 's_w3', 's_w2', 'r_w1', 'r_w2')}
    del _L2_cond_all

    def _L3_cond_setup():
        import jax, jax.numpy as jnp
        import numpy as np
        NUM_EXPERTS = 4
        TOP_K = 2
        key = jax.random.key(seed)
        ks = jax.random.split(key, 16)
        B, L, D, E, H = (8, 192, 256, NUM_EXPERTS, 1024)
        s = 0.02
        return {'context_c': jax.random.normal(ks[0], (B, L, D), jnp.float32), 'time_cond': jax.random.normal(ks[1], (B, D), jnp.float32), 'gate_w': jax.random.normal(ks[2], (3 * D, E), jnp.float32) * s, 'gate_b': jnp.zeros((E,), jnp.float32), 'time_w': jax.random.normal(ks[3], (D, 2 * E), jnp.float32) * s, 'time_b': jnp.zeros((2 * E,), jnp.float32), 'ew1': jax.random.normal(ks[4], (E, D, H), jnp.float32) * s, 'eb1': jnp.zeros((E, H), jnp.float32), 'ew2': jax.random.normal(ks[5], (E, H, D), jnp.float32) * s, 'eb2': jnp.zeros((E, D), jnp.float32), 'sw1': jax.random.normal(ks[6], (D, H), jnp.float32) * s, 'sb1': jnp.zeros((H,), jnp.float32), 'sw2': jax.random.normal(ks[7], (H, D), jnp.float32) * s, 'sb2': jnp.zeros((D,), jnp.float32)}
    _L3_cond_all = _L3_cond_setup()
    _L3_cond_in = {k: v for k, v in _L3_cond_all.items() if k in ('gate_w', 'gate_b', 'time_w', 'time_b', 'ew1', 'eb1', 'ew2', 'eb2', 'sw1', 'sb1', 'sw2', 'sb2')}
    del _L3_cond_all
    return {'x': x, 'cond_1024': cond_1024, 'L0_cond_w_q': _L0_cond_in['w_q'], 'L0_cond_b_q': _L0_cond_in['b_q'], 'L0_cond_w_k': _L0_cond_in['w_k'], 'L0_cond_b_k': _L0_cond_in['b_k'], 'L0_cond_w_v': _L0_cond_in['w_v'], 'L0_cond_b_v': _L0_cond_in['b_v'], 'L0_cond_w_o': _L0_cond_in['w_o'], 'L0_cond_b_o': _L0_cond_in['b_o'], 'L0_cond_w_f1': _L0_cond_in['w_f1'], 'L0_cond_b_f1': _L0_cond_in['b_f1'], 'L0_cond_w_f2': _L0_cond_in['w_f2'], 'L0_cond_b_f2': _L0_cond_in['b_f2'], 'L0_cond_w_ada': _L0_cond_in['w_ada'], 'L0_cond_b_ada': _L0_cond_in['b_ada'], 'L1_cond_W_z': _L1_cond_in['W_z'], 'L1_cond_U_z': _L1_cond_in['U_z'], 'L1_cond_C_z': _L1_cond_in['C_z'], 'L1_cond_b_z': _L1_cond_in['b_z'], 'L1_cond_W_r': _L1_cond_in['W_r'], 'L1_cond_U_r': _L1_cond_in['U_r'], 'L1_cond_C_r': _L1_cond_in['C_r'], 'L1_cond_b_r': _L1_cond_in['b_r'], 'L1_cond_W': _L1_cond_in['W'], 'L1_cond_U': _L1_cond_in['U'], 'L1_cond_C': _L1_cond_in['C'], 'L1_cond_b': _L1_cond_in['b'], 'L2_cond_W_router': _L2_cond_in['W_router'], 'L2_cond_router_bias': _L2_cond_in['router_bias'], 'L2_cond_s_w1': _L2_cond_in['s_w1'], 'L2_cond_s_w3': _L2_cond_in['s_w3'], 'L2_cond_s_w2': _L2_cond_in['s_w2'], 'L2_cond_r_w1': _L2_cond_in['r_w1'], 'L2_cond_r_w2': _L2_cond_in['r_w2'], 'L3_cond_gate_w': _L3_cond_in['gate_w'], 'L3_cond_gate_b': _L3_cond_in['gate_b'], 'L3_cond_time_w': _L3_cond_in['time_w'], 'L3_cond_time_b': _L3_cond_in['time_b'], 'L3_cond_ew1': _L3_cond_in['ew1'], 'L3_cond_eb1': _L3_cond_in['eb1'], 'L3_cond_ew2': _L3_cond_in['ew2'], 'L3_cond_eb2': _L3_cond_in['eb2'], 'L3_cond_sw1': _L3_cond_in['sw1'], 'L3_cond_sb1': _L3_cond_in['sb1'], 'L3_cond_sw2': _L3_cond_in['sw2'], 'L3_cond_sb2': _L3_cond_in['sb2']}

def reference(x, cond_1024, L0_cond_w_q, L0_cond_b_q, L0_cond_w_k, L0_cond_b_k, L0_cond_w_v, L0_cond_b_v, L0_cond_w_o, L0_cond_b_o, L0_cond_w_f1, L0_cond_b_f1, L0_cond_w_f2, L0_cond_b_f2, L0_cond_w_ada, L0_cond_b_ada, L1_cond_W_z, L1_cond_U_z, L1_cond_C_z, L1_cond_b_z, L1_cond_W_r, L1_cond_U_r, L1_cond_C_r, L1_cond_b_r, L1_cond_W, L1_cond_U, L1_cond_C, L1_cond_b, L2_cond_W_router, L2_cond_router_bias, L2_cond_s_w1, L2_cond_s_w3, L2_cond_s_w2, L2_cond_r_w1, L2_cond_r_w2, L3_cond_gate_w, L3_cond_gate_b, L3_cond_time_w, L3_cond_time_b, L3_cond_ew1, L3_cond_eb1, L3_cond_ew2, L3_cond_eb2, L3_cond_sw1, L3_cond_sb1, L3_cond_sw2, L3_cond_sb2):
    import jax
    import jax.numpy as jnp

    def _L0_cond_ref(x, t_emb, w_q, b_q, w_k, b_k, w_v, b_v, w_o, b_o, w_f1, b_f1, w_f2, b_f2, w_ada, b_ada):
        import math
        import jax, jax.numpy as jnp
        import numpy as np
        EPS = 1e-07
        MAX_TANH_ARG = 1.0 - 1e-05

        def _norm(x):
            return jnp.sqrt(jnp.sum(x * x, axis=-1, keepdims=True)).clip(EPS)

        def logmap0(x):
            n = _norm(x)
            return jnp.arctanh(jnp.clip(n, EPS, MAX_TANH_ARG)) * x / n

        def expmap0(v):
            n = _norm(v)
            return jnp.tanh(n) * v / n

        def mobius_add(x, y):
            x2 = jnp.sum(x * x, -1, keepdims=True)
            y2 = jnp.sum(y * y, -1, keepdims=True)
            xy = jnp.sum(x * y, -1, keepdims=True)
            num = (1 + 2 * xy + y2) * x + (1 - x2) * y
            den = (1 + 2 * xy + x2 * y2).clip(EPS)
            return num / den

        def plin(x, w, b):
            return expmap0(logmap0(x) @ w + b)

        def layer_norm(x, eps=1e-06):
            m = x.mean(-1, keepdims=True)
            v = ((x - m) ** 2).mean(-1, keepdims=True)
            return (x - m) / jnp.sqrt(v + eps)

        def _beta(a, b):
            return math.exp(math.lgamma(a) + math.lgamma(b) - math.lgamma(a + b))
        D, H, FF = (256, 16, 1024)
        HD = D // H
        BETA_N = _beta(D / 2, 0.5)
        BETA_H = _beta(HD / 2, 0.5)

        def _to_heads(p):
            B, S, _ = p.shape
            t = logmap0(p).reshape(B, S, H, HD) * (BETA_H / BETA_N)
            return expmap0(jnp.transpose(t, (0, 2, 1, 3)))

        def _from_heads(ph):
            B, _, S, _ = ph.shape
            t = logmap0(ph) * (BETA_N / BETA_H)
            t = jnp.transpose(t, (0, 2, 1, 3)).reshape(B, S, D)
            return expmap0(t)
        ada = t_emb @ w_ada + b_ada
        sh_msa, sc_msa, g_msa, sh_mlp, sc_mlp, g_mlp = jnp.split(ada, 6, axis=-1)
        residual = x
        xn = layer_norm(logmap0(x))
        xm = expmap0(xn * (1 + sc_msa) + sh_msa)
        q = _to_heads(plin(xm, w_q, b_q))
        k = _to_heads(plin(xm, w_k, b_k))
        v = _to_heads(plin(xm, w_v, b_v))
        qt, kt, vt = (logmap0(q), logmap0(k), logmap0(v))
        scores = jnp.einsum('bhqd,bhkd->bhqk', qt, kt) / math.sqrt(HD)
        attn = jax.nn.softmax(scores, axis=-1)
        out_h = expmap0(jnp.einsum('bhqk,bhkd->bhqd', attn, vt))
        attn_out = plin(_from_heads(out_h), w_o, b_o)
        attn_t = g_msa * logmap0(attn_out)
        x = mobius_add(residual, expmap0(attn_t))
        residual = x
        xn = layer_norm(logmap0(x))
        xm = expmap0(xn * (1 + sc_mlp) + sh_mlp)
        ff = plin(plin(xm, w_f1, b_f1), w_f2, b_f2)
        ff_t = g_mlp * logmap0(ff)
        return mobius_add(residual, expmap0(ff_t))

    def _L1_cond_ref(video, seq, W_z, U_z, C_z, b_z, W_r, U_r, C_r, b_r, W, U, C, b):
        import jax, jax.numpy as jnp
        import numpy as np
        B, T, D_IN, V_IN, E = (64, 128, 256, 256, 256)
        vz = video @ C_z + b_z
        vr = video @ C_r + b_r
        vh = video @ C + b
        xz = jnp.einsum('btd,de->bte', seq, W_z)
        xr = jnp.einsum('btd,de->bte', seq, W_r)
        xh = jnp.einsum('btd,de->bte', seq, W)

        def step(h, xs):
            xzt, xrt, xht = xs
            z = jax.nn.sigmoid(xzt + h @ U_z + vz)
            r = jax.nn.sigmoid(xrt + h @ U_r + vr)
            hh = jnp.tanh(xht + r * h @ U + vh)
            h_new = (1.0 - z) * h + z * hh
            return (h_new, h_new)
        h0 = jnp.zeros((seq.shape[0], U.shape[0]), seq.dtype)
        xs = (jnp.swapaxes(xz, 0, 1), jnp.swapaxes(xr, 0, 1), jnp.swapaxes(xh, 0, 1))
        _, out_t = jax.lax.scan(step, h0, xs)
        return jnp.swapaxes(out_t, 0, 1)

    def _L2_cond_ref(x, t_emb, W_router, router_bias, s_w1, s_w3, s_w2, r_w1, r_w2):
        import jax, jax.numpy as jnp
        import numpy as np
        D_MODEL = 256
        D_FF = 1024
        N_EXPERTS = 8
        TOP_K = 2
        N_SHARED = 2
        B, T = (4, 512)
        Bn, Tn, C = x.shape
        N = Bn * Tn
        x_flat = x.reshape(N, C)
        t_flat = jnp.broadcast_to(t_emb[:, None, :], (Bn, Tn, C)).reshape(N, C)
        shared_out = jnp.zeros_like(x_flat)
        for e in range(N_SHARED):
            h = jax.nn.silu(x_flat @ s_w1[e].T) * (x_flat @ s_w3[e].T)
            shared_out = shared_out + h @ s_w2[e].T
        shared_out = shared_out / N_SHARED
        router_in = jnp.concatenate([x_flat, t_flat], axis=-1)
        s = jax.nn.sigmoid((router_in @ W_router.T).astype(jnp.float32))
        sel_scores = s + router_bias
        _, topk_idx = jax.lax.top_k(sel_scores, TOP_K)
        s_sel = jnp.take_along_axis(s, topk_idx, axis=1)
        denom = jnp.sum(s_sel, axis=1, keepdims=True)
        gates = jnp.where(denom > 1e-09, s_sel / (denom + 1e-09), 1.0 / TOP_K).astype(x.dtype)
        gates_full = jnp.sum(jax.nn.one_hot(topk_idx, N_EXPERTS, dtype=x.dtype) * gates[..., None], axis=1)
        routed_out = jnp.zeros_like(x_flat)
        for e in range(N_EXPERTS):
            h = jax.nn.gelu(x_flat @ r_w1[e].T, approximate=False)
            routed_out = routed_out + h @ r_w2[e].T * gates_full[:, e:e + 1]
        out = (shared_out + routed_out) / (N_SHARED + TOP_K)
        return out.reshape(Bn, Tn, C)

    def _L3_cond_ref(context_c, time_cond, gate_w, gate_b, time_w, time_b, ew1, eb1, ew2, eb2, sw1, sb1, sw2, sb2):
        import jax, jax.numpy as jnp
        import numpy as np
        NUM_EXPERTS = 4
        TOP_K = 2
        B, L, D = context_c.shape
        E, K = (NUM_EXPERTS, TOP_K)
        L_head = L_wrist = L // 3
        head = context_c[:, :L_head]
        wrist = context_c[:, L_head:L_head + L_wrist]
        proprio = context_c[:, L_head + L_wrist:]
        full_agg = context_c.mean(axis=1)
        hp_agg = jnp.concatenate([head, proprio], axis=1).mean(axis=1)
        wp_agg = jnp.concatenate([wrist, proprio], axis=1).mean(axis=1)
        gate_in = jnp.concatenate([full_agg, hp_agg, wp_agg], axis=-1)
        gate_logits = gate_in @ gate_w + gate_b
        mod = jax.nn.silu(time_cond) @ time_w + time_b
        scale, shift = jnp.split(mod, 2, axis=-1)
        gate_logits = gate_logits * (1.0 + scale) + shift
        gate_scores = jax.nn.softmax(gate_logits, axis=-1)
        topk_w, topk_i = jax.lax.top_k(gate_scores, K)
        topk_w = topk_w / (topk_w.sum(axis=-1, keepdims=True) + 1e-08)
        onehot = (topk_i[..., None] == jnp.arange(E)[None, None, :]).astype(context_c.dtype)
        w_be = jnp.sum(topk_w[..., None] * onehot, axis=1)
        mask = np.ones((E, L), dtype=np.float32)
        mask[1, L_head:L_head + L_wrist] = 0.0
        mask[2, :L_head] = 0.0
        mask = jnp.asarray(mask)
        out = jnp.zeros_like(context_c)
        for e in range(E):
            h = jax.nn.gelu(context_c @ ew1[e] + eb1[e], approximate=True)
            y = h @ ew2[e] + eb2[e]
            out = out + w_be[:, e][:, None, None] * mask[e][None, :, None] * y
        shared = jax.nn.gelu(context_c @ sw1 + sb1, approximate=True) @ sw2 + sb2
        return out + shared
    x = x + _L0_cond_ref(x, cond_1024[:, None, :], L0_cond_w_q, L0_cond_b_q, L0_cond_w_k, L0_cond_b_k, L0_cond_w_v, L0_cond_b_v, L0_cond_w_o, L0_cond_b_o, L0_cond_w_f1, L0_cond_b_f1, L0_cond_w_f2, L0_cond_b_f2, L0_cond_w_ada, L0_cond_b_ada)
    x = x + _L1_cond_ref(cond_1024, x, L1_cond_W_z, L1_cond_U_z, L1_cond_C_z, L1_cond_b_z, L1_cond_W_r, L1_cond_U_r, L1_cond_C_r, L1_cond_b_r, L1_cond_W, L1_cond_U, L1_cond_C, L1_cond_b)
    x = x + _L2_cond_ref(x, cond_1024, L2_cond_W_router, L2_cond_router_bias, L2_cond_s_w1, L2_cond_s_w3, L2_cond_s_w2, L2_cond_r_w1, L2_cond_r_w2)
    x = x + _L3_cond_ref(x, cond_1024, L3_cond_gate_w, L3_cond_gate_b, L3_cond_time_w, L3_cond_time_b, L3_cond_ew1, L3_cond_eb1, L3_cond_ew2, L3_cond_eb2, L3_cond_sw1, L3_cond_sb1, L3_cond_sw2, L3_cond_sb2)
    return x

_drawn_inputs = setup_inputs


def setup_inputs(seed=0):
    import zlib

    import numpy as np

    out = dict(_drawn_inputs(seed))
    spreads = {'L0_cond_b_q': (0.0, 2.0),
     'L0_cond_b_k': (0.0, 2.0),
     'L0_cond_b_v': (0.0, 0.1),
     'L0_cond_b_o': (0.0, 0.1),
     'L0_cond_b_f1': (0.0, 0.1),
     'L0_cond_b_f2': (0.0, 0.1),
     'L0_cond_b_ada': (0.0, 0.1),
     'L1_cond_b_z': (0.0, 2.0),
     'L1_cond_b_r': (0.0, 2.0),
     'L1_cond_b': (0.0, 0.1),
     'L2_cond_router_bias': (0.0, 0.73),
     'L3_cond_gate_b': (0.0, 0.743),
     'L3_cond_time_b': (0.0, 0.8),
     'L3_cond_eb1': (0.0, 0.1),
     'L3_cond_eb2': (0.0, 0.1),
     'L3_cond_sb1': (0.0, 0.1),
     'L3_cond_sb2': (0.0, 0.1)}
    factors = {'L0_cond_w_q': 64.0,
     'L0_cond_w_k': 33.575,
     'L0_cond_w_v': 2.879,
     'L1_cond_W_z': 64.0,
     'L1_cond_U_z': 62.979,
     'L1_cond_C_z': 8.0,
     'L1_cond_W_r': 200.0,
     'L1_cond_U_r': 64.0,
     'L1_cond_C_r': 8.0,
     'L2_cond_W_router': 8.0,
     'L2_cond_s_w1': 8.0,
     'L2_cond_s_w3': 8.0,
     'L2_cond_s_w2': 8.0,
     'L2_cond_r_w1': 7.316,
     'L2_cond_r_w2': 7.26}
    for name, (base, spread) in spreads.items():
        noise = np.random.default_rng([zlib.crc32(name.encode()), seed]).standard_normal(out[name].shape)
        drawn = base * np.exp(spread * noise) if base else spread * noise
        out[name] = jnp.asarray(drawn.astype(out[name].dtype))
    for name, factor in factors.items():
        out[name] = (out[name] * factor).astype(out[name].dtype)
    return out
```

```python
import math
from contextlib import ExitStack

import concourse.bass as bass
from concourse import mybir
import numpy as np

ALU = mybir.AluOpType
ACT = mybir.ActivationFunctionType
AX = mybir.AxisListType
F32 = mybir.dt.float32
BF16 = mybir.dt.bfloat16
F16 = mybir.dt.float16

P = 128
B, S, D = 4, 512, 256
NT = S // P
H = 16
HD = D // H
FF = 1024
EPS = 1e-7
EPS2 = EPS * EPS
MAX_TANH = float(np.float32(1.0 - 1e-5))
ATANH_MAX = float(np.arctanh(np.float64(np.float32(1.0 - 1e-5))))


def beta(a, b):
    return math.exp(math.lgamma(a) + math.lgamma(b) - math.lgamma(a + b))


TO_HEADS = beta(HD / 2, 0.5) / beta(D / 2, 0.5)
SLOTS = 8
Q_SLOTS = ((0, 0, 1, 2), (0, 4, 1, 1), (1, 2, 1, 2), (1, 6, 1, 1), (2, 5, 2, 2))
K_SLOTS = ((0, 0, 2, 2), (0, 5, 1, 1), (1, 1, 2, 2), (1, 7, 1, 1), (2, 4, 2, 2))
L0_DVE_STEPS = 206
CH = 16
XT_COLS = B * S
TOP_K = 2


def hyperbolic_block(nc, x, cond_t, w_qkv, b_qkv, w_o, b_o, w_f1, b_f1, w_f2, b_f2, w_ada, b_ada, XT, ident, ident_bf):
    with ExitStack() as ctx:
        def sb(name, shape, dt=F32):
            return ctx.enter_context(nc.sbuf_tensor(name, shape, dt))

        def sem(name):
            return ctx.enter_context(nc.semaphore(name))

        X = sb("x_tokens", [P, B * NT, D])
        Wqkv = sb("w_qkv_sb", [P, 2, 3 * D])
        Wo = sb("w_o_sb", [P, 2, D])
        F1 = sb("w_f1_sb", [P, 2, FF])
        F2 = sb("w_f2_sb", [P, FF // P, D])
        cond = sb("cond_sb", [P, 2, B])
        ada = sb("ada", [P, B, 6, D])
        bias_qkv = sb("bias_qkv", [P, 3 * D])
        bias_o = sb("bias_o", [P, D])
        bias_f1 = sb("bias_f1", [P, FF])
        bias_f2 = sb("bias_f2", [P, D])
        X1 = sb("x1", [P, NT, D])
        X2 = sb("x2", [P, NT, D])
        U = sb("u", [P, NT, D])
        UT = sb("u_t", [P, NT, 2, P])
        QKV = sb("qkv", [P, NT, 3 * H, HD])
        SQ = sb("squares", [P, 2, FF])
        cond_rep = SQ[:, :, 0:B * P].rearrange("p k (b t) -> p k b t", b=B)
        QS, R1 = (SQ[:, n, 0:2 * D].rearrange("p (h d) -> p h d", d=HD) for n in range(2))
        PT = sb("qk_parts", [P, 3, 2 * H, HD], BF16)
        ST = sb("qk_stack", [P, 2 * H, SLOTS, HD], BF16)
        QKT = sb("qk_t", [P, 2 * H, S], BF16)
        early = QKT[:].rearrange("p h t -> p (h t)").bitcast(F32)
        W_ada = early[:, 0:12 * D].rearrange("p (k n) -> p k n", k=2)
        bias_ada = early[:, 12 * D:18 * D]
        VP = sb("v_ones", [P, NT, H, 32])
        PR = sb("probs", [P, 4, 2, S])
        OT = QKV[:].rearrange("p j h d -> p (j h d)")[:, 0:4 * S].rearrange("p (g t) -> p g t", g=4)
        OV = U[:].rearrange("p j (h d) -> p j h d", h=H)
        AT = sb("tangent", [P, NT, D])
        HB = PR[:].rearrange("p m c t -> p m (c t)")
        HTR = ST[:].rearrange("p h s d -> p (h s d)").bitcast(F32).rearrange("p (j f) -> p j f", j=2)
        BS = sb("bn", [P, NT, 6])
        MV = sb("mean_var", [P, 2, NT])
        C = sb("cols", [P, 24, NT])
        SSH = sb("head_ss", [P, NT, 3 * H])
        HR = sb("head_rsqrt", [P, NT, 3 * H])
        HF = sb("head_factor", [P, NT, 3 * H])
        HT2 = sb("head_tmp", [P, NT, 3 * H])
        LT = sb("log_tmp", [P, NT, 3 * H])
        T3 = sb("qkv_cols", [P, 5, NT * 3])
        RS = sb("row_recip", [P, NT, H])
        JKA = sb("junk_act", [P, D])
        JKV = sb("junk_dve", [P, D])
        PS = ctx.enter_context(nc.psum_tensor("ps", [P, 8, 512], F32))

        loads, cond_in = sem("loads"), sem("cond_in")
        cond_ready, ada_mm, ada_done = sem("cond_ready"), sem("ada_mm"), sem("ada_done")
        dve_step, act_step = sem("dve_step"), sem("act_step")
        cols_ready, cols_done = sem("cols_ready"), sem("cols_done")
        u_ready, u_turned, u_copied, u_ss = sem("u_ready"), sem("u_turned"), sem("u_copied"), sem("u_ss")
        qkv_mm, qkv_out, qkv_sq, sq_summed = sem("qkv_mm"), sem("qkv_out"), sem("qkv_sq"), sem("sq_summed")
        stacked, stack_turned = sem("stacked"), sem("stack_turned")
        stack_copied_v, stack_copied_a = sem("stack_copied_v"), sem("stack_copied_a")
        scores_mm, probs_ready, pv_mm = sem("scores_mm"), sem("probs_ready"), sem("pv_mm")
        o_copied, o_turned, o_out, o_sq = sem("o_copied"), sem("o_turned"), sem("o_out"), sem("o_sq")
        attn_in, attn_turned, attn_copied = sem("attn_in"), sem("attn_turned"), sem("attn_copied")
        attn_mm, attn_out, attn_ss = sem("attn_mm"), sem("attn_out"), sem("attn_ss")
        h_mm, h_out, h_ss, h_turned, h_copied, ff_mm = (
            sem("h_mm"), sem("h_out"), sem("h_ss"), sem("h_turned"), sem("h_copied"), sem("ff_mm"))
        x_out, x_turned, x_copied = sem("x_out"), sem("x_turned"), sem("x_copied")

        def bank(n, a=0, z=512):
            return PS[:, n, a:z]

        def bank_bf(n):
            return PS[:, n, :].bitcast(BF16)

        def flat(ap):
            return ap.rearrange("p a b -> p (a b)")

        DVE_STEPS, ACT_STEPS, COLS = L0_DVE_STEPS, 15, 19
        LOADS = 16 * 10

        with nc.Block() as block:
            @block.sync
            def _(sp):
                sp.dma_start(cond[:], cond_t.rearrange("(k p) b -> p k b", p=P)).then_inc(cond_in, 16)
                sp.dma_start(W_ada, w_ada.rearrange("(k p) n -> p k n", p=P)).then_inc(cond_in, 16)
                sp.dma_start(X[:], x.rearrange("b (j p) d -> p (b j) d", p=P)).then_inc(loads, 16)
                for dst, src in ((Wqkv, w_qkv), (Wo, w_o), (F1, w_f1), (F2, w_f2)):
                    sp.dma_start(dst[:], src.rearrange("(k p) n -> p k n", p=P)).then_inc(loads, 16)
                for dst, src in ((bias_qkv, b_qkv), (bias_o, b_o), (bias_f1, b_f1), (bias_f2, b_f2), (bias_ada, b_ada)):
                    n = src.shape[0]
                    sp.dma_start(dst[:, 0:n], src.rearrange("(a n) -> a n", a=1).broadcast_to([P, n])).then_inc(loads, 16)

            @block.tensor
            def _(pe):
                pe.wait_ge(cond_in, 32)
                pe.wait_ge(cond_ready, 1)
                for b in range(B):
                    for n in range(3):
                        g = b * 3 + n
                        if g >= 8:
                            pe.wait_ge(ada_done, g - 7)
                        for k in range(2):
                            mm = pe.matmul(bank(g % 8), cond_rep[:, k, b, :], W_ada[:, k, n * 512:(n + 1) * 512],
                                           start=(k == 0), stop=(k == 1))
                        mm.then_inc(ada_mm, 1)
                pe.wait_ge(loads, LOADS)
                pe.wait_ge(ada_done, 12)

                with pe.Fori(0, B) as i:
                    def turn(src, ready, ready_at, copied, copied_at, turned, b0):
                        for j in range(NT):
                            pe.wait_ge(ready, ready_at + j + 1)
                            if j >= 2:
                                pe.wait_ge(copied, copied_at + j - 1)
                            for k in range(2):
                                mm = pe.transpose(bank(b0 + j % 2, k * P, k * P + P), src[:, j, k * P:k * P + P], ident[:])
                            mm.then_inc(turned, 1)

                    turn(U, u_ready, i * 2 * NT, u_copied, i * 2 * NT, u_turned, 0)
                    for j in range(NT):
                        pe.wait_ge(u_copied, i * 2 * NT + j + 1)
                        if j >= 2:
                            pe.wait_ge(qkv_out, i * NT * 2 + 2 * (j - 1))
                        for a, z, bk in ((0, 512, 2 + 2 * (j % 2)), (512, 768, 3 + 2 * (j % 2))):
                            for k in range(2):
                                mm = pe.matmul(bank(bk, 0, z - a), UT[:, j, k, :], Wqkv[:, k, a:z],
                                               start=(k == 0), stop=(k == 1))
                        mm.then_inc(qkv_mm, 1)
                    for j in range(NT):
                        pe.wait_ge(stacked, i * NT * 10 + (j + 1) * 10)
                        for g in range(4):
                            n = j * 4 + g
                            if n >= 2:
                                pe.wait_ge((stack_copied_v, stack_copied_a)[n % 2], i * 8 + (n - 2) // 2 + 1)
                            for h in range(8):
                                mm = pe.transpose(bank_bf(6 + n % 2)[:, h * P:h * P + P],
                                                  flat(ST[:, g * 8 + h, :, :]), ident_bf[:])
                            mm.then_inc(stack_turned, 1)
                    pe.wait_ge(stack_copied_v, i * 8 + 8)
                    pe.wait_ge(stack_copied_a, i * 8 + 8)

                    def scores(n, e):
                        hg, kt = n // 4, n % 4
                        m = 2 * n + e
                        if m >= 3:
                            pe.wait_ge(probs_ready, i * 32 + m - 2)
                        for c in range(2):
                            h = hg * 4 + e * 2 + c
                            mm = pe.matmul(bank(2 * (m % 3) + c), QKT[:, H + h, kt * P:kt * P + P], QKT[:, h, :],
                                           start=True, stop=True)
                        mm.then_inc(scores_mm, 1)

                    def weighted(n):
                        hg, kt = n // 4, n % 4
                        pe.wait_ge(probs_ready, i * 32 + 2 * n + 2)
                        if kt == 0 and hg >= 2:
                            pe.wait_ge(o_copied, i * 4 + hg - 1)
                        for q in range(4):
                            mm = pe.matmul(PS[32 * q:32 * q + 32, 6 + hg % 2, :], VP[:, kt, hg * 4 + q, :],
                                           PR[:, (2 * n + q // 2) % 4, q % 2, :], start=(kt == 0), stop=(kt == 3),
                                           skip_group_check=True)
                        mm.then_inc(pv_mm, 1)

                    scores(0, 0)
                    scores(0, 1)
                    for n in range(16):
                        if n < 15:
                            scores(n + 1, 0)
                        weighted(n)
                        if n < 15:
                            scores(n + 1, 1)
                    for j in range(NT):
                        pe.wait_ge(o_copied, i * 4 + 4)
                        if j >= 2:
                            pe.wait_ge(o_out, i * NT + j - 1)
                        for g in range(4):
                            mm = pe.transpose(bank(j % 2, g * P, g * P + P), OT[:, g, j * P:j * P + P], ident[:])
                        mm.then_inc(o_turned, 1)
                    turn(AT, attn_in, i * NT, attn_copied, i * NT, attn_turned, 2)
                    for j in range(NT):
                        pe.wait_ge(attn_copied, i * NT + j + 1)
                        if j >= 2:
                            pe.wait_ge(attn_out, i * NT * 4 + j - 1)
                        for k in range(2):
                            mm = pe.matmul(bank(4 + j % 2, 0, D), UT[:, j, k, :], Wo[:, k, :], start=(k == 0), stop=(k == 1))
                        mm.then_inc(attn_mm, 1)
                    turn(U, u_ready, i * 2 * NT + NT, u_copied, i * 2 * NT + NT, u_turned, 6)
                    for j in range(NT):
                        pe.wait_ge(u_copied, i * 2 * NT + NT + j + 1)
                        if j >= 2:
                            pe.wait_ge(h_out, i * NT * 2 + 2 * (j - 1))
                        for c in range(2):
                            for k in range(2):
                                mm = pe.matmul(bank(2 * (j % 2) + c), UT[:, j, k, :], F1[:, k, c * 512:c * 512 + 512],
                                               start=(k == 0), stop=(k == 1))
                        mm.then_inc(h_mm, 1)
                    for j in range(NT):
                        pe.wait_ge(h_out, i * NT * 2 + 2 * (j + 1))
                        for c in range(8):
                            mm = pe.transpose(bank(4 + c // 4, c % 4 * P, c % 4 * P + P), HB[:, j, c * P:c * P + P], ident[:])
                        mm.then_inc(h_turned, 1)
                        pe.wait_ge(h_copied, i * NT + j + 1)
                        for c in range(8):
                            mm = pe.matmul(bank((6, 7, 0, 1)[j], 0, D), HTR[:, j % 2, c * P:c * P + P],
                                           F2[:, c, :], start=(c == 0), stop=(c == 7), skip_group_check=True)
                        mm.then_inc(ff_mm, 1)
                    turn(X2, x_out, i * NT, x_copied, i * NT, x_turned, 0)

            @block.scalar
            def _(act):
                act.preload_act_table_set("natural_log_exp_and_others")
                with act.Fori(0, B) as i:
                    step, col = [0], [0]

                    def arrive():
                        col[0] += 1
                        act.wait_ge(cols_ready, i * COLS + col[0])

                    def rsqrt(dst, src, tmp):
                        arrive()
                        act.activation(tmp, src, ACT.Ln).then_inc(act_step, 1)
                        step[0] += 1
                        act.wait_ge(act_step, i * ACT_STEPS + step[0])
                        act.activation(dst, tmp, ACT.Exp, scale=-0.5).then_inc(cols_done, 1)

                    def norm_and_turn(r, b0):
                        rsqrt(C[:, 1, :], C[:, 0, :], C[:, 20, :])
                        arrive()
                        act.activation(C[:, 3, :], C[:, 2, :], ACT.Ln, scale=1.0, bias=1.0)
                        act.activation(C[:, 4, :], C[:, 2, :], ACT.Ln, scale=-1.0, bias=1.0).then_inc(cols_done, 1)
                        rsqrt(C[:, 6, :], C[:, 5, :], C[:, 20, :])
                        for j in range(NT):
                            act.wait_ge(u_ready, i * 2 * NT + r * NT + j + 1)
                            if j:
                                act.wait_ge(u_ss, i * 2 * NT + r * NT + j)
                            act.activation(JKA[:], U[:, j, :], ACT.Square, accum_out=C[:, 7, j:j + 1]).then_inc(u_ss, 1)
                            act.wait_ge(u_turned, i * 2 * NT + r * NT + j + 1)
                            act.activation(flat(UT[:, j, :, :]), bank(b0 + j % 2, 0, D), ACT.Copy).then_inc(u_copied, 1)
                        rsqrt(C[:, 8, :], C[:, 7, :], C[:, 20, :])

                    norm_and_turn(0, 0)
                    for j in range(NT):
                        act.wait_ge(qkv_out, i * NT * 2 + 2 * (j + 1))
                        if j >= 2:
                            act.wait_ge(sq_summed, i * NT + j - 1)
                        act.activation(SQ[:, j % 2, 0:3 * D], flat(QKV[:, j, :, :]), ACT.Square).then_inc(qkv_sq, 1)
                    rsqrt(T3[:, 1, :], T3[:, 0, :], T3[:, 3, :])
                    rsqrt(HR[:], SSH[:], LT[:])
                    for n in range(1, 16, 2):
                        act.wait_ge(stack_turned, i * 16 + n + 1)
                        j, g = n // 4, n % 4
                        act.activation(QKT[:, g * 8:g * 8 + 8, j * P:j * P + P],
                                       bank_bf(7).rearrange("p (h t) -> p h t", t=P), ACT.Copy).then_inc(stack_copied_a, 1)
                    for m in range(32):
                        act.wait_ge(scores_mm, i * 32 + m + 1)
                        if m >= 4:
                            act.wait_ge(pv_mm, i * 16 + (m - 4) // 2 + 1)
                        act.activation(PR[:, m % 4, :, :], PS[:, 2 * (m % 3):2 * (m % 3) + 2, :], ACT.Exp,
                                       scale=1.0 / math.sqrt(HD)).then_inc(probs_ready, 1)
                    for j in range(NT):
                        act.wait_ge(o_out, i * NT + j + 1)
                        act.activation(SQ[:, j // 2, (j % 2) * D:(j % 2) * D + D], flat(OV[:, j, :, :]),
                                       ACT.Square).then_inc(o_sq, 1)
                    rsqrt(HR[:, :, 0:H], SSH[:, :, 0:H], LT[:, :, 0:H])
                    rsqrt(C[:, 1, :], C[:, 0, :], C[:, 20, :])
                    for j in range(NT):
                        act.wait_ge(attn_turned, i * NT + j + 1)
                        act.activation(flat(UT[:, j, :, :]), bank(2 + j % 2, 0, D), ACT.Copy).then_inc(attn_copied, 1)

                    def mobius(r):
                        for j in range(NT):
                            act.wait_ge(attn_out, i * NT * 4 + r * NT * 2 + j + 1)
                            if j:
                                act.wait_ge(attn_ss, i * NT * 4 + r * NT * 2 + j)
                            act.activation(JKA[:], AT[:, j, :], ACT.Square, accum_out=C[:, 9, j:j + 1]).then_inc(attn_ss, 1)
                        rsqrt(C[:, 10, :], C[:, 9, :], C[:, 20, :])
                        for j in range(NT):
                            act.wait_ge(attn_out, i * NT * 4 + r * NT * 2 + NT + j + 1)
                            if j:
                                act.wait_ge(attn_ss, i * NT * 4 + r * NT * 2 + NT + j)
                            act.activation(JKA[:], AT[:, j, :], ACT.Square, accum_out=C[:, 11, j:j + 1]).then_inc(attn_ss, 1)
                        rsqrt(C[:, 13, :], C[:, 12, :], C[:, 20, :])
                        arrive()
                        act.activation(C[:, 15, :], C[:, 14, :], ACT.Tanh).then_inc(cols_done, 1)
                        act.preload_act_table_set("natural_log_exp_and_others")

                    mobius(0)
                    norm_and_turn(1, 6)
                    for j in range(NT):
                        act.wait_ge(h_out, i * NT * 2 + 2 * (j + 1))
                        if j:
                            act.wait_ge(h_ss, i * NT + j)
                        act.activation(SQ[:, 0, :], HB[:, j, :], ACT.Square, accum_out=C[:, 7, j:j + 1]).then_inc(h_ss, 1)
                        act.wait_ge(h_turned, i * NT + j + 1)
                        if j >= 2:
                            act.wait_ge(ff_mm, i * NT + j - 1)
                        act.activation(HTR[:, j % 2, :], flat(PS[:, 4:6, :]), ACT.Copy).then_inc(h_copied, 1)
                    rsqrt(C[:, 8, :], C[:, 7, :], C[:, 20, :])
                    mobius(1)
                    assert (step[0], col[0]) == (ACT_STEPS, COLS), (step, col)

            @block.vector
            def _(dve):
                dve.wait_ge(cond_in, 32)
                dve.tensor_copy(cond_rep, cond[:].unsqueeze(3).broadcast_to([P, 2, B, P])).then_inc(cond_ready, 1)
                dve.memset(VP[:], 0.0).then_inc(cond_ready, 1)
                dve.wait_ge(cond_ready, 2)
                dve.memset(VP[:, :, :, HD:HD + 1], 1.0).then_inc(cond_ready, 1)
                dve.wait_ge(loads, LOADS)
                for b in range(B):
                    for n in range(3):
                        g = b * 3 + n
                        dve.wait_ge(ada_mm, g + 1)
                        dve.tensor_tensor(flat(ada[:, b, :, :])[:, n * 512:n * 512 + 512], bank(g % 8),
                                          bias_ada[:, n * 512:n * 512 + 512], ALU.add).then_inc(ada_done, 1)
                dve.wait_ge(ada_done, 3 * B)
                for m in (1, 4):
                    dve.tensor_scalar(ada[:, :, m, :], ada[:, :, m, :], 1.0, None, ALU.add).then_inc(cond_ready, 1)
                dve.wait_ge(cond_ready, 5)

                with dve.Fori(0, B) as i:
                    step, col, done = [0], [0], [0]

                    def link(ins):
                        step[0] += 1
                        ins.then_inc(dve_step, 1)
                        dve.wait_ge(dve_step, i * DVE_STEPS + step[0])

                    def ask(ins):
                        col[0] += 1
                        ins.then_inc(cols_ready, 1)
                        dve.wait_ge(cols_ready, i * COLS + col[0])

                    def answered():
                        done[0] += 1
                        dve.wait_ge(cols_done, i * COLS + done[0])

                    def newton(y, v, t):
                        answered()
                        link(dve.tensor_tensor(t, y, y, ALU.mult))
                        link(dve.scalar_tensor_tensor(t, t, -0.5, v, ALU.mult, ALU.mult))
                        link(dve.scalar_tensor_tensor(y, t, 1.5, y, ALU.add, ALU.mult))

                    def c(n):
                        return C[:, n, :]

                    def norm(r, src, scale, shift):
                        mean, var = MV[:, 0, :], MV[:, 1, :]
                        for j in range(NT):
                            ins = dve.bn_stats(BS[:, j, :], src(j))
                        link(ins)
                        link(dve.tensor_tensor(mean, BS[:, :, 1], BS[:, :, 4], ALU.add))
                        link(dve.tensor_scalar(mean, mean, 0.5, None, ALU.mult))
                        link(dve.tensor_tensor(c(16), BS[:, :, 1], BS[:, :, 4], ALU.subtract))
                        link(dve.tensor_tensor(c(16), c(16), c(16), ALU.mult))
                        link(dve.tensor_tensor(var, BS[:, :, 2], BS[:, :, 5], ALU.add))
                        link(dve.tensor_scalar(var, var, 1.0 / D, None, ALU.mult))
                        link(dve.scalar_tensor_tensor(var, c(16), 0.25, var, ALU.mult, ALU.add))
                        link(dve.tensor_tensor(c(21), mean, mean, ALU.mult))
                        link(dve.tensor_tensor(c(21), c(21), var, ALU.add))
                        link(dve.tensor_scalar(c(22), c(21), float(D), None, ALU.mult))
                        ask(dve.tensor_scalar(c(0), c(22), EPS2, None, ALU.max))
                        newton(c(1), c(0), c(16))
                        link(dve.tensor_tensor(c(2), c(0), c(1), ALU.mult))
                        ask(dve.tensor_scalar(c(2), c(2), MAX_TANH, None, ALU.min))
                        link(dve.tensor_tensor(c(16), c(2), c(2), ALU.mult))
                        link(dve.tensor_scalar(c(17), c(16), 1.0 / 15, None, ALU.mult))
                        for odd in (13, 11, 9, 7, 5, 3):
                            link(dve.scalar_tensor_tensor(c(17), c(17), 1.0 / odd, c(16), ALU.add, ALU.mult))
                        link(dve.scalar_tensor_tensor(c(17), c(17), 1.0, c(2), ALU.add, ALU.mult))
                        link(dve.tensor_scalar(c(18), c(2), 0.25, None, ALU.is_lt))
                        answered()
                        link(dve.tensor_tensor(c(3), c(3), c(4), ALU.subtract))
                        link(dve.scalar_tensor_tensor(c(17), c(3), -0.5, c(17), ALU.mult, ALU.add))
                        link(dve.tensor_tensor(c(17), c(17), c(18), ALU.mult))
                        link(dve.scalar_tensor_tensor(c(17), c(3), 0.5, c(17), ALU.mult, ALU.add))
                        link(dve.tensor_tensor(c(17), c(17), c(1), ALU.mult))
                        link(dve.tensor_tensor(c(16), c(17), c(17), ALU.mult))
                        link(dve.tensor_tensor(c(16), c(16), var, ALU.mult))
                        ask(dve.tensor_scalar(c(5), c(16), 1e-6, None, ALU.add))
                        newton(c(6), c(5), c(16))
                        link(dve.tensor_tensor(c(18), c(17), c(6), ALU.mult))
                        for j in range(NT):
                            link(dve.scalar_tensor_tensor(U[:, j, :], src(j), MV[:, 0, j:j + 1], ada[:, i, scale, :],
                                                          ALU.subtract, ALU.mult))
                            dve.scalar_tensor_tensor(U[:, j, :], U[:, j, :], C[:, 18, j:j + 1], ada[:, i, shift, :],
                                                     ALU.mult, ALU.add).then_inc(u_ready, 1)
                        dve.wait_ge(u_ss, i * 2 * NT + r * NT + NT)
                        clamp(7, 8, 19)

                    def clamp(ss, root, out):
                        ask(dve.tensor_scalar(c(ss), c(ss), EPS2, None, ALU.max))
                        newton(c(root), c(ss), c(16))
                        link(dve.tensor_scalar(c(out), c(root), ATANH_MAX, 1.0, ALU.mult, ALU.min))

                    def x_in(j):
                        return X[:, i * NT + j, :]

                    def x_mid(j):
                        return X1[:, j, :]

                    def heads(j, a, z):
                        return HF[:, j, a:z].unsqueeze(2).broadcast_to([P, z - a, HD])

                    norm(0, x_in, 1, 0)

                    def sum_squares(j):
                        dve.wait_ge(qkv_sq, i * NT + j + 1)
                        dve.tensor_reduce(SSH[:, j, :], SQ[:, j % 2, 0:3 * D].rearrange("p (h d) -> p h d", d=HD),
                                          AX.X, ALU.add).then_inc(sq_summed, 1)

                    for j in range(NT):
                        dve.wait_ge(qkv_mm, i * NT + j + 1)
                        out = flat(QKV[:, j, :, :])
                        for a, z, bk in ((0, 512, 2 + 2 * (j % 2)), (512, 768, 3 + 2 * (j % 2))):
                            dve.scalar_tensor_tensor(out[:, a:z], bank(bk, 0, z - a), C[:, 19, j:j + 1],
                                                     bias_qkv[:, a:z], ALU.mult, ALU.add).then_inc(qkv_out, 1)
                        if j:
                            sum_squares(j - 1)
                    sum_squares(NT - 1)
                    dve.wait_ge(sq_summed, i * NT + NT)
                    link(dve.tensor_reduce(T3[:, 0, :], SSH[:].rearrange("p j (t h) -> p (j t) h", h=H), AX.X, ALU.add))
                    ask(dve.tensor_scalar(T3[:, 0, :], T3[:, 0, :], EPS2, None, ALU.max))
                    ask(dve.tensor_scalar(SSH[:], SSH[:], EPS2, None, ALU.max))
                    newton(T3[:, 1, :], T3[:, 0, :], T3[:, 2, :])
                    link(dve.tensor_scalar(T3[:, 1, :], T3[:, 1, :], ATANH_MAX, 1.0, ALU.mult, ALU.min))
                    link(dve.tensor_scalar(T3[:, 1, :], T3[:, 1, :], TO_HEADS, None, ALU.mult))
                    newton(HR[:], SSH[:], HT2[:])
                    link(dve.scalar_tensor_tensor(HF[:].rearrange("p j (t h) -> p (j t) h", h=H),
                                                  HR[:].rearrange("p j (t h) -> p (j t) h", h=H), ATANH_MAX,
                                                  T3[:, 1, :].unsqueeze(2).broadcast_to([P, NT * 3, H]), ALU.mult, ALU.min))

                    def copy_stack(n):
                        dve.wait_ge(stack_turned, i * 16 + n + 1)
                        j, g = n // 4, n % 4
                        dve.tensor_copy(QKT[:, g * 8:g * 8 + 8, j * P:j * P + P],
                                        bank_bf(6).rearrange("p (h t) -> p h t", t=P)).then_inc(stack_copied_v, 1)

                    for j in range(NT):
                        link(dve.tensor_tensor(QS, QKV[:, j, 0:2 * H, :], heads(j, 0, 2 * H), ALU.mult))
                        dve.tensor_tensor(VP[:, j, :, 0:HD], QKV[:, j, 2 * H:3 * H, :], heads(j, 2 * H, 3 * H), ALU.mult)
                        p1, p2, p3 = (PT[:, n, :, :] for n in range(3))
                        link(dve.tensor_copy(p1, QS))
                        link(dve.tensor_tensor(R1, QS, p1, ALU.subtract))
                        link(dve.tensor_copy(p2, R1))
                        link(dve.tensor_tensor(p3, R1, p2, ALU.subtract))
                        if j:
                            copy_stack(4 * (j - 1))
                            copy_stack(4 * (j - 1) + 2)
                            dve.wait_ge(stack_turned, i * 16 + j * 4)
                        for half, copies in ((0, Q_SLOTS), (1, K_SLOTS)):
                            hs = slice(half * H, half * H + H)
                            for part, first, slot_step, n in copies:
                                dst = ST[:, hs, first:first + slot_step * (n - 1) + 1:slot_step, :]
                                src = PT[:, part, hs, :].unsqueeze(2).broadcast_to([P, H, n, HD])
                                dve.tensor_copy(dst, src).then_inc(stacked, 1)
                    copy_stack(12)
                    copy_stack(14)
                    for g in range(4):
                        dve.wait_ge(pv_mm, i * 16 + 4 * g + 4)
                        dve.tensor_copy(OT[:, g, :], bank(6 + g % 2)).then_inc(o_copied, 1)

                    def sum_o(j):
                        dve.wait_ge(o_sq, i * NT + j + 1)
                        return dve.tensor_reduce(SSH[:, j, 0:H], SQ[:, j // 2, (j % 2) * D:(j % 2) * D + D].rearrange(
                            "p (h d) -> p h d", d=HD), AX.X, ALU.add)

                    for j in range(NT):
                        dve.wait_ge(o_turned, i * NT + j + 1)
                        o = bank(j % 2).rearrange("p (h d) -> p h d", d=32)
                        link(dve.reciprocal(RS[:, j, :].unsqueeze(2), o[:, :, HD:HD + 1]))
                        dve.tensor_tensor(OV[:, j, :, :], o[:, :, 0:HD], RS[:, j, :].unsqueeze(2).broadcast_to([P, H, HD]),
                                          ALU.mult).then_inc(o_out, 1)
                        if j:
                            sum_o(j - 1)
                    link(sum_o(NT - 1))
                    ssh, hr, hf, ht = SSH[:, :, 0:H], HR[:, :, 0:H], HF[:, :, 0:H], HT2[:, :, 0:H]
                    ask(dve.tensor_scalar(ssh, ssh, EPS2, None, ALU.max))
                    newton(hr, ssh, ht)
                    link(dve.tensor_scalar(hf, hr, ATANH_MAX, 1.0, ALU.mult, ALU.min))
                    link(dve.tensor_tensor(ht, hf, hf, ALU.mult))
                    link(dve.tensor_tensor(ht, ht, ssh, ALU.mult))
                    link(dve.tensor_reduce(c(0), ht, AX.X, ALU.add))
                    ask(dve.tensor_scalar(c(0), c(0), 1.0 / TO_HEADS ** 2, EPS2, ALU.mult, ALU.max))
                    newton(c(1), c(0), c(16))
                    link(dve.tensor_scalar(c(2), c(1), ATANH_MAX, 1.0, ALU.mult, ALU.min))
                    link(dve.tensor_scalar(c(2), c(2), 1.0 / TO_HEADS, None, ALU.mult))
                    link(dve.tensor_tensor(hf, hf, c(2).unsqueeze(2).broadcast_to([P, NT, H]), ALU.mult))
                    for j in range(NT):
                        dve.tensor_tensor(AT[:, j, :].rearrange("p (h d) -> p h d", d=HD), OV[:, j, :, :], heads(j, 0, H),
                                          ALU.mult).then_inc(attn_in, 1)
                    for j in range(NT):
                        dve.wait_ge(attn_mm, i * NT + j + 1)
                        dve.tensor_tensor(AT[:, j, :], bank(4 + j % 2, 0, D), bias_o[:], ALU.add).then_inc(attn_out, 1)

                    def mobius(r, src, gain, out):
                        dve.wait_ge(attn_ss, i * NT * 4 + r * NT * 2 + NT)
                        clamp(9, 10, 10)
                        for j in range(NT):
                            dve.scalar_tensor_tensor(AT[:, j, :], AT[:, j, :], C[:, 10, j:j + 1], ada[:, i, gain, :],
                                                     ALU.mult, ALU.mult).then_inc(attn_out, 1)
                            dve.wait_ge(attn_out, i * NT * 4 + r * NT * 2 + NT + j + 1)
                            link(dve.scalar_tensor_tensor(JKV[:], src(j), 1.0, AT[:, j, :], ALU.mult, ALU.mult,
                                                          accum_out=C[:, 16, j:j + 1]))
                        dve.wait_ge(attn_ss, i * NT * 4 + r * NT * 2 + 2 * NT)
                        ask(dve.tensor_scalar(c(12), c(11), EPS2, None, ALU.max))
                        newton(c(13), c(12), c(17))
                        ask(dve.tensor_tensor(c(14), c(12), c(13), ALU.mult))
                        answered()
                        link(dve.tensor_tensor(c(17), c(15), c(13), ALU.mult))
                        link(dve.tensor_tensor(c(18), c(17), c(17), ALU.mult))
                        link(dve.tensor_tensor(c(18), c(18), c(11), ALU.mult))
                        link(dve.tensor_tensor(c(19), c(17), c(16), ALU.mult))
                        link(dve.tensor_scalar(c(19), c(19), 2.0, 1.0, ALU.mult, ALU.add))
                        link(dve.tensor_tensor(c(2), c(19), c(18), ALU.add))
                        link(dve.tensor_tensor(c(3), c(22), c(18), ALU.mult))
                        link(dve.tensor_tensor(c(3), c(3), c(19), ALU.add))
                        link(dve.tensor_scalar(c(3), c(3), EPS, None, ALU.max))
                        link(dve.reciprocal(c(3), c(3)))
                        link(dve.tensor_tensor(c(4), c(2), c(3), ALU.mult))
                        link(dve.tensor_scalar(c(5), c(22), -1.0, 1.0, ALU.mult, ALU.add))
                        link(dve.tensor_tensor(c(5), c(5), c(3), ALU.mult))
                        link(dve.tensor_tensor(c(5), c(5), c(17), ALU.mult))
                        for j in range(NT):
                            link(dve.tensor_scalar(AT[:, j, :], AT[:, j, :], C[:, 5, j:j + 1], None, ALU.mult))
                            link(dve.scalar_tensor_tensor(out[:, j, :], src(j), C[:, 4, j:j + 1], AT[:, j, :],
                                                          ALU.mult, ALU.add))

                    mobius(0, x_in, 2, X1)
                    norm(1, x_mid, 4, 3)
                    for j in range(NT):
                        dve.wait_ge(h_mm, i * NT + j + 1)
                        for n in range(2):
                            dve.scalar_tensor_tensor(HB[:, j, n * 512:n * 512 + 512], bank(2 * (j % 2) + n),
                                                     C[:, 19, j:j + 1], bias_f1[:, n * 512:n * 512 + 512],
                                                     ALU.mult, ALU.add).then_inc(h_out, 1)
                    dve.wait_ge(h_ss, i * NT + NT)
                    clamp(7, 8, 19)
                    for j in range(NT):
                        dve.wait_ge(ff_mm, i * NT + j + 1)
                        dve.scalar_tensor_tensor(AT[:, j, :], bank((6, 7, 0, 1)[j], 0, D),
                                                 C[:, 19, j:j + 1], bias_f2[:], ALU.mult, ALU.add).then_inc(attn_out, 1)
                    mobius(1, x_mid, 5, X2)
                    for j in range(NT):
                        dve.tensor_tensor(X2[:, j, :], X2[:, j, :], x_in(j), ALU.add).then_inc(x_out, 1)
                    for j in range(NT):
                        dve.wait_ge(x_turned, i * NT + j + 1)
                        dve.tensor_copy(XT[:].rearrange("p k (t b) -> p k t b", b=B)[:, :, j * P:j * P + P, bass.ds(i, 1)],
                                        bank(j % 2, 0, D).rearrange("p (k t a) -> p k t a", k=2, a=1)).then_inc(x_copied, 1)
                    assert (step[0], col[0], done[0]) == (DVE_STEPS, COLS, COLS), (step, col, done)


def gru(nc, w_x, u_h, c_v, b_v, cond_t, XT, ident_bf):
    with ExitStack() as ctx:
        def sb(name, shape, dt=F32):
            return ctx.enter_context(nc.sbuf_tensor(name, shape, dt))

        def sem(name):
            return ctx.enter_context(nc.semaphore(name))

        Wx = sb("w_x_sb", [P, 2, 3 * D])
        Uf = sb("u_h_sb", [P, 2, 3 * D])
        Ur = sb("u_rest", [P, 2, 3 * D])
        U = sb("u_parts", [P, 3, 2, 3 * D], BF16)
        Cv = sb("c_v_sb", [P, 2, 3 * D])
        cond = sb("cond_v", [P, 2, B])
        bias = sb("gru_bias", [B, 3 * D])
        V = sb("v_sum", [B, 3 * D])
        V1 = sb("v_parts", [B, 3, 3 * D], BF16)
        pick = sb("pick_batch", [B, CH, B], BF16)
        HS = sb("states", [P, 2, 2 * CH + 1, B])
        HP = sb("state_parts", [P, 2, 2, B], F16)
        RP = sb("reset_parts", [P, 2, 2, B], F16)
        RH = sb("reset_state", [P, 2, B])
        G = sb("gates", [P, 3, 2, B])
        KEEP = sb("kept", [P, 2, B])
        NEW = sb("new", [P, 2, B])
        PS = ctx.enter_context(nc.psum_tensor("gate_sums", [P, 2, 3, 512], F32))

        w_in, c_in = sem("gru_weights"), sem("gru_c")
        prep, v_mm, v_ready = sem("gru_prep"), sem("v_mm"), sem("v_ready")
        x_sum = sem("x_sum")
        r_mm, z_mm, n_mm = sem("r_mm"), sem("z_mm"), sem("n_mm")
        r_ready, z_ready, n_ready = sem("r_ready"), sem("z_ready"), sem("n_ready")
        ra_ready, rh_ready, rb_ready = sem("ra_ready"), sem("rh_ready"), sem("rb_ready")
        zh_ready, keep_ready, new_ready = sem("zh_ready"), sem("keep_ready"), sem("new_ready")
        ha_ready, h_ready, hb_ready = sem("ha_ready"), sem("h_ready"), sem("hb_ready")
        x_added = sem("x_added")
        N = 2 * CH
        STATE = 2.0 ** 10

        def gate(half, g):
            return PS[:, half, g, 0:CH * 2 * B].rearrange("p (t m b) -> p t m b", m=2, b=B)

        with nc.Block() as block:
            @block.sync
            def _(sp):
                sp.dma_start(Cv[:], c_v.rearrange("(k p) n -> p k n", p=P)).then_inc(c_in, 16)
                sp.dma_start(cond[:], cond_t.rearrange("(k p) b -> p k b", p=P)).then_inc(c_in, 16)
                sp.dma_start(bias[:], b_v.rearrange("(a n) -> a n", a=1).broadcast_to([B, 3 * D])).then_inc(c_in, 16)
                sp.dma_start(Wx[:], w_x.rearrange("(k p) n -> p k n", p=P)).then_inc(w_in, 16)
                sp.dma_start(Uf[:], u_h.rearrange("(k p) n -> p k n", p=P)).then_inc(w_in, 16)

            @block.tensor
            def _(pe):
                pe.wait_ge(c_in, 48)
                for n, (a, z) in enumerate(((0, 512), (512, 768))):
                    for k in range(2):
                        mm = pe.matmul(PS[0:B, 0, n, 0:z - a], cond[:, k, :], Cv[:, k, a:z], start=(k == 0), stop=(k == 1))
                mm.then_inc(v_mm, 1)
                pe.wait_ge(v_ready, 5)
                pe.wait_ge(w_in, 32)

                def project(half, at, pieces):
                    for g, m in pieces:
                        w = slice(g * D + m * P, g * D + m * P + P)
                        out = gate(half, g)[:, :, m, :]
                        for k in range(2):
                            pe.matmul(out, Wx[:, k, w], XT[:, k, bass.ds(at, CH * B)].rearrange("p (t b) -> p t b", b=B),
                                      start=(m == 0 and k == 0), stop=False, skip_group_check=True)
                        for part in range(3):
                            mm = pe.matmul(out, V1[:, part, w], pick[:], start=False, stop=True, skip_group_check=True)
                    return mm

                PIECES = [(g, m) for g in (1, 0, 2) for m in range(2)]
                project(0, 0, PIECES).then_inc(x_sum, 1)

                def state_share(out, g, parts, first, second):
                    for (ready, value), part, pieces in ((first, 0, 3), (second, 1, 2)):
                        pe.wait_ge(ready, value)
                        for m in range(2):
                            w = slice(g * D + m * P, g * D + m * P + P)
                            for k in range(2):
                                for u in range(pieces):
                                    mm = pe.matmul(out[:, m, :], U[:, u, k, w], parts[:, part, k, :],
                                                   start=False, stop=(part == 1), skip_group_check=True)
                    return mm

                with pe.Fori(0, S // N) as i:
                    for s in range(N):
                        half, t = s // CH, s % CH
                        a, b = (ha_ready, i * N + s + 1), (hb_ready, i * N + s + 1)
                        state_share(gate(half, 1)[:, t, :, :], 1, HP, a, b).then_inc(r_mm, 1)
                        state_share(gate(half, 0)[:, t, :, :], 0, HP, a, b).then_inc(z_mm, 1)
                        if t % 2 == 0 and t // 2 < 6:
                            nxt = i * N * B + (half + 1) * CH * B
                            project(1 - half, nxt, [PIECES[t // 2]])
                        state_share(gate(half, 2)[:, t, :, :], 2, RP, (ra_ready, i * N + s + 1),
                                    (rb_ready, i * N + s + 1)).then_inc(n_mm, 1)

            @block.scalar
            def _(act):
                act.preload_act_table_set("sigmoid_and_others")
                with act.Fori(0, S // N) as i:
                    for s in range(N):
                        half, t = s // CH, s % CH
                        act.wait_ge(r_mm, i * N + s + 1)
                        act.activation(G[:, 1, :, :], gate(half, 1)[:, t, :, :], ACT.Sigmoid).then_inc(r_ready, 1)
                        act.wait_ge(z_mm, i * N + s + 1)
                        act.activation(G[:, 0, :, :], gate(half, 0)[:, t, :, :], ACT.Sigmoid).then_inc(z_ready, 1)
                        act.wait_ge(n_mm, i * N + s + 1)
                        act.activation(G[:, 2, :, :], gate(half, 2)[:, t, :, :], ACT.Tanh).then_inc(n_ready, 1)

            @block.vector
            def _(dve):
                dve.memset(HS[:, :, 0, :], 0.0).then_inc(h_ready, 1)
                dve.memset(HP[:], 0.0).then_inc(ha_ready, 1)
                dve.tensor_copy(pick[:], ident_bf[0:B, 0:B].unsqueeze(1).broadcast_to([B, CH, B])).then_inc(v_ready, 1)
                dve.wait_ge(w_in, 32)
                dve.tensor_scalar(Uf[:], Uf[:], 1.0 / STATE, None, ALU.mult).then_inc(prep, 1)
                dve.wait_ge(prep, 1)
                dve.tensor_copy(U[:, 0, :, :], Uf[:]).then_inc(prep, 1)
                dve.wait_ge(prep, 2)
                dve.tensor_tensor(Ur[:], Uf[:], U[:, 0, :, :], ALU.subtract).then_inc(prep, 1)
                dve.wait_ge(prep, 3)
                dve.tensor_copy(U[:, 1, :, :], Ur[:]).then_inc(prep, 1)
                dve.wait_ge(prep, 4)
                dve.tensor_tensor(U[:, 2, :, :], Ur[:], U[:, 1, :, :], ALU.subtract).then_inc(v_ready, 1)
                dve.wait_ge(v_mm, 1)
                dve.tensor_tensor(V[:, 0:512], PS[0:B, 0, 0, :], bias[:, 0:512], ALU.add).then_inc(prep, 1)
                dve.tensor_tensor(V[:, 512:768], PS[0:B, 0, 1, 0:256], bias[:, 512:768], ALU.add).then_inc(prep, 1)
                dve.wait_ge(prep, 6)
                dve.tensor_copy(V1[:, 0, :], V[:]).then_inc(v_ready, 1)
                dve.wait_ge(v_ready, 3)
                dve.tensor_tensor(V[:], V[:], V1[:, 0, :], ALU.subtract).then_inc(prep, 1)
                dve.wait_ge(prep, 7)
                dve.tensor_copy(V1[:, 1, :], V[:]).then_inc(v_ready, 1)
                dve.wait_ge(v_ready, 4)
                dve.tensor_tensor(V1[:, 2, :], V[:], V1[:, 1, :], ALU.subtract).then_inc(v_ready, 1)
                dve.memset(KEEP[:], 0.0).then_inc(hb_ready, 1)

                with dve.Fori(0, S // N) as i:
                    for s in range(N):
                        at = i * N + s + 1
                        old, new = HS[:, :, s, :], HS[:, :, s + 1, :]
                        dve.wait_ge(h_ready, at)
                        dve.wait_ge(r_ready, at)
                        dve.tensor_tensor(RP[:, 0, :, :], G[:, 1, :, :], old, ALU.mult).then_inc(ra_ready, 1)
                        dve.tensor_tensor(RH[:], G[:, 1, :, :], old, ALU.mult).then_inc(rh_ready, 1)
                        dve.wait_ge(ra_ready, at)
                        dve.wait_ge(rh_ready, at)
                        dve.tensor_tensor(RP[:, 1, :, :], RH[:], RP[:, 0, :, :], ALU.subtract).then_inc(rb_ready, 1)
                        dve.wait_ge(z_ready, at)
                        dve.tensor_tensor(KEEP[:], G[:, 0, :, :], old, ALU.mult).then_inc(zh_ready, 1)
                        dve.wait_ge(zh_ready, at)
                        dve.tensor_tensor(KEEP[:], old, KEEP[:], ALU.subtract).then_inc(keep_ready, 1)
                        dve.wait_ge(n_ready, at)
                        dve.scalar_tensor_tensor(NEW[:], G[:, 2, :, :], STATE, G[:, 0, :, :], ALU.mult,
                                                 ALU.mult).then_inc(new_ready, 1)
                        dve.wait_ge(keep_ready, at)
                        dve.wait_ge(new_ready, at)
                        dve.tensor_tensor(HP[:, 0, :, :], KEEP[:], NEW[:], ALU.add).then_inc(ha_ready, 1)
                        dve.tensor_tensor(new, KEEP[:], NEW[:], ALU.add).then_inc(h_ready, 1)
                        dve.wait_ge(ha_ready, at + 1)
                        dve.wait_ge(h_ready, at + 1)
                        dve.tensor_tensor(HP[:, 1, :, :], new, HP[:, 0, :, :], ALU.subtract).then_inc(hb_ready, 1)
                    dve.tensor_copy(HS[:, :, 0, :], HS[:, :, N, :])
                    xs = XT[:, :, bass.ds(i * N * B, N * B)]
                    dve.scalar_tensor_tensor(xs, HS[:, :, 1:N + 1, :].rearrange("p k t b -> p k (t b)"), 1.0 / STATE, xs,
                                             ALU.mult, ALU.add).then_inc(x_added, 1)
                    dve.wait_ge(x_added, i + 1)


def top_two(dve, link, scores, picked, t, m, rank, shape):
    def over(v):
        return v.unsqueeze(len(shape) - 1).broadcast_to(shape)

    one = t[1]
    for n in range(2):
        link(dve.tensor_reduce(m, scores, AX.X, ALU.max))
        link(dve.tensor_tensor(t[0], scores, over(m), ALU.is_equal))
        link(dve.tensor_tensor(t[0], t[0], rank, ALU.mult))
        link(dve.tensor_reduce(m, t[0], AX.X, ALU.max))
        link(dve.tensor_tensor(one, t[0], over(m), ALU.is_equal))
        if n == 0:
            link(dve.tensor_copy(picked, one))
            link(dve.scalar_tensor_tensor(scores, one, -1e30, scores, ALU.mult, ALU.add))
        else:
            link(dve.tensor_tensor(picked, picked, one, ALU.add))


def shared_and_routed(nc, w_router, router_bias, s_w1, s_w3, s_w2, r_w1, r_w2, cond_t, XT, ident):
    NS, NE = s_w1.shape[0], r_w1.shape[0]
    HS_T, HR_T = s_w1.shape[2] // P, r_w1.shape[2] // P
    T = XT_COLS // P
    with ExitStack() as ctx:
        def sb(name, shape, dt=F32):
            return ctx.enter_context(nc.sbuf_tensor(name, shape, dt))

        def sem(name):
            return ctx.enter_context(nc.semaphore(name))

        SW1 = sb("s_w1_sb", [P, NS, 2, HS_T * P])
        SW3 = sb("s_w3_sb", [P, NS, 2, HS_T * P])
        SW2 = sb("s_w2_sb", [P, NS, HS_T, D])
        RW1 = sb("r_w1_sb", [P, NE, 2, HR_T * P])
        RW2 = sb("r_w2_sb", [P, NE, HR_T, D])
        WR = sb("w_router_sb", [P, 4, NE])
        cond = sb("cond_r", [P, 2, B])
        cond_rep = sb("cond_cols", [P, 2, P])
        bias = sb("router_bias_sb", [P, NE])
        rank = sb("rank", [P, NE])
        SIG = sb("router_scores", [P, T, NE])
        SEL = sb("selection", [P, T, NE])
        BOTH = sb("picked_two", [P, T, NE])
        T0 = sb("router_t0", [P, T, NE])
        T1 = sb("router_t1", [P, T, NE])
        M = sb("router_m", [P, 3, T])
        CL = sb("cond_logits", [P, NE])
        GT = sb("gates_t", [NE, XT_COLS])
        pick = sb("pick_expert", [NE, NE, P])
        A1 = sb("activated", [P, 2, 512])
        HB = sb("hidden_2", [P, 3, 512])
        PS = ctx.enter_context(nc.psum_tensor("ps2", [P, 8, 512], F32))
        OUT, PAIR, GATE = 0, 2, 6

        w_in, r_in = sem("moe_weights"), sem("router_in")
        step, rows_ready, logit_mm, scored = sem("router_step"), sem("rows_ready"), sem("logit_mm"), sem("scored")
        gates_ready, gates_turned, gates_copied = sem("gates_ready"), sem("gates_turned"), sem("gates_copied")
        first_mm, gate_mm, activated, h_ready, second_mm, added = (
            sem("first_mm"), sem("gate_mm"), sem("activated"), sem("hidden_ready"), sem("second_mm"), sem("added"))

        units = [("s", e, m) for e in range(NS) for m in range(HS_T)] + [("r", e, m) for e in range(NE) for m in range(HR_T)]
        NU = len(units)

        with nc.Block() as block:
            @block.sync
            def _(sp):
                sp.dma_start(WR[:], w_router.rearrange("(k p) n -> p k n", p=P)).then_inc(r_in, 16)
                sp.dma_start(cond[:], cond_t.rearrange("(k p) b -> p k b", p=P)).then_inc(r_in, 16)
                sp.dma_start(bias[:], router_bias.rearrange("(a n) -> a n", a=1).broadcast_to([P, NE])).then_inc(r_in, 16)
                for dst, src in ((SW1, s_w1), (SW3, s_w3), (SW2, s_w2), (RW1, r_w1), (RW2, r_w2)):
                    for e in range(src.shape[0]):
                        sp.dma_start(dst[:, e, :, :], src[e].rearrange("(k p) n -> p k n", p=P)).then_inc(w_in, 16)
            WEIGHTS = 16 * (3 * NS + 2 * NE)

            @block.tensor
            def _(pe):
                pe.wait_ge(r_in, 48)
                pe.wait_ge(rows_ready, 1)
                for k in range(2):
                    pe.matmul(PS[:, 1, 0:NE], cond_rep[:, k, :], WR[:, 2 + k, :], start=(k == 0), stop=(k == 1))
                for t in range(T):
                    for k in range(2):
                        mm = pe.matmul(PS[:, 0, t * NE:t * NE + NE], XT[:, k, t * P:t * P + P], WR[:, k, :],
                                       start=(k == 0), stop=(k == 1), skip_group_check=True)
                mm.then_inc(logit_mm, 1)
                pe.wait_ge(gates_ready, 1)
                for t in range(T):
                    mm = pe.transpose(PS[0:NE, 2 + t // 4, t % 4 * P:t % 4 * P + P], BOTH[:, t, :], ident[:])
                mm.then_inc(gates_turned, 1)
                pe.wait_ge(gates_copied, 1)
                pe.wait_ge(w_in, WEIGHTS)
                with pe.Fori(0, XT_COLS // 512) as i:
                    def second(u):
                        kind, e, m = units[u]
                        w = SW2 if kind == "s" else RW2
                        pe.wait_ge(h_ready, i * NU + u + 1)
                        for f in range(2):
                            mm = pe.matmul(PS[:, OUT + f, :], w[:, e, m, f * P:f * P + P], HB[:, u % 3, :],
                                           start=(u == 0), stop=(u == NU - 1), skip_group_check=True)
                        mm.then_inc(second_mm, 1)

                    for u, (kind, e, m) in enumerate(units):
                        if u >= 2:
                            pe.wait_ge(h_ready, i * NU + u - 1)
                        pair = PAIR + 2 * (u % 2)
                        for n, w in enumerate((SW1, SW3) if kind == "s" else (RW1,)):
                            for k in range(2):
                                mm = pe.matmul(PS[:, pair + n, :], w[:, e, k, m * P:m * P + P],
                                               XT[:, k, bass.ds(i * 512, 512)], start=(k == 0), stop=(k == 1))
                        mm.then_inc(first_mm, 1)
                        if kind == "r" and m == 0:
                            pe.matmul(PS[:, GATE + e % 2, :], pick[:, e, :], GT[:, bass.ds(i * 512, 512)],
                                      start=True, stop=True).then_inc(gate_mm, 1)
                        if u == 1:
                            pe.wait_ge(added, 2 * i + 1)
                        if u:
                            second(u - 1)
                    second(NU - 1)

            @block.scalar
            def _(act):
                act.wait_ge(logit_mm, 1)
                act.wait_ge(rows_ready, 2)
                act.activation(SIG[:], SEL[:], ACT.Sigmoid).then_inc(scored, 1)
                with act.Fori(0, XT_COLS // 512) as i:
                    for u, (kind, e, m) in enumerate(units):
                        act.wait_ge(first_mm, i * NU + u + 1)
                        if u >= 2:
                            act.wait_ge(h_ready, i * NU + u - 1)
                        act.activation(A1[:, u % 2, :], PS[:, PAIR + 2 * (u % 2), :],
                                       ACT.Silu if kind == "s" else ACT.Gelu).then_inc(activated, 1)

            @block.vector
            def _(dve):
                count = [0]

                def link(ins):
                    count[0] += 1
                    ins.then_inc(step, 1)
                    dve.wait_ge(step, count[0])

                for e in range(NE):
                    dve.memset(rank[:, e:e + 1], float(NE - e))
                link(dve.tensor_copy(pick[:], ident[0:NE, 0:NE].unsqueeze(2).broadcast_to([NE, NE, P])))
                dve.wait_ge(r_in, 48)
                dve.tensor_copy(cond_rep[:].rearrange("p k (t b) -> p k t b", b=B),
                                cond[:].unsqueeze(2).broadcast_to([P, 2, P // B, B])).then_inc(rows_ready, 1)
                dve.wait_ge(logit_mm, 1)
                link(dve.tensor_copy(CL[:], PS[:, 1, 0:NE]))
                dve.tensor_tensor(SEL[:], PS[:, 0, 0:T * NE].rearrange("p (t e) -> p t e", e=NE),
                                  CL[:].unsqueeze(1).broadcast_to([P, T, NE]), ALU.add).then_inc(rows_ready, 1)
                dve.wait_ge(scored, 1)
                link(dve.tensor_tensor(SEL[:], SIG[:], bias[:].unsqueeze(1).broadcast_to([P, T, NE]), ALU.add))
                top_two(dve, link, SEL[:], BOTH[:], (T0[:], T1[:]), M[:, 0, :],
                        rank[:].unsqueeze(1).broadcast_to([P, T, NE]), [P, T, NE])
                link(dve.tensor_tensor(SIG[:], SIG[:], BOTH[:], ALU.mult))
                link(dve.tensor_reduce(M[:, 0, :], SIG[:], AX.X, ALU.add))
                link(dve.tensor_scalar(M[:, 1, :], M[:, 0, :], 1e-9, None, ALU.is_gt))
                link(dve.tensor_scalar(M[:, 0, :], M[:, 0, :], 1e-9, None, ALU.add))
                link(dve.reciprocal(M[:, 2, :], M[:, 0, :]))
                link(dve.tensor_tensor(M[:, 2, :], M[:, 2, :], M[:, 1, :], ALU.mult))
                link(dve.tensor_scalar(M[:, 1, :], M[:, 1, :], -0.5, 0.5, ALU.mult, ALU.add))
                link(dve.tensor_tensor(SIG[:], SIG[:], M[:, 2, :].unsqueeze(2).broadcast_to([P, T, NE]), ALU.mult))
                link(dve.tensor_tensor(BOTH[:], BOTH[:], M[:, 1, :].unsqueeze(2).broadcast_to([P, T, NE]), ALU.mult))
                dve.tensor_tensor(BOTH[:], BOTH[:], SIG[:], ALU.add).then_inc(gates_ready, 1)
                dve.sem_inc(added, 1)
                dve.wait_ge(gates_turned, 1)
                dve.tensor_copy(GT[:], PS[0:NE, 2:6, :].rearrange("p a b -> p (a b)")).then_inc(gates_copied, 1)
                with dve.Fori(0, XT_COLS // 512) as i:
                    for u, (kind, e, m) in enumerate(units):
                        dve.wait_ge(activated, i * NU + u + 1)
                        if u >= 3:
                            dve.wait_ge(second_mm, i * NU + u - 2)
                        if kind == "s":
                            dve.scalar_tensor_tensor(HB[:, u % 3, :], PS[:, PAIR + 2 * (u % 2) + 1, :], 1.0 / NS,
                                                     A1[:, u % 2, :], ALU.mult, ALU.mult).then_inc(h_ready, 1)
                        else:
                            dve.wait_ge(gate_mm, i * NE + e + 1)
                            dve.tensor_tensor(HB[:, u % 3, :], PS[:, GATE + e % 2, :], A1[:, u % 2, :],
                                              ALU.mult).then_inc(h_ready, 1)
                    dve.wait_ge(second_mm, (i + 1) * NU)
                    for f in range(2):
                        xs = XT[:, f, bass.ds(i * 512, 512)]
                        dve.scalar_tensor_tensor(xs, PS[:, OUT + f, :], 1.0 / (NS + TOP_K), xs,
                                                 ALU.mult, ALU.add).then_inc(added, 1)
                dve.wait_ge(added, 2 * (XT_COLS // 512) + 1)


def gated_experts(nc, gate_w, gate_b, time_w, time_b, ew1, ew2, sw1, sw2, b1, b2, cond_t, XT, ident, out):
    NE = ew1.shape[0]
    HT = FF // P
    L1_3 = S // 3
    with ExitStack() as ctx:
        def sb(name, shape, dt=F32):
            return ctx.enter_context(nc.sbuf_tensor(name, shape, dt))

        def sem(name):
            return ctx.enter_context(nc.semaphore(name))

        W1 = sb("e_w1", [P, NE + 1, 2, FF])
        W2 = sb("e_w2", [P, NE + 1, HT, D])
        B1 = sb("e_b1", [P, NE + 1, HT])
        B2 = sb("e_b2", [P, NE + 1, 2])
        GW = sb("gate_w_sb", [P, 6, NE])
        TW = sb("time_w_sb", [P, 2, 2 * NE])
        GB = sb("gate_b_sb", [B, NE])
        TB = sb("time_b_sb", [B, 2 * NE])
        cond = sb("cond_g", [P, 2, B])
        SC = sb("silu_cond", [P, 2, B])
        SM = sb("range_sums", [P, 3, 2, B])
        GI = sb("gate_in", [P, 3, 2, B])
        LG = sb("gate_logits", [B, NE])
        MOD = sb("modulation", [B, 2 * NE])
        rank = sb("rank3", [B, NE])
        T0 = sb("g_t0", [B, NE])
        T1 = sb("g_t1", [B, NE])
        BOTH = sb("g_picked", [B, NE])
        WS = sb("g_spoiled", [B, NE])
        M = sb("g_m", [B, 4])
        BD = sb("block_diag", [B, B, NE])
        ones = sb("ones", [B, P])
        WB = sb("weights_all", [P, B, NE])
        F = sb("token_weights", [P, NE, XT_COLS])
        A1 = sb("activated3", [P, 2, 512])
        HB = sb("hidden3", [P, 3, 512])
        PS = ctx.enter_context(nc.psum_tensor("ps3", [P, 8, 512], F32))

        w_in, g_in, silu_done = sem("e_weights"), sem("g_in"), sem("silu_done")
        step, gate_in, gate_mm, ready, exped, diag, spread = (
            sem("g_step"), sem("gate_in_s"), sem("gate_mm3"), sem("logits_ready"), sem("exped"), sem("diag"), sem("spread"))
        first_mm, activated, h_ready, second_mm, summed, stored = (
            sem("first_mm3"), sem("activated_s"), sem("hidden_ready3"), sem("second_mm3"), sem("summed"), sem("stored"))
        units = [(e, m) for e in range(NE + 1) for m in range(HT)]
        NU = len(units)
        CHUNKS = XT_COLS // 512

        with nc.Block() as block:
            @block.sync
            def _(sp):
                sp.dma_start(GW[:], gate_w.rearrange("(k p) n -> p k n", p=P)).then_inc(g_in, 16)
                sp.dma_start(TW[:], time_w.rearrange("(k p) n -> p k n", p=P)).then_inc(g_in, 16)
                sp.dma_start(cond[:], cond_t.rearrange("(k p) b -> p k b", p=P)).then_inc(g_in, 16)
                sp.dma_start(GB[:], gate_b.rearrange("(a n) -> a n", a=1).broadcast_to([B, NE])).then_inc(g_in, 16)
                sp.dma_start(TB[:], time_b.rearrange("(a n) -> a n", a=1).broadcast_to([B, 2 * NE])).then_inc(g_in, 16)
                sp.dma_start(B1[:], b1).then_inc(w_in, 16)
                sp.dma_start(B2[:], b2).then_inc(w_in, 16)
                for e in range(NE + 1):
                    w1, w2 = (ew1[e], ew2[e]) if e < NE else (sw1, sw2)
                    sp.dma_start(W1[:, e, :, :], w1.rearrange("(k p) n -> p k n", p=P)).then_inc(w_in, 16)
                    sp.dma_start(W2[:, e, :, :], w2.rearrange("(k p) n -> p k n", p=P)).then_inc(w_in, 16)
                with sp.Fori(0, CHUNKS) as i:
                    sp.wait_ge(summed, (i + 1) * 2 + 1)
                    sp.dma_start(out.rearrange("(k p) n -> p k n", p=P)[:, :, bass.ds(i * 512, 512)],
                                 XT[:, :, bass.ds(i * 512, 512)]).then_inc(stored, 16)
                sp.wait_ge(stored, 16 * CHUNKS)
            WEIGHTS = 16 * 2 * (NE + 2)

            @block.tensor
            def _(pe):
                pe.wait_ge(g_in, 80)
                pe.wait_ge(silu_done, 1)
                for k in range(2):
                    pe.matmul(PS[0:B, 0, 0:2 * NE], SC[:, k, :], TW[:, k, :], start=(k == 0), stop=(k == 1))
                pe.wait_ge(gate_in, 1)
                for k in range(6):
                    mm = pe.matmul(PS[0:B, 1, 0:NE], GI[:, k // 2, k % 2, :], GW[:, k, :], start=(k == 0), stop=(k == 5))
                mm.then_inc(gate_mm, 1)
                pe.wait_ge(diag, 1)
                pe.matmul(PS[:, 2, 0:B * NE], ones[:], BD[:].rearrange("p b e -> p (b e)"),
                          start=True, stop=True).then_inc(spread, 1)
                pe.wait_ge(w_in, WEIGHTS)
                with pe.Fori(0, CHUNKS) as i:
                    def second(u):
                        e, m = units[u]
                        pe.wait_ge(h_ready, i * NU + u + 1)
                        for f in range(2):
                            mm = pe.matmul(PS[:, f, :], W2[:, e, m, f * P:f * P + P], HB[:, u % 3, :],
                                           start=(u == 0), stop=(u == NU - 1), skip_group_check=True)
                        mm.then_inc(second_mm, 1)

                    for u, (e, m) in enumerate(units):
                        if u >= 3:
                            pe.wait_ge(activated, i * NU + u - 2)
                        for k in range(2):
                            mm = pe.matmul(PS[:, 3 + u % 3, :], W1[:, e, k, m * P:m * P + P],
                                           XT[:, k, bass.ds(i * 512, 512)], start=(k == 0), stop=(k == 1))
                        mm.then_inc(first_mm, 1)
                        if u == 1:
                            pe.wait_ge(summed, 2 * i + 1)
                        if u:
                            second(u - 1)
                    second(NU - 1)

            @block.scalar
            def _(act):
                act.wait_ge(g_in, 80)
                act.activation(SC[:], cond[:], ACT.Silu).then_inc(silu_done, 1)
                act.wait_ge(ready, 1)
                act.activation(LG[:], LG[:], ACT.Exp, bias=M[:, 1:2], accum_out=M[:, 2:3]).then_inc(exped, 1)
                act.wait_ge(w_in, WEIGHTS)
                with act.Fori(0, CHUNKS) as i:
                    for u, (e, m) in enumerate(units):
                        act.wait_ge(first_mm, i * NU + u + 1)
                        if u >= 2:
                            act.wait_ge(h_ready, i * NU + u - 1)
                        act.activation(A1[:, u % 2, :], PS[:, 3 + u % 3, :], ACT.Gelu_apprx_tanh,
                                       bias=B1[:, e, m:m + 1]).then_inc(activated, 1)

            @block.vector
            def _(dve):
                count = [0]

                def link(ins):
                    count[0] += 1
                    ins.then_inc(step, 1)
                    dve.wait_ge(step, count[0])

                for e in range(NE):
                    dve.memset(rank[:, e:e + 1], float(NE - e))
                dve.memset(ones[:], 1.0)
                x4 = XT[:, :, 0:XT_COLS].rearrange("p k (t b) -> p k b t", b=B)
                bounds = (0, L1_3, 2 * L1_3, S)
                for r in range(3):
                    ins = dve.tensor_reduce(SM[:, r, :, :], x4[:, :, :, bounds[r]:bounds[r + 1]], AX.X, ALU.add)
                link(ins)
                both = float(S - L1_3)
                dve.tensor_tensor(GI[:, 1, :, :], SM[:, 0, :, :], SM[:, 2, :, :], ALU.add)
                dve.tensor_tensor(GI[:, 2, :, :], SM[:, 1, :, :], SM[:, 2, :, :], ALU.add)
                link(dve.tensor_tensor(GI[:, 0, :, :], SM[:, 0, :, :], SM[:, 1, :, :], ALU.add))
                link(dve.tensor_tensor(GI[:, 0, :, :], GI[:, 0, :, :], SM[:, 2, :, :], ALU.add))
                link(dve.tensor_scalar(GI[:, 0, :, :], GI[:, 0, :, :], 1.0 / S, None, ALU.mult))
                dve.tensor_scalar(GI[:, 1:3, :, :], GI[:, 1:3, :, :], 1.0 / both, None, ALU.mult).then_inc(gate_in, 1)
                dve.wait_ge(gate_mm, 1)
                dve.wait_ge(g_in, 80)
                link(dve.tensor_tensor(LG[:], PS[0:B, 1, 0:NE], GB[:], ALU.add))
                link(dve.tensor_tensor(MOD[:], PS[0:B, 0, 0:2 * NE], TB[:], ALU.add))
                link(dve.scalar_tensor_tensor(LG[:], MOD[:, 0:NE], 1.0, LG[:], ALU.add, ALU.mult))
                link(dve.tensor_tensor(LG[:], LG[:], MOD[:, NE:2 * NE], ALU.add))
                link(dve.tensor_reduce(M[:, 0:1], LG[:], AX.X, ALU.max))
                dve.tensor_scalar(M[:, 1:2], M[:, 0:1], -1.0, None, ALU.mult).then_inc(ready, 1)
                dve.wait_ge(exped, 1)
                link(dve.reciprocal(M[:, 3:4], M[:, 2:3]))
                link(dve.tensor_scalar(LG[:], LG[:], M[:, 3:4], None, ALU.mult))
                link(dve.tensor_copy(WS[:], LG[:]))
                rows = [v[:].unsqueeze(1) for v in (WS, BOTH, T0, T1, rank)]
                top_two(dve, link, rows[0], rows[1], rows[2:4], M[:, 0:1], rows[4], [B, 1, NE])
                link(dve.tensor_tensor(BOTH[:], BOTH[:], LG[:], ALU.mult))
                link(dve.tensor_reduce(M[:, 0:1], BOTH[:], AX.X, ALU.add))
                link(dve.tensor_scalar(M[:, 0:1], M[:, 0:1], 1e-8, None, ALU.add))
                link(dve.reciprocal(M[:, 3:4], M[:, 0:1]))
                link(dve.tensor_scalar(BOTH[:], BOTH[:], M[:, 3:4], None, ALU.mult))
                dve.tensor_tensor(BD[:], BOTH[:].unsqueeze(1).broadcast_to([B, B, NE]),
                                  ident[0:B, 0:B].unsqueeze(2).broadcast_to([B, B, NE]), ALU.mult).then_inc(diag, 1)
                dve.wait_ge(spread, 1)
                link(dve.tensor_copy(WB[:].rearrange("p b e -> p (b e)"), PS[:, 2, 0:B * NE]))
                for e in range(NE):
                    f = F[:, e, :].rearrange("p (t b) -> p t b", b=B)
                    ins = dve.tensor_copy(f, WB[:, :, e].unsqueeze(1).broadcast_to([P, S, B]))
                link(ins)
                dve.memset(F[:, 1, L1_3 * B:2 * L1_3 * B], 0.0)
                link(dve.memset(F[:, 2, 0:L1_3 * B], 0.0))
                dve.wait_ge(w_in, WEIGHTS)
                dve.sem_inc(summed, 1)
                SUMS = 8
                before = count[0]
                with dve.Fori(0, CHUNKS) as i:
                    for u, (e, m) in enumerate(units):
                        dve.wait_ge(activated, i * NU + u + 1)
                        if u >= 3:
                            dve.wait_ge(second_mm, i * NU + u - 2)
                        if e < NE:
                            dve.tensor_tensor(HB[:, u % 3, :], A1[:, u % 2, :], F[:, e, bass.ds(i * 512, 512)],
                                              ALU.mult).then_inc(h_ready, 1)
                        else:
                            dve.tensor_copy(HB[:, u % 3, :], A1[:, u % 2, :]).then_inc(h_ready, 1)
                    dve.wait_ge(second_mm, (i + 1) * NU)
                    k = 0
                    for f in range(2):
                        xs = XT[:, f, bass.ds(i * 512, 512)]
                        dve.scalar_tensor_tensor(xs, PS[:, f, :], B2[:, NE, f:f + 1], xs, ALU.add, ALU.add).then_inc(step, 1)
                        k += 1
                        for e in range(NE):
                            dve.wait_ge(step, before + i * SUMS + k)
                            ins = dve.scalar_tensor_tensor(xs, F[:, e, bass.ds(i * 512, 512)], B2[:, e, f:f + 1], xs,
                                                           ALU.mult, ALU.add)
                            if e < NE - 1:
                                ins.then_inc(step, 1)
                                k += 1
                        ins.then_inc(summed, 1)


def layers(nc, x, cond_t, l0, l1, l2, l3, eye, out):
    with ExitStack() as ctx:
        XT = ctx.enter_context(nc.sbuf_tensor("xt", [P, 2, XT_COLS + CH * B], F32))
        ident = ctx.enter_context(nc.sbuf_tensor("ident", [P, P], F32))
        ident_bf = ctx.enter_context(nc.sbuf_tensor("ident_bf", [P, P], BF16))
        eye_in, ident_ready = ctx.enter_context(nc.semaphore("eye_in")), ctx.enter_context(nc.semaphore("ident_ready"))
        with nc.Block() as block:
            @block.sync
            def _(sp):
                sp.dma_start(ident[:], eye).then_inc(eye_in, 16)

            @block.vector
            def _(dve):
                dve.memset(XT[:, :, XT_COLS:], 0.0)
                dve.wait_ge(eye_in, 16)
                dve.tensor_copy(ident_bf[:], ident[:]).then_inc(ident_ready, 1)
                dve.wait_ge(ident_ready, 1)

        hyperbolic_block(nc, x, cond_t, *l0, XT, ident, ident_bf)
        gru(nc, *l1, cond_t, XT, ident_bf)
        shared_and_routed(nc, *l2, cond_t, XT, ident)
        gated_experts(nc, *l3, cond_t, XT, ident, out)


def kernel(**inputs):
    from concourse import bacc
    from concourse.bass_utils import run_bass_kernel_spmd

    def own(name):
        return np.asarray(inputs[name])

    def joined(prefix, names):
        return np.concatenate([own(prefix + n) for n in names], axis=-1)

    def turned(name):
        return own(name).swapaxes(-1, -2)

    def features_first(prefix, routed, shared):
        both = np.concatenate([own(prefix + routed), own(prefix + shared)[None]])
        return both.reshape(len(both), -1, P).transpose(2, 0, 1)

    a, g, m, e = "L0_cond_", "L1_cond_", "L2_cond_", "L3_cond_"
    groups = {
        "x": [own("x")], "cond_t": [turned("cond_1024")],
        "l0": [joined(a, ("w_q", "w_k", "w_v")), joined(a, ("b_q", "b_k", "b_v"))]
              + [own(a + n) for n in ("w_o", "b_o", "w_f1", "b_f1", "w_f2", "b_f2", "w_ada", "b_ada")],
        "l1": [joined(g, ("W_z", "W_r", "W")), joined(g, ("U_z", "U_r", "U")), joined(g, ("C_z", "C_r", "C")),
               joined(g, ("b_z", "b_r", "b"))],
        "l2": [turned(m + "W_router"), own(m + "router_bias")] + [turned(m + n) for n in ("s_w1", "s_w3", "s_w2", "r_w1", "r_w2")],
        "l3": [own(e + n) for n in ("gate_w", "gate_b", "time_w", "time_b", "ew1", "ew2", "sw1", "sw2")]
              + [features_first(e, "eb1", "sb1"), features_first(e, "eb2", "sb2")],
        "eye": [np.eye(P, dtype=np.float32)],
    }
    nc = bacc.Bacc("TRN2", target_bir_lowering=False, num_devices=1)
    arrays, args = {}, {}
    for group, values in groups.items():
        args[group] = []
        for n, v in enumerate(values):
            name = f"in_{group}_{n}"
            arrays[name] = np.ascontiguousarray(v)
            args[group].append(nc.dram_tensor(name, arrays[name].shape, mybir.dt.from_np(arrays[name].dtype),
                                              kind="ExternalInput").ap())
    out = nc.dram_tensor("out_t", (D, XT_COLS), F32, kind="ExternalOutput").ap()
    layers(nc, args["x"][0], args["cond_t"][0], args["l0"], args["l1"], args["l2"], args["l3"], args["eye"][0], out)
    r = run_bass_kernel_spmd(nc, [arrays], core_ids=[0])
    return r.results[0]["out_t"].reshape(D, S, B).transpose(2, 1, 0)
```

```python
import math
from contextlib import ExitStack

import concourse.bass as bass
from concourse import mybir
import numpy as np

ALU = mybir.AluOpType
ACT = mybir.ActivationFunctionType
AX = mybir.AxisListType
F32 = mybir.dt.float32
F32R = mybir.dt.float32r
BF16 = mybir.dt.bfloat16
F16 = mybir.dt.float16
I32 = mybir.dt.int32

P = 128
B, S, D = 4, 512, 256
NT = S // P
H = 16
HD = D // H
FF = 1024
EPS = 1e-7
EPS2 = EPS * EPS
MAX_TANH = float(np.float32(1.0 - 1e-5))
ATANH_MAX = float(np.arctanh(np.float64(np.float32(1.0 - 1e-5))))


def beta(a, b):
    return math.exp(math.lgamma(a) + math.lgamma(b) - math.lgamma(a + b))


TO_HEADS = beta(HD / 2, 0.5) / beta(D / 2, 0.5)
SLOTS = 8
Q_SLOTS = ((0, 0, 1, 2), (0, 4, 1, 1), (1, 2, 1, 2), (1, 6, 1, 1), (2, 5, 2, 2))
K_SLOTS = ((0, 0, 2, 2), (0, 5, 1, 1), (1, 1, 2, 2), (1, 7, 1, 1), (2, 4, 2, 2))
L0_DVE_STEPS = 206
CH = 16
XT_COLS = B * S
TOP_K = 2
N_SHARED, N_ROUTED = 2, 8
HID_S, HID_R = 512, 256
PRODUCTS = ((0, 0), (0, 1), (1, 0))
L2_SHAPES = ((N_SHARED, 2, HID_S), (N_SHARED, 2, HID_S), (N_SHARED, HID_S // P, D), (N_ROUTED, 2, HID_R), (N_ROUTED, HID_R // P, D))
L2_COLS = sum(e * k * n for e, k, n in L2_SHAPES)


def parts_of(w, n):
    at = sum(e * k * c for e, k, c in L2_SHAPES[:n])
    e, k, c = L2_SHAPES[n]
    return w[:, at:at + e * k * c].rearrange("p (e k c) -> p e k c", e=e, k=k)




def hyperbolic_block(nc, x, cond_t, w_qkv, b_qkv, w_o, b_o, w_f1, b_f1, w_f2, b_f2, w_ada, b_ada, XT, ident, ident_bf):
    with ExitStack() as ctx:
        def sb(name, shape, dt=F32):
            return ctx.enter_context(nc.sbuf_tensor(name, shape, dt))

        def sem(name):
            return ctx.enter_context(nc.semaphore(name))

        X = sb("x_tokens", [P, B * NT, D])
        Wqkv = sb("w_qkv_sb", [P, 2, 3 * D])
        Wo = sb("w_o_sb", [P, 2, D])
        F1 = sb("w_f1_sb", [P, 2, FF])
        F2 = sb("w_f2_sb", [P, FF // P, D])
        cond = sb("cond_sb", [P, 2, B])
        ada = sb("ada", [P, B, 6, D])
        bias_qkv = sb("bias_qkv", [P, 3 * D])
        bias_o = sb("bias_o", [P, D])
        bias_f1 = sb("bias_f1", [P, FF])
        bias_f2 = sb("bias_f2", [P, D])
        X1 = sb("x1", [P, NT, D])
        X2 = sb("x2", [P, NT, D])
        U = sb("u", [P, NT, D])
        UT = sb("u_t", [P, NT, 2, P])
        QKV = sb("qkv", [P, NT, 3 * H, HD])
        SQ = sb("squares", [P, 2, FF])
        cond_rep = SQ[:, :, 0:B * P].rearrange("p k (b t) -> p k b t", b=B)
        QS, R1 = (SQ[:, n, 0:2 * D].rearrange("p (h d) -> p h d", d=HD) for n in range(2))
        PT = sb("qk_parts", [P, 3, 2 * H, HD], BF16)
        ST = sb("qk_stack", [P, 2 * H, SLOTS, HD], BF16)
        QKT = sb("qk_t", [P, 2 * H, S], BF16)
        early = QKT[:].rearrange("p h t -> p (h t)").bitcast(F32)
        W_ada = early[:, 0:12 * D].rearrange("p (k n) -> p k n", k=2)
        bias_ada = early[:, 12 * D:18 * D]
        VP = sb("v_ones", [P, NT, H, 32])
        PR = sb("probs", [P, 4, 2, S])
        OT = QKV[:].rearrange("p j h d -> p (j h d)")[:, 0:4 * S].rearrange("p (g t) -> p g t", g=4)
        OV = U[:].rearrange("p j (h d) -> p j h d", h=H)
        AT = sb("tangent", [P, NT, D])
        HB = PR[:].rearrange("p m c t -> p m (c t)")
        HTR = ST[:].rearrange("p h s d -> p (h s d)").bitcast(F32).rearrange("p (j f) -> p j f", j=2)
        BS = sb("bn", [P, NT, 6])
        MV = sb("mean_var", [P, 2, NT])
        C = sb("cols", [P, 24, NT])
        SSH = sb("head_ss", [P, NT, 3 * H])
        HR = sb("head_rsqrt", [P, NT, 3 * H])
        HF = sb("head_factor", [P, NT, 3 * H])
        HT2 = sb("head_tmp", [P, NT, 3 * H])
        LT = sb("log_tmp", [P, NT, 3 * H])
        T3 = sb("qkv_cols", [P, 5, NT * 3])
        RS = sb("row_recip", [P, NT, H])
        JKA = sb("junk_act", [P, D])
        JKV = sb("junk_dve", [P, D])
        PS = ctx.enter_context(nc.psum_tensor("ps", [P, 8, 512], F32))

        loads, cond_in = sem("loads"), sem("cond_in")
        cond_ready, ada_mm, ada_done = sem("cond_ready"), sem("ada_mm"), sem("ada_done")
        dve_step, act_step = sem("dve_step"), sem("act_step")
        cols_ready, cols_done = sem("cols_ready"), sem("cols_done")
        u_ready, u_turned, u_copied, u_ss = sem("u_ready"), sem("u_turned"), sem("u_copied"), sem("u_ss")
        qkv_mm, qkv_out, qkv_sq, sq_summed = sem("qkv_mm"), sem("qkv_out"), sem("qkv_sq"), sem("sq_summed")
        stacked, stack_turned = sem("stacked"), sem("stack_turned")
        stack_copied_v, stack_copied_a = sem("stack_copied_v"), sem("stack_copied_a")
        scores_mm, probs_ready, pv_mm = sem("scores_mm"), sem("probs_ready"), sem("pv_mm")
        o_copied, o_turned, o_out, o_sq = sem("o_copied"), sem("o_turned"), sem("o_out"), sem("o_sq")
        attn_in, attn_turned, attn_copied = sem("attn_in"), sem("attn_turned"), sem("attn_copied")
        attn_mm, attn_out, attn_ss = sem("attn_mm"), sem("attn_out"), sem("attn_ss")
        h_mm, h_out, h_ss, h_turned, h_copied, ff_mm = (
            sem("h_mm"), sem("h_out"), sem("h_ss"), sem("h_turned"), sem("h_copied"), sem("ff_mm"))
        x_out, x_turned, x_copied = sem("x_out"), sem("x_turned"), sem("x_copied")

        def bank(n, a=0, z=512):
            return PS[:, n, a:z]

        def bank_bf(n):
            return PS[:, n, :].bitcast(BF16)

        def flat(ap):
            return ap.rearrange("p a b -> p (a b)")

        DVE_STEPS, ACT_STEPS, COLS = L0_DVE_STEPS, 15, 19
        LOADS = 16 * 10

        with nc.Block() as block:
            @block.sync
            def _(sp):
                sp.dma_start(cond[:], cond_t.rearrange("(k p) b -> p k b", p=P)).then_inc(cond_in, 16)
                sp.dma_start(W_ada, w_ada.rearrange("(k p) n -> p k n", p=P)).then_inc(cond_in, 16)
                sp.dma_start(X[:], x.rearrange("b (j p) d -> p (b j) d", p=P)).then_inc(loads, 16)
                for dst, src in ((Wqkv, w_qkv), (Wo, w_o), (F1, w_f1), (F2, w_f2)):
                    sp.dma_start(dst[:], src.rearrange("(k p) n -> p k n", p=P)).then_inc(loads, 16)
                for dst, src in ((bias_qkv, b_qkv), (bias_o, b_o), (bias_f1, b_f1), (bias_f2, b_f2), (bias_ada, b_ada)):
                    n = src.shape[0]
                    sp.dma_start(dst[:, 0:n], src.rearrange("(a n) -> a n", a=1).broadcast_to([P, n])).then_inc(loads, 16)

            @block.tensor
            def _(pe):
                pe.wait_ge(cond_in, 32)
                pe.wait_ge(cond_ready, 1)
                for b in range(B):
                    for n in range(3):
                        g = b * 3 + n
                        if g >= 8:
                            pe.wait_ge(ada_done, g - 7)
                        for k in range(2):
                            mm = pe.matmul(bank(g % 8), cond_rep[:, k, b, :], W_ada[:, k, n * 512:(n + 1) * 512],
                                           start=(k == 0), stop=(k == 1))
                        mm.then_inc(ada_mm, 1)
                pe.wait_ge(loads, LOADS)
                pe.wait_ge(ada_done, 12)

                with pe.Fori(0, B) as i:
                    def turn(src, ready, ready_at, copied, copied_at, turned, b0):
                        for j in range(NT):
                            pe.wait_ge(ready, ready_at + j + 1)
                            if j >= 2:
                                pe.wait_ge(copied, copied_at + j - 1)
                            for k in range(2):
                                mm = pe.transpose(bank(b0 + j % 2, k * P, k * P + P), src[:, j, k * P:k * P + P], ident[:])
                            mm.then_inc(turned, 1)

                    turn(U, u_ready, i * 2 * NT, u_copied, i * 2 * NT, u_turned, 0)
                    for j in range(NT):
                        pe.wait_ge(u_copied, i * 2 * NT + j + 1)
                        if j >= 2:
                            pe.wait_ge(qkv_out, i * NT * 2 + 2 * (j - 1))
                        for a, z, bk in ((0, 512, 2 + 2 * (j % 2)), (512, 768, 3 + 2 * (j % 2))):
                            for k in range(2):
                                mm = pe.matmul(bank(bk, 0, z - a), UT[:, j, k, :], Wqkv[:, k, a:z],
                                               start=(k == 0), stop=(k == 1))
                        mm.then_inc(qkv_mm, 1)
                    for j in range(NT):
                        pe.wait_ge(stacked, i * NT * 10 + (j + 1) * 10)
                        for g in range(4):
                            n = j * 4 + g
                            if n >= 2:
                                pe.wait_ge((stack_copied_v, stack_copied_a)[n % 2], i * 8 + (n - 2) // 2 + 1)
                            for h in range(8):
                                mm = pe.transpose(bank_bf(6 + n % 2)[:, h * P:h * P + P],
                                                  flat(ST[:, g * 8 + h, :, :]), ident_bf[:])
                            mm.then_inc(stack_turned, 1)
                    pe.wait_ge(stack_copied_v, i * 8 + 8)
                    pe.wait_ge(stack_copied_a, i * 8 + 8)

                    def scores(n, e):
                        hg, kt = n // 4, n % 4
                        m = 2 * n + e
                        if m >= 3:
                            pe.wait_ge(probs_ready, i * 32 + m - 2)
                        for c in range(2):
                            h = hg * 4 + e * 2 + c
                            mm = pe.matmul(bank(2 * (m % 3) + c), QKT[:, H + h, kt * P:kt * P + P], QKT[:, h, :],
                                           start=True, stop=True)
                        mm.then_inc(scores_mm, 1)

                    def weighted(n):
                        hg, kt = n // 4, n % 4
                        pe.wait_ge(probs_ready, i * 32 + 2 * n + 2)
                        if kt == 0 and hg >= 2:
                            pe.wait_ge(o_copied, i * 4 + hg - 1)
                        for q in range(4):
                            mm = pe.matmul(PS[32 * q:32 * q + 32, 6 + hg % 2, :], VP[:, kt, hg * 4 + q, :],
                                           PR[:, (2 * n + q // 2) % 4, q % 2, :], start=(kt == 0), stop=(kt == 3),
                                           skip_group_check=True)
                        mm.then_inc(pv_mm, 1)

                    scores(0, 0)
                    scores(0, 1)
                    for n in range(16):
                        if n < 15:
                            scores(n + 1, 0)
                        weighted(n)
                        if n < 15:
                            scores(n + 1, 1)
                    for j in range(NT):
                        pe.wait_ge(o_copied, i * 4 + 4)
                        if j >= 2:
                            pe.wait_ge(o_out, i * NT + j - 1)
                        for g in range(4):
                            mm = pe.transpose(bank(j % 2, g * P, g * P + P), OT[:, g, j * P:j * P + P], ident[:])
                        mm.then_inc(o_turned, 1)
                    turn(AT, attn_in, i * NT, attn_copied, i * NT, attn_turned, 2)
                    for j in range(NT):
                        pe.wait_ge(attn_copied, i * NT + j + 1)
                        if j >= 2:
                            pe.wait_ge(attn_out, i * NT * 4 + j - 1)
                        for k in range(2):
                            mm = pe.matmul(bank(4 + j % 2, 0, D), UT[:, j, k, :], Wo[:, k, :], start=(k == 0), stop=(k == 1))
                        mm.then_inc(attn_mm, 1)
                    turn(U, u_ready, i * 2 * NT + NT, u_copied, i * 2 * NT + NT, u_turned, 6)
                    for j in range(NT):
                        pe.wait_ge(u_copied, i * 2 * NT + NT + j + 1)
                        if j >= 2:
                            pe.wait_ge(h_out, i * NT * 2 + 2 * (j - 1))
                        for c in range(2):
                            for k in range(2):
                                mm = pe.matmul(bank(2 * (j % 2) + c), UT[:, j, k, :], F1[:, k, c * 512:c * 512 + 512],
                                               start=(k == 0), stop=(k == 1))
                        mm.then_inc(h_mm, 1)
                    for j in range(NT):
                        pe.wait_ge(h_out, i * NT * 2 + 2 * (j + 1))
                        for c in range(8):
                            mm = pe.transpose(bank(4 + c // 4, c % 4 * P, c % 4 * P + P), HB[:, j, c * P:c * P + P], ident[:])
                        mm.then_inc(h_turned, 1)
                        pe.wait_ge(h_copied, i * NT + j + 1)
                        for c in range(8):
                            mm = pe.matmul(bank((6, 7, 0, 1)[j], 0, D), HTR[:, j % 2, c * P:c * P + P],
                                           F2[:, c, :], start=(c == 0), stop=(c == 7), skip_group_check=True)
                        mm.then_inc(ff_mm, 1)
                    turn(X2, x_out, i * NT, x_copied, i * NT, x_turned, 0)

            @block.scalar
            def _(act):
                act.preload_act_table_set("natural_log_exp_and_others")
                with act.Fori(0, B) as i:
                    step, col = [0], [0]

                    def arrive():
                        col[0] += 1
                        act.wait_ge(cols_ready, i * COLS + col[0])

                    def rsqrt(dst, src, tmp):
                        arrive()
                        act.activation(tmp, src, ACT.Ln).then_inc(act_step, 1)
                        step[0] += 1
                        act.wait_ge(act_step, i * ACT_STEPS + step[0])
                        act.activation(dst, tmp, ACT.Exp, scale=-0.5).then_inc(cols_done, 1)

                    def norm_and_turn(r, b0):
                        rsqrt(C[:, 1, :], C[:, 0, :], C[:, 20, :])
                        arrive()
                        act.activation(C[:, 3, :], C[:, 2, :], ACT.Ln, scale=1.0, bias=1.0)
                        act.activation(C[:, 4, :], C[:, 2, :], ACT.Ln, scale=-1.0, bias=1.0).then_inc(cols_done, 1)
                        rsqrt(C[:, 6, :], C[:, 5, :], C[:, 20, :])
                        for j in range(NT):
                            act.wait_ge(u_ready, i * 2 * NT + r * NT + j + 1)
                            if j:
                                act.wait_ge(u_ss, i * 2 * NT + r * NT + j)
                            act.activation(JKA[:], U[:, j, :], ACT.Square, accum_out=C[:, 7, j:j + 1]).then_inc(u_ss, 1)
                            act.wait_ge(u_turned, i * 2 * NT + r * NT + j + 1)
                            act.activation(flat(UT[:, j, :, :]), bank(b0 + j % 2, 0, D), ACT.Copy).then_inc(u_copied, 1)
                        rsqrt(C[:, 8, :], C[:, 7, :], C[:, 20, :])

                    norm_and_turn(0, 0)
                    for j in range(NT):
                        act.wait_ge(qkv_out, i * NT * 2 + 2 * (j + 1))
                        if j >= 2:
                            act.wait_ge(sq_summed, i * NT + j - 1)
                        act.activation(SQ[:, j % 2, 0:3 * D], flat(QKV[:, j, :, :]), ACT.Square).then_inc(qkv_sq, 1)
                    rsqrt(T3[:, 1, :], T3[:, 0, :], T3[:, 3, :])
                    rsqrt(HR[:], SSH[:], LT[:])
                    for n in range(1, 16, 2):
                        act.wait_ge(stack_turned, i * 16 + n + 1)
                        j, g = n // 4, n % 4
                        act.activation(QKT[:, g * 8:g * 8 + 8, j * P:j * P + P],
                                       bank_bf(7).rearrange("p (h t) -> p h t", t=P), ACT.Copy).then_inc(stack_copied_a, 1)
                    for m in range(32):
                        act.wait_ge(scores_mm, i * 32 + m + 1)
                        if m >= 4:
                            act.wait_ge(pv_mm, i * 16 + (m - 4) // 2 + 1)
                        act.activation(PR[:, m % 4, :, :], PS[:, 2 * (m % 3):2 * (m % 3) + 2, :], ACT.Exp,
                                       scale=1.0 / math.sqrt(HD)).then_inc(probs_ready, 1)
                    for j in range(NT):
                        act.wait_ge(o_out, i * NT + j + 1)
                        act.activation(SQ[:, j // 2, (j % 2) * D:(j % 2) * D + D], flat(OV[:, j, :, :]),
                                       ACT.Square).then_inc(o_sq, 1)
                    rsqrt(HR[:, :, 0:H], SSH[:, :, 0:H], LT[:, :, 0:H])
                    rsqrt(C[:, 1, :], C[:, 0, :], C[:, 20, :])
                    for j in range(NT):
                        act.wait_ge(attn_turned, i * NT + j + 1)
                        act.activation(flat(UT[:, j, :, :]), bank(2 + j % 2, 0, D), ACT.Copy).then_inc(attn_copied, 1)

                    def mobius(r):
                        for j in range(NT):
                            act.wait_ge(attn_out, i * NT * 4 + r * NT * 2 + j + 1)
                            if j:
                                act.wait_ge(attn_ss, i * NT * 4 + r * NT * 2 + j)
                            act.activation(JKA[:], AT[:, j, :], ACT.Square, accum_out=C[:, 9, j:j + 1]).then_inc(attn_ss, 1)
                        rsqrt(C[:, 10, :], C[:, 9, :], C[:, 20, :])
                        for j in range(NT):
                            act.wait_ge(attn_out, i * NT * 4 + r * NT * 2 + NT + j + 1)
                            if j:
                                act.wait_ge(attn_ss, i * NT * 4 + r * NT * 2 + NT + j)
                            act.activation(JKA[:], AT[:, j, :], ACT.Square, accum_out=C[:, 11, j:j + 1]).then_inc(attn_ss, 1)
                        rsqrt(C[:, 13, :], C[:, 12, :], C[:, 20, :])
                        arrive()
                        act.activation(C[:, 15, :], C[:, 14, :], ACT.Tanh).then_inc(cols_done, 1)
                        act.preload_act_table_set("natural_log_exp_and_others")

                    mobius(0)
                    norm_and_turn(1, 6)
                    for j in range(NT):
                        act.wait_ge(h_out, i * NT * 2 + 2 * (j + 1))
                        if j:
                            act.wait_ge(h_ss, i * NT + j)
                        act.activation(SQ[:, 0, :], HB[:, j, :], ACT.Square, accum_out=C[:, 7, j:j + 1]).then_inc(h_ss, 1)
                        act.wait_ge(h_turned, i * NT + j + 1)
                        if j >= 2:
                            act.wait_ge(ff_mm, i * NT + j - 1)
                        act.activation(HTR[:, j % 2, :], flat(PS[:, 4:6, :]), ACT.Copy).then_inc(h_copied, 1)
                    rsqrt(C[:, 8, :], C[:, 7, :], C[:, 20, :])
                    mobius(1)
                    assert (step[0], col[0]) == (ACT_STEPS, COLS), (step, col)

            @block.vector
            def _(dve):
                dve.wait_ge(cond_in, 32)
                dve.tensor_copy(cond_rep, cond[:].unsqueeze(3).broadcast_to([P, 2, B, P])).then_inc(cond_ready, 1)
                dve.memset(VP[:], 0.0).then_inc(cond_ready, 1)
                dve.wait_ge(cond_ready, 2)
                dve.memset(VP[:, :, :, HD:HD + 1], 1.0).then_inc(cond_ready, 1)
                dve.wait_ge(loads, LOADS)
                for b in range(B):
                    for n in range(3):
                        g = b * 3 + n
                        dve.wait_ge(ada_mm, g + 1)
                        dve.tensor_tensor(flat(ada[:, b, :, :])[:, n * 512:n * 512 + 512], bank(g % 8),
                                          bias_ada[:, n * 512:n * 512 + 512], ALU.add).then_inc(ada_done, 1)
                dve.wait_ge(ada_done, 3 * B)
                for m in (1, 4):
                    dve.tensor_scalar(ada[:, :, m, :], ada[:, :, m, :], 1.0, None, ALU.add).then_inc(cond_ready, 1)
                dve.wait_ge(cond_ready, 5)

                with dve.Fori(0, B) as i:
                    step, col, done = [0], [0], [0]

                    def link(ins):
                        step[0] += 1
                        ins.then_inc(dve_step, 1)
                        dve.wait_ge(dve_step, i * DVE_STEPS + step[0])

                    def ask(ins):
                        col[0] += 1
                        ins.then_inc(cols_ready, 1)
                        dve.wait_ge(cols_ready, i * COLS + col[0])

                    def answered():
                        done[0] += 1
                        dve.wait_ge(cols_done, i * COLS + done[0])

                    def newton(y, v, t):
                        answered()
                        link(dve.tensor_tensor(t, y, y, ALU.mult))
                        link(dve.scalar_tensor_tensor(t, t, -0.5, v, ALU.mult, ALU.mult))
                        link(dve.scalar_tensor_tensor(y, t, 1.5, y, ALU.add, ALU.mult))

                    def c(n):
                        return C[:, n, :]

                    def norm(r, src, scale, shift):
                        mean, var = MV[:, 0, :], MV[:, 1, :]
                        for j in range(NT):
                            ins = dve.bn_stats(BS[:, j, :], src(j))
                        link(ins)
                        link(dve.tensor_tensor(mean, BS[:, :, 1], BS[:, :, 4], ALU.add))
                        link(dve.tensor_scalar(mean, mean, 0.5, None, ALU.mult))
                        link(dve.tensor_tensor(c(16), BS[:, :, 1], BS[:, :, 4], ALU.subtract))
                        link(dve.tensor_tensor(c(16), c(16), c(16), ALU.mult))
                        link(dve.tensor_tensor(var, BS[:, :, 2], BS[:, :, 5], ALU.add))
                        link(dve.tensor_scalar(var, var, 1.0 / D, None, ALU.mult))
                        link(dve.scalar_tensor_tensor(var, c(16), 0.25, var, ALU.mult, ALU.add))
                        link(dve.tensor_tensor(c(21), mean, mean, ALU.mult))
                        link(dve.tensor_tensor(c(21), c(21), var, ALU.add))
                        link(dve.tensor_scalar(c(22), c(21), float(D), None, ALU.mult))
                        ask(dve.tensor_scalar(c(0), c(22), EPS2, None, ALU.max))
                        newton(c(1), c(0), c(16))
                        link(dve.tensor_tensor(c(2), c(0), c(1), ALU.mult))
                        ask(dve.tensor_scalar(c(2), c(2), MAX_TANH, None, ALU.min))
                        link(dve.tensor_tensor(c(16), c(2), c(2), ALU.mult))
                        link(dve.tensor_scalar(c(17), c(16), 1.0 / 15, None, ALU.mult))
                        for odd in (13, 11, 9, 7, 5, 3):
                            link(dve.scalar_tensor_tensor(c(17), c(17), 1.0 / odd, c(16), ALU.add, ALU.mult))
                        link(dve.scalar_tensor_tensor(c(17), c(17), 1.0, c(2), ALU.add, ALU.mult))
                        link(dve.tensor_scalar(c(18), c(2), 0.25, None, ALU.is_lt))
                        answered()
                        link(dve.tensor_tensor(c(3), c(3), c(4), ALU.subtract))
                        link(dve.scalar_tensor_tensor(c(17), c(3), -0.5, c(17), ALU.mult, ALU.add))
                        link(dve.tensor_tensor(c(17), c(17), c(18), ALU.mult))
                        link(dve.scalar_tensor_tensor(c(17), c(3), 0.5, c(17), ALU.mult, ALU.add))
                        link(dve.tensor_tensor(c(17), c(17), c(1), ALU.mult))
                        link(dve.tensor_tensor(c(16), c(17), c(17), ALU.mult))
                        link(dve.tensor_tensor(c(16), c(16), var, ALU.mult))
                        ask(dve.tensor_scalar(c(5), c(16), 1e-6, None, ALU.add))
                        newton(c(6), c(5), c(16))
                        link(dve.tensor_tensor(c(18), c(17), c(6), ALU.mult))
                        for j in range(NT):
                            link(dve.scalar_tensor_tensor(U[:, j, :], src(j), MV[:, 0, j:j + 1], ada[:, i, scale, :],
                                                          ALU.subtract, ALU.mult))
                            dve.scalar_tensor_tensor(U[:, j, :], U[:, j, :], C[:, 18, j:j + 1], ada[:, i, shift, :],
                                                     ALU.mult, ALU.add).then_inc(u_ready, 1)
                        dve.wait_ge(u_ss, i * 2 * NT + r * NT + NT)
                        clamp(7, 8, 19)

                    def clamp(ss, root, out):
                        ask(dve.tensor_scalar(c(ss), c(ss), EPS2, None, ALU.max))
                        newton(c(root), c(ss), c(16))
                        link(dve.tensor_scalar(c(out), c(root), ATANH_MAX, 1.0, ALU.mult, ALU.min))

                    def x_in(j):
                        return X[:, i * NT + j, :]

                    def x_mid(j):
                        return X1[:, j, :]

                    def heads(j, a, z):
                        return HF[:, j, a:z].unsqueeze(2).broadcast_to([P, z - a, HD])

                    norm(0, x_in, 1, 0)

                    def sum_squares(j):
                        dve.wait_ge(qkv_sq, i * NT + j + 1)
                        dve.tensor_reduce(SSH[:, j, :], SQ[:, j % 2, 0:3 * D].rearrange("p (h d) -> p h d", d=HD),
                                          AX.X, ALU.add).then_inc(sq_summed, 1)

                    for j in range(NT):
                        dve.wait_ge(qkv_mm, i * NT + j + 1)
                        out = flat(QKV[:, j, :, :])
                        for a, z, bk in ((0, 512, 2 + 2 * (j % 2)), (512, 768, 3 + 2 * (j % 2))):
                            dve.scalar_tensor_tensor(out[:, a:z], bank(bk, 0, z - a), C[:, 19, j:j + 1],
                                                     bias_qkv[:, a:z], ALU.mult, ALU.add).then_inc(qkv_out, 1)
                        if j:
                            sum_squares(j - 1)
                    sum_squares(NT - 1)
                    dve.wait_ge(sq_summed, i * NT + NT)
                    link(dve.tensor_reduce(T3[:, 0, :], SSH[:].rearrange("p j (t h) -> p (j t) h", h=H), AX.X, ALU.add))
                    ask(dve.tensor_scalar(T3[:, 0, :], T3[:, 0, :], EPS2, None, ALU.max))
                    ask(dve.tensor_scalar(SSH[:], SSH[:], EPS2, None, ALU.max))
                    newton(T3[:, 1, :], T3[:, 0, :], T3[:, 2, :])
                    link(dve.tensor_scalar(T3[:, 1, :], T3[:, 1, :], ATANH_MAX, 1.0, ALU.mult, ALU.min))
                    link(dve.tensor_scalar(T3[:, 1, :], T3[:, 1, :], TO_HEADS, None, ALU.mult))
                    newton(HR[:], SSH[:], HT2[:])
                    link(dve.scalar_tensor_tensor(HF[:].rearrange("p j (t h) -> p (j t) h", h=H),
                                                  HR[:].rearrange("p j (t h) -> p (j t) h", h=H), ATANH_MAX,
                                                  T3[:, 1, :].unsqueeze(2).broadcast_to([P, NT * 3, H]), ALU.mult, ALU.min))

                    def copy_stack(n):
                        dve.wait_ge(stack_turned, i * 16 + n + 1)
                        j, g = n // 4, n % 4
                        dve.tensor_copy(QKT[:, g * 8:g * 8 + 8, j * P:j * P + P],
                                        bank_bf(6).rearrange("p (h t) -> p h t", t=P)).then_inc(stack_copied_v, 1)

                    for j in range(NT):
                        link(dve.tensor_tensor(QS, QKV[:, j, 0:2 * H, :], heads(j, 0, 2 * H), ALU.mult))
                        dve.tensor_tensor(VP[:, j, :, 0:HD], QKV[:, j, 2 * H:3 * H, :], heads(j, 2 * H, 3 * H), ALU.mult)
                        p1, p2, p3 = (PT[:, n, :, :] for n in range(3))
                        link(dve.tensor_copy(p1, QS))
                        link(dve.tensor_tensor(R1, QS, p1, ALU.subtract))
                        link(dve.tensor_copy(p2, R1))
                        link(dve.tensor_tensor(p3, R1, p2, ALU.subtract))
                        if j:
                            copy_stack(4 * (j - 1))
                            copy_stack(4 * (j - 1) + 2)
                            dve.wait_ge(stack_turned, i * 16 + j * 4)
                        for half, copies in ((0, Q_SLOTS), (1, K_SLOTS)):
                            hs = slice(half * H, half * H + H)
                            for part, first, slot_step, n in copies:
                                dst = ST[:, hs, first:first + slot_step * (n - 1) + 1:slot_step, :]
                                src = PT[:, part, hs, :].unsqueeze(2).broadcast_to([P, H, n, HD])
                                dve.tensor_copy(dst, src).then_inc(stacked, 1)
                    copy_stack(12)
                    copy_stack(14)
                    for g in range(4):
                        dve.wait_ge(pv_mm, i * 16 + 4 * g + 4)
                        dve.tensor_copy(OT[:, g, :], bank(6 + g % 2)).then_inc(o_copied, 1)

                    def sum_o(j):
                        dve.wait_ge(o_sq, i * NT + j + 1)
                        return dve.tensor_reduce(SSH[:, j, 0:H], SQ[:, j // 2, (j % 2) * D:(j % 2) * D + D].rearrange(
                            "p (h d) -> p h d", d=HD), AX.X, ALU.add)

                    for j in range(NT):
                        dve.wait_ge(o_turned, i * NT + j + 1)
                        o = bank(j % 2).rearrange("p (h d) -> p h d", d=32)
                        link(dve.reciprocal(RS[:, j, :].unsqueeze(2), o[:, :, HD:HD + 1]))
                        dve.tensor_tensor(OV[:, j, :, :], o[:, :, 0:HD], RS[:, j, :].unsqueeze(2).broadcast_to([P, H, HD]),
                                          ALU.mult).then_inc(o_out, 1)
                        if j:
                            sum_o(j - 1)
                    link(sum_o(NT - 1))
                    ssh, hr, hf, ht = SSH[:, :, 0:H], HR[:, :, 0:H], HF[:, :, 0:H], HT2[:, :, 0:H]
                    ask(dve.tensor_scalar(ssh, ssh, EPS2, None, ALU.max))
                    newton(hr, ssh, ht)
                    link(dve.tensor_scalar(hf, hr, ATANH_MAX, 1.0, ALU.mult, ALU.min))
                    link(dve.tensor_tensor(ht, hf, hf, ALU.mult))
                    link(dve.tensor_tensor(ht, ht, ssh, ALU.mult))
                    link(dve.tensor_reduce(c(0), ht, AX.X, ALU.add))
                    ask(dve.tensor_scalar(c(0), c(0), 1.0 / TO_HEADS ** 2, EPS2, ALU.mult, ALU.max))
                    newton(c(1), c(0), c(16))
                    link(dve.tensor_scalar(c(2), c(1), ATANH_MAX, 1.0, ALU.mult, ALU.min))
                    link(dve.tensor_scalar(c(2), c(2), 1.0 / TO_HEADS, None, ALU.mult))
                    link(dve.tensor_tensor(hf, hf, c(2).unsqueeze(2).broadcast_to([P, NT, H]), ALU.mult))
                    for j in range(NT):
                        dve.tensor_tensor(AT[:, j, :].rearrange("p (h d) -> p h d", d=HD), OV[:, j, :, :], heads(j, 0, H),
                                          ALU.mult).then_inc(attn_in, 1)
                    for j in range(NT):
                        dve.wait_ge(attn_mm, i * NT + j + 1)
                        dve.tensor_tensor(AT[:, j, :], bank(4 + j % 2, 0, D), bias_o[:], ALU.add).then_inc(attn_out, 1)

                    def mobius(r, src, gain, out):
                        dve.wait_ge(attn_ss, i * NT * 4 + r * NT * 2 + NT)
                        clamp(9, 10, 10)
                        for j in range(NT):
                            dve.scalar_tensor_tensor(AT[:, j, :], AT[:, j, :], C[:, 10, j:j + 1], ada[:, i, gain, :],
                                                     ALU.mult, ALU.mult).then_inc(attn_out, 1)
                            dve.wait_ge(attn_out, i * NT * 4 + r * NT * 2 + NT + j + 1)
                            link(dve.scalar_tensor_tensor(JKV[:], src(j), 1.0, AT[:, j, :], ALU.mult, ALU.mult,
                                                          accum_out=C[:, 16, j:j + 1]))
                        dve.wait_ge(attn_ss, i * NT * 4 + r * NT * 2 + 2 * NT)
                        ask(dve.tensor_scalar(c(12), c(11), EPS2, None, ALU.max))
                        newton(c(13), c(12), c(17))
                        ask(dve.tensor_tensor(c(14), c(12), c(13), ALU.mult))
                        answered()
                        link(dve.tensor_tensor(c(17), c(15), c(13), ALU.mult))
                        link(dve.tensor_tensor(c(18), c(17), c(17), ALU.mult))
                        link(dve.tensor_tensor(c(18), c(18), c(11), ALU.mult))
                        link(dve.tensor_tensor(c(19), c(17), c(16), ALU.mult))
                        link(dve.tensor_scalar(c(19), c(19), 2.0, 1.0, ALU.mult, ALU.add))
                        link(dve.tensor_tensor(c(2), c(19), c(18), ALU.add))
                        link(dve.tensor_tensor(c(3), c(22), c(18), ALU.mult))
                        link(dve.tensor_tensor(c(3), c(3), c(19), ALU.add))
                        link(dve.tensor_scalar(c(3), c(3), EPS, None, ALU.max))
                        link(dve.reciprocal(c(3), c(3)))
                        link(dve.tensor_tensor(c(4), c(2), c(3), ALU.mult))
                        link(dve.tensor_scalar(c(5), c(22), -1.0, 1.0, ALU.mult, ALU.add))
                        link(dve.tensor_tensor(c(5), c(5), c(3), ALU.mult))
                        link(dve.tensor_tensor(c(5), c(5), c(17), ALU.mult))
                        for j in range(NT):
                            link(dve.tensor_scalar(AT[:, j, :], AT[:, j, :], C[:, 5, j:j + 1], None, ALU.mult))
                            link(dve.scalar_tensor_tensor(out[:, j, :], src(j), C[:, 4, j:j + 1], AT[:, j, :],
                                                          ALU.mult, ALU.add))

                    mobius(0, x_in, 2, X1)
                    norm(1, x_mid, 4, 3)
                    for j in range(NT):
                        dve.wait_ge(h_mm, i * NT + j + 1)
                        for n in range(2):
                            dve.scalar_tensor_tensor(HB[:, j, n * 512:n * 512 + 512], bank(2 * (j % 2) + n),
                                                     C[:, 19, j:j + 1], bias_f1[:, n * 512:n * 512 + 512],
                                                     ALU.mult, ALU.add).then_inc(h_out, 1)
                    dve.wait_ge(h_ss, i * NT + NT)
                    clamp(7, 8, 19)
                    for j in range(NT):
                        dve.wait_ge(ff_mm, i * NT + j + 1)
                        dve.scalar_tensor_tensor(AT[:, j, :], bank((6, 7, 0, 1)[j], 0, D),
                                                 C[:, 19, j:j + 1], bias_f2[:], ALU.mult, ALU.add).then_inc(attn_out, 1)
                    mobius(1, x_mid, 5, X2)
                    for j in range(NT):
                        dve.tensor_tensor(X2[:, j, :], X2[:, j, :], x_in(j), ALU.add).then_inc(x_out, 1)
                    for j in range(NT):
                        dve.wait_ge(x_turned, i * NT + j + 1)
                        dve.tensor_copy(XT[:].rearrange("p k (t b) -> p k t b", b=B)[:, :, j * P:j * P + P, bass.ds(i, 1)],
                                        bank(j % 2, 0, D).rearrange("p (k t a) -> p k t a", k=2, a=1)).then_inc(x_copied, 1)
                    assert (step[0], col[0], done[0]) == (DVE_STEPS, COLS, COLS), (step, col, done)


def gru(nc, w_x, u_h, c_v, b_v, cond_t, XT, ident_bf, w_next, next_parts, ident):
    NEXT = L2_COLS // (S // (2 * CH))
    with ExitStack() as ctx:
        def sb(name, shape, dt=F32):
            return ctx.enter_context(nc.sbuf_tensor(name, shape, dt))

        def sem(name):
            return ctx.enter_context(nc.semaphore(name))

        Wf = sb("w_x_sb", [P, 2, 3 * D])
        Wx = sb("w_x_parts", [P, 3, 2, 3 * D], BF16)
        XP = sb("x_parts", [P, 3, 2, CH * B], BF16)
        XR = sb("x_rest", [P, 2, CH * B])
        Uf = sb("u_h_sb", [P, 2, 3 * D])
        U = sb("u_parts", [P, 2, 2, 3 * D], F16)
        largest = sb("largest", [P, 3])
        row = sb("largest_row", [1, 2 * P])
        ones = sb("ones_row", [1, P])
        scales = sb("scales", [P, 4])
        Cv = sb("c_v_sb", [P, 2, 3 * D])
        cond = sb("cond_v", [P, 2, B])
        bias = sb("gru_bias", [B, 3 * D])
        V = sb("v_sum", [B, 3 * D])
        V1 = sb("v_parts", [B, 3, 3 * D], BF16)
        pick = sb("pick_batch", [B, CH, B], BF16)
        HS = sb("states", [P, 2 * CH + 1, 2 * B * 2])
        HA = sb("state_a", [P, 2 * B * 2], F16)
        HB = sb("state_b", [P, 2, B], F16)
        ZS = sb("scan_factors", [P, 2 * B * 2])
        NK = sb("scan_terms", [P, 2 * B * 2])
        RP = sb("reset_parts", [P, 2, 2, B], F16)
        RH = sb("reset_state", [P, 2, B])
        G = sb("gates", [P, 2, 2, B])
        ZH = sb("z_state", [P, 2, B])
        WN = sb("next_weights", [P, 2, NEXT // 2])
        PS = ctx.enter_context(nc.psum_tensor("gate_sums", [P, 2, 3, 512], F32))

        w_in, c_in = sem("gru_weights"), sem("gru_c")
        largest_ready, largest_mm = sem("largest_ready"), sem("largest_mm")
        prep, v_mm, v_ready = sem("gru_prep"), sem("v_mm"), sem("v_ready")
        r_mm, z_mm, n_mm = sem("r_mm"), sem("z_mm"), sem("n_mm")
        r_ready, z_ready, n_ready = sem("r_ready"), sem("z_ready"), sem("n_ready")
        ra_ready, rh_ready, rb_ready = sem("ra_ready"), sem("rh_ready"), sem("rb_ready")
        zh_ready, zs_ready, keep_ready = sem("zh_ready"), sem("zs_ready"), sem("keep_ready")
        ha_ready, h_ready, hb_ready = sem("ha_ready"), sem("h_ready"), sem("hb_ready")
        x_added, x_split = sem("x_added"), sem("x_split")
        next_in, next_split = [sem("next_in_0"), sem("next_in_1")], sem("next_split")
        N = 2 * CH
        SUMS, SMALL, LARGE = 2.0 ** 6, 2.0 ** 3, 2.0 ** 14
        EXPONENT = 0x7F800000

        def pairs(ap, n):
            return ap.rearrange("p (k b n) -> p k b n", b=B, n=2)[:, :, :, n]

        def gate(half, g):
            return PS[:, half, g, 0:CH * 2 * B].rearrange("p (t m b) -> p t m b", m=2, b=B)

        with nc.Block() as block:
            @block.sync
            def _(sp):
                sp.dma_start(Cv[:], c_v.rearrange("(k p) n -> p k n", p=P)).then_inc(c_in, 16)
                sp.dma_start(cond[:], cond_t.rearrange("(k p) b -> p k b", p=P)).then_inc(c_in, 16)
                sp.dma_start(bias[:], b_v.rearrange("(a n) -> a n", a=1).broadcast_to([B, 3 * D])).then_inc(c_in, 16)
                sp.dma_start(Wf[:], w_x.rearrange("(k p) n -> p k n", p=P)).then_inc(w_in, 16)
                sp.dma_start(Uf[:], u_h.rearrange("(k p) n -> p k n", p=P)).then_inc(w_in, 16)
                for half in range(2):
                    sp.dma_start(WN[:, half, :], w_next[:, half * NEXT // 2:(half + 1) * NEXT // 2]).then_inc(next_in[half], 16)
                with sp.Fori(0, S // N - 1) as i:
                    for half in range(2):
                        sp.wait_ge(next_split, i * 8 + half * 4 + 4)
                        sp.dma_start(WN[:, half, :], w_next[:, bass.ds(i * NEXT + NEXT + half * NEXT // 2, NEXT // 2)]
                                     ).then_inc(next_in[half], 16)

            @block.tensor
            def _(pe):
                pe.wait_ge(c_in, 48)
                for n, (a, z) in enumerate(((0, 512), (512, 768))):
                    for k in range(2):
                        mm = pe.matmul(PS[0:B, 0, n, 0:z - a], cond[:, k, :], Cv[:, k, a:z], start=(k == 0), stop=(k == 1))
                mm.then_inc(v_mm, 1)
                pe.wait_ge(largest_ready, 1)
                pe.transpose(PS[0:1, 0, 2, 0:P], largest[:, 2:3], ident[:]).then_inc(largest_mm, 1)
                pe.wait_ge(largest_ready, 2)
                pe.matmul(PS[:, 1, 0, 0:1], ones[:], row[:, P:P + 1], start=True, stop=True).then_inc(largest_mm, 1)
                pe.wait_ge(v_ready, 6)
                pe.wait_ge(w_in, 32)

                def project(half, pieces):
                    for g, m in pieces:
                        w = slice(g * D + m * P, g * D + m * P + P)
                        out = gate(half, g)[:, :, m, :]
                        for k in range(2):
                            for wp, xp in ((0, 0), (0, 1), (1, 0), (1, 1), (0, 2), (2, 0)):
                                pe.matmul(out, Wx[:, wp, k, w], XP[:, xp, k, :].rearrange("p (t b) -> p t b", b=B),
                                          start=(m == 0 and k == 0 and wp + xp == 0), stop=False, skip_group_check=True)
                        for part in range(3):
                            pe.matmul(out, V1[:, part, w], pick[:], start=False, stop=True, skip_group_check=True)

                PIECES = [(g, m) for g in (1, 0, 2) for m in range(2)]
                pe.wait_ge(x_split, 4)
                project(0, PIECES)

                def state_parts(part, k):
                    return HB[:, k, :] if part else pairs(HA[:], 1)[:, k, :]

                def reset_parts(part, k):
                    return RP[:, part, k, :]

                def state_share(out, g, parts, first, second):
                    for (ready, value), part, pieces in ((first, 0, 2), (second, 1, 1)):
                        pe.wait_ge(ready, value)
                        for m in range(2):
                            w = slice(g * D + m * P, g * D + m * P + P)
                            for k in range(2):
                                for u in range(pieces):
                                    mm = pe.matmul(out[:, m, :], U[:, u, k, w], parts(part, k),
                                                   start=False, stop=(part == 1), skip_group_check=True)
                    return mm

                with pe.Fori(0, S // N) as i:
                    for s in range(N):
                        half, t = s // CH, s % CH
                        a, b = (ha_ready, i * N + s + 1), (hb_ready, i * N + s + 1)
                        state_share(gate(half, 1)[:, t, :, :], 1, state_parts, a, b).then_inc(r_mm, 1)
                        state_share(gate(half, 0)[:, t, :, :], 0, state_parts, a, b).then_inc(z_mm, 1)
                        state_share(gate(half, 2)[:, t, :, :], 2, reset_parts, (ra_ready, i * N + s + 1),
                                    (rb_ready, i * N + s + 1)).then_inc(n_mm, 1)
                        if t == 4:
                            pe.wait_ge(x_split, i * 8 + half * 4 + 8)
                        if t >= 4 and t % 2 == 0:
                            project(1 - half, [PIECES[t // 2 - 2]])

            @block.scalar
            def _(act):
                act.preload_act_table_set("sigmoid_and_others")
                with act.Fori(0, S // N) as i:
                    for s in range(N):
                        half, t = s // CH, s % CH
                        act.wait_ge(r_mm, i * N + s + 1)
                        act.activation(G[:, 1, :, :], gate(half, 1)[:, t, :, :], ACT.Sigmoid, scale=1.0 / SUMS).then_inc(r_ready, 1)
                        act.wait_ge(z_mm, i * N + s + 1)
                        act.activation(G[:, 0, :, :], gate(half, 0)[:, t, :, :], ACT.Sigmoid, scale=1.0 / SUMS).then_inc(z_ready, 1)
                        act.wait_ge(n_mm, i * N + s + 1)
                        act.activation(pairs(NK[:], 0), gate(half, 2)[:, t, :, :], ACT.Tanh, scale=1.0 / SUMS).then_inc(n_ready, 1)

            @block.vector
            def _(dve):
                dve.memset(HS[:, 0, :], 0.0).then_inc(h_ready, 1)
                dve.memset(HA[:], 0.0).then_inc(ha_ready, 1)
                dve.memset(ZS[:], 0.0).then_inc(prep, 1)
                dve.memset(HB[:], 0.0).then_inc(hb_ready, 1)
                dve.tensor_copy(pick[:], ident_bf[0:B, 0:B].unsqueeze(1).broadcast_to([B, CH, B])).then_inc(v_ready, 1)
                dve.wait_ge(w_in, 32)
                count = [1]

                def link(ins):
                    count[0] += 1
                    ins.then_inc(prep, 1)
                    dve.wait_ge(prep, count[0])

                dve.tensor_reduce(largest[:, 0:1], Uf[:].rearrange("p k n -> p (k n)"), AX.X, ALU.max)
                link(dve.tensor_reduce(largest[:, 1:2], Uf[:].rearrange("p k n -> p (k n)"), AX.X, ALU.min))
                link(dve.tensor_scalar(largest[:, 1:2], largest[:, 1:2], -1.0, None, ALU.mult))
                dve.tensor_tensor(largest[:, 2:3], largest[:, 0:1], largest[:, 1:2], ALU.max).then_inc(largest_ready, 1)
                link(dve.memset(ones[:], 1.0))
                dve.wait_ge(largest_mm, 1)
                link(dve.tensor_reduce(row[:, P:P + 1], PS[0:1, 0, 2, 0:P], AX.X, ALU.max))
                dve.tensor_scalar(row[:, P:P + 1], row[:, P:P + 1], 2.0 ** -6, 2.0 ** 23, ALU.max, ALU.min
                                  ).then_inc(largest_ready, 1)
                dve.wait_ge(largest_mm, 2)
                power, factor_u, factor_h, undo = (scales[:, n:n + 1] for n in range(4))
                link(dve.tensor_copy(power, PS[:, 1, 0, 0:1]))
                link(dve.tensor_scalar(power.bitcast(I32), power.bitcast(I32), EXPONENT, None, ALU.bitwise_and))
                link(dve.reciprocal(factor_u, power))
                link(dve.tensor_scalar(factor_u, factor_u, 1.0 + 2.0 ** -10, None, ALU.mult))
                link(dve.tensor_scalar(factor_u.bitcast(I32), factor_u.bitcast(I32), EXPONENT, None, ALU.bitwise_and))
                link(dve.tensor_scalar(factor_u, factor_u, LARGE, SMALL, ALU.mult, ALU.min))
                link(dve.tensor_scalar(factor_h, power, 1.0 / LARGE, 1.0 / SMALL, ALU.mult, ALU.max))
                link(dve.tensor_scalar(factor_h, factor_h, SUMS, None, ALU.mult))
                link(dve.tensor_scalar(undo, factor_u, 1.0 / SUMS, None, ALU.mult))
                link(dve.tensor_scalar(Uf[:], Uf[:], factor_u, None, ALU.mult))
                link(dve.tensor_copy(U[:, 0, :, :], Uf[:]))
                dve.tensor_tensor(U[:, 1, :, :], Uf[:], U[:, 0, :, :], ALU.subtract).then_inc(v_ready, 1)
                dve.wait_ge(v_mm, 1)
                dve.tensor_tensor(V[:, 0:512], PS[0:B, 0, 0, :], bias[:, 0:512], ALU.add)
                link(dve.tensor_tensor(V[:, 512:768], PS[0:B, 0, 1, 0:256], bias[:, 512:768], ALU.add))
                link(dve.tensor_scalar(V[:], V[:], SUMS, None, ALU.mult))
                dve.tensor_copy(V1[:, 0, :], V[:]).then_inc(v_ready, 1)
                dve.wait_ge(v_ready, 3)
                link(dve.tensor_tensor(V[:], V[:], V1[:, 0, :], ALU.subtract))
                dve.tensor_copy(V1[:, 1, :], V[:]).then_inc(v_ready, 1)
                dve.wait_ge(v_ready, 4)
                dve.tensor_tensor(V1[:, 2, :], V[:], V1[:, 1, :], ALU.subtract).then_inc(v_ready, 1)

                link(dve.tensor_scalar(Wf[:], Wf[:], SUMS, None, ALU.mult))
                link(dve.tensor_copy(Wx[:, 0, :, :], Wf[:]))
                link(dve.tensor_tensor(Wf[:], Wf[:], Wx[:, 0, :, :], ALU.subtract))
                link(dve.tensor_copy(Wx[:, 1, :, :], Wf[:]))
                dve.tensor_tensor(Wx[:, 2, :, :], Wf[:], Wx[:, 1, :, :], ALU.subtract).then_inc(v_ready, 1)

                def split_x(n, at, done):
                    xs = XT[:, :, bass.ds(at, CH * B)]
                    if n:
                        dve.wait_ge(x_split, done + n)
                    if n == 0:
                        ins = dve.tensor_copy(XP[:, 0, :, :], xs)
                    elif n == 1:
                        ins = dve.tensor_tensor(XR[:], xs, XP[:, 0, :, :], ALU.subtract)
                    elif n == 2:
                        ins = dve.tensor_copy(XP[:, 1, :, :], XR[:])
                    else:
                        ins = dve.tensor_tensor(XP[:, 2, :, :], XR[:], XP[:, 1, :, :], ALU.subtract)
                    ins.then_inc(x_split, 1)

                for n in range(4):
                    split_x(n, 0, 0)

                def split_next(n):
                    half, piece, low = n // 4, n // 2 % 2, n % 2
                    a = piece * NEXT // 4
                    src = WN[:, half, a:a + NEXT // 4]
                    high, rest = (w[:, bass.ds(i * NEXT + half * NEXT // 2 + a, NEXT // 4)] for w in next_parts)
                    if low:
                        dve.wait_ge(next_split, i * 8 + n)
                        dve.tensor_tensor(rest, src, high.bitcast(F32), ALU.subtract).then_inc(next_split, 1)
                    else:
                        if piece == 0:
                            dve.wait_ge(next_in[half], i * 16 + 16)
                        dve.tensor_copy(high, src).then_inc(next_split, 1)

                with dve.Fori(0, S // N) as i:
                    for s in range(N):
                        at = i * N + s + 1
                        old, new = pairs(HS[:, s, :], 1), HS[:, s + 1, :]
                        if s == 0:
                            dve.wait_ge(h_ready, at)
                        dve.wait_ge(r_ready, at)
                        dve.tensor_tensor(RP[:, 0, :, :], G[:, 1, :, :], old, ALU.mult).then_inc(ra_ready, 1)
                        dve.tensor_tensor(RH[:], G[:, 1, :, :], old, ALU.mult).then_inc(rh_ready, 1)
                        dve.wait_ge(ra_ready, at)
                        dve.wait_ge(rh_ready, at)
                        dve.tensor_tensor(RP[:, 1, :, :], RH[:], RP[:, 0, :, :], ALU.subtract).then_inc(rb_ready, 1)
                        dve.wait_ge(z_ready, at)
                        dve.tensor_tensor(ZH[:], G[:, 0, :, :], old, ALU.mult).then_inc(zh_ready, 1)
                        dve.tensor_scalar(pairs(ZS[:], 1), G[:, 0, :, :], factor_h, None, ALU.mult).then_inc(zs_ready, 1)
                        dve.wait_ge(zh_ready, at)
                        dve.tensor_tensor(pairs(NK[:], 1), old, ZH[:], ALU.subtract).then_inc(keep_ready, 1)
                        dve.wait_ge(keep_ready, at)
                        dve.wait_ge(zs_ready, at)
                        dve.wait_ge(n_ready, at)
                        dve.tensor_tensor_scan(HA[:], ZS[:], NK[:], 0.0, ALU.mult, ALU.add).then_inc(ha_ready, 1)
                        dve.tensor_tensor_scan(new, ZS[:], NK[:], 0.0, ALU.mult, ALU.add).then_inc(h_ready, 1)
                        dve.wait_ge(ha_ready, at + 1)
                        dve.wait_ge(h_ready, at + 1)
                        dve.tensor_tensor(HB[:], pairs(new, 1), pairs(HA[:], 1), ALU.subtract).then_inc(hb_ready, 1)
                        if s % CH < 4:
                            split_x(s % CH, (i * N + (s // CH + 1) * CH) * B, i * 8 + s // CH * 4 + 4)
                        elif s % CH % 2 == 0 and s % CH < 12:
                            split_next(s // CH * 4 + (s % CH - 4) // 2)
                    dve.tensor_copy(HS[:, 0, :], HS[:, N, :]).then_inc(x_added, 1)
                    xs = XT[:, :, bass.ds(i * N * B, N * B)]
                    for k in range(2):
                        states = HS[:, 1:N + 1, :].rearrange("p t (k b n) -> p k t b n", b=B, n=2)[:, k, :, :, 1]
                        dve.scalar_tensor_tensor(xs[:, k, :].rearrange("p (t b) -> p t b", b=B), states, undo,
                                                 xs[:, k, :].rearrange("p (t b) -> p t b", b=B),
                                                 ALU.mult, ALU.add).then_inc(x_added, 1)
                    dve.wait_ge(x_added, i * 3 + 3)
                dve.wait_ge(next_split, S // N * 8)


def top_two(dve, link, scores, picked, t, m, rank, shape):
    def over(v):
        return v.unsqueeze(len(shape) - 1).broadcast_to(shape)

    one = t[1]
    for n in range(2):
        link(dve.tensor_reduce(m, scores, AX.X, ALU.max))
        link(dve.tensor_tensor(t[0], scores, over(m), ALU.is_equal))
        link(dve.tensor_tensor(t[0], t[0], rank, ALU.mult))
        link(dve.tensor_reduce(m, t[0], AX.X, ALU.max))
        link(dve.tensor_tensor(one, t[0], over(m), ALU.is_equal))
        if n == 0:
            link(dve.tensor_copy(picked, one))
            link(dve.scalar_tensor_tensor(scores, one, -1e30, scores, ALU.mult, ALU.add))
        else:
            link(dve.tensor_tensor(picked, picked, one, ALU.add))


def shared_and_routed(nc, w_router, router_bias, W, cond_t, XT, ident):
    NS, NE, HS_T, HR_T = N_SHARED, N_ROUTED, HID_S // P, HID_R // P
    SW1, SW3, SW2, RW1, RW2 = ([parts_of(w, n) for w in W] for n in range(5))
    T = XT_COLS // P
    with ExitStack() as ctx:
        def sb(name, shape, dt=F32):
            return ctx.enter_context(nc.sbuf_tensor(name, shape, dt))

        def sem(name):
            return ctx.enter_context(nc.semaphore(name))

        XP = [sb(f"x_part_{n}", [P, 2, XT_COLS], F32R) for n in range(2)]
        WR = sb("w_router_sb", [P, 4, NE])
        cond = sb("cond_r", [P, 2, B])
        cond_rep = sb("cond_cols", [P, 2, P])
        bias = sb("router_bias_sb", [P, NE])
        rank = sb("rank", [P, NE])
        SIG = sb("router_scores", [P, T, NE])
        SEL = sb("selection", [P, T, NE])
        BOTH = sb("picked_two", [P, T, NE])
        T0 = sb("router_t0", [P, T, NE])
        T1 = sb("router_t1", [P, T, NE])
        M = sb("router_m", [P, 3, T])
        CL = sb("cond_logits", [P, NE])
        GT = sb("gates_t", [NE, XT_COLS])
        pick = sb("pick_expert", [NE, NE, P])
        A1 = sb("activated", [P, 2, 512])
        HB = sb("hidden_2", [P, 2, 512])
        HP = [sb(f"hidden_part_{n}", [P, 3, 512], F32R) for n in range(2)]
        PS = ctx.enter_context(nc.psum_tensor("ps2", [P, 8, 512], F32))
        OUT, PAIR, GATE = 0, 2, 6

        r_in, x_split, h_full, h_high = sem("router_in"), sem("x_split_2"), sem("h_full"), sem("h_high")
        step, rows_ready, logit_mm, scored = sem("router_step"), sem("rows_ready"), sem("logit_mm"), sem("scored")
        gates_ready, gates_turned, gates_copied = sem("gates_ready"), sem("gates_turned"), sem("gates_copied")
        first_mm, gate_mm, activated, h_ready, second_mm, added = (
            sem("first_mm"), sem("gate_mm"), sem("activated"), sem("hidden_ready"), sem("second_mm"), sem("added"))

        units = [("s", e, m) for e in range(NS) for m in range(HS_T)] + [("r", e, m) for e in range(NE) for m in range(HR_T)]
        NU = len(units)

        with nc.Block() as block:
            @block.sync
            def _(sp):
                sp.dma_start(WR[:], w_router.rearrange("(k p) n -> p k n", p=P)).then_inc(r_in, 16)
                sp.dma_start(cond[:], cond_t.rearrange("(k p) b -> p k b", p=P)).then_inc(r_in, 16)
                sp.dma_start(bias[:], router_bias.rearrange("(a n) -> a n", a=1).broadcast_to([P, NE])).then_inc(r_in, 16)

            @block.tensor
            def _(pe):
                pe.wait_ge(r_in, 48)
                pe.wait_ge(rows_ready, 1)
                for k in range(2):
                    pe.matmul(PS[:, 1, 0:NE], cond_rep[:, k, :], WR[:, 2 + k, :], start=(k == 0), stop=(k == 1))
                for t in range(T):
                    for k in range(2):
                        mm = pe.matmul(PS[:, 0, t * NE:t * NE + NE], XT[:, k, t * P:t * P + P], WR[:, k, :],
                                       start=(k == 0), stop=(k == 1), skip_group_check=True)
                mm.then_inc(logit_mm, 1)
                pe.wait_ge(gates_ready, 1)
                for t in range(T):
                    mm = pe.transpose(PS[0:NE, 2 + t // 4, t % 4 * P:t % 4 * P + P], BOTH[:, t, :], ident[:])
                mm.then_inc(gates_turned, 1)
                pe.wait_ge(gates_copied, 1)
                pe.wait_ge(x_split, 2)
                with pe.Fori(0, XT_COLS // 512) as i:
                    def second(u):
                        kind, e, m = units[u]
                        w = SW2 if kind == "s" else RW2
                        pe.wait_ge(h_ready, i * NU + u + 1)
                        for f in range(2):
                            for wp, hp in PRODUCTS:
                                mm = pe.matmul(PS[:, OUT + f, :], w[wp][:, e, m, f * P:f * P + P], HP[hp][:, u % 3, :],
                                               start=(u == 0 and wp + hp == 0), stop=(u == NU - 1), skip_group_check=True)
                        mm.then_inc(second_mm, 1)

                    for u, (kind, e, m) in enumerate(units):
                        if u >= 2:
                            pe.wait_ge(h_full, i * NU + u - 1)
                        pair = PAIR + 2 * (u % 2)
                        for n, w in enumerate((SW1, SW3) if kind == "s" else (RW1,)):
                            for k in range(2):
                                for wp, xp in PRODUCTS:
                                    mm = pe.matmul(PS[:, pair + n, :], w[wp][:, e, k, m * P:m * P + P],
                                                   XP[xp][:, k, bass.ds(i * 512, 512)], start=(k == 0 and wp + xp == 0),
                                                   stop=(k == 1), skip_group_check=True)
                        mm.then_inc(first_mm, 1)
                        if kind == "r" and m == 0:
                            pe.matmul(PS[:, GATE + e % 2, :], pick[:, e, :], GT[:, bass.ds(i * 512, 512)],
                                      start=True, stop=True).then_inc(gate_mm, 1)
                        if u == 1:
                            pe.wait_ge(added, 2 * i + 1)
                        if u:
                            second(u - 1)
                    second(NU - 1)

            @block.scalar
            def _(act):
                act.wait_ge(logit_mm, 1)
                act.wait_ge(rows_ready, 2)
                act.activation(SIG[:], SEL[:], ACT.Sigmoid).then_inc(scored, 1)
                with act.Fori(0, XT_COLS // 512) as i:
                    for u, (kind, e, m) in enumerate(units):
                        act.wait_ge(first_mm, i * NU + u + 1)
                        if u >= 2:
                            act.wait_ge(h_full, i * NU + u - 1)
                        act.activation(A1[:, u % 2, :], PS[:, PAIR + 2 * (u % 2), :],
                                       ACT.Silu if kind == "s" else ACT.Gelu).then_inc(activated, 1)

            @block.vector
            def _(dve):
                count = [0]

                def link(ins):
                    count[0] += 1
                    ins.then_inc(step, 1)
                    dve.wait_ge(step, count[0])

                for e in range(NE):
                    dve.memset(rank[:, e:e + 1], float(NE - e))
                link(dve.tensor_copy(pick[:], ident[0:NE, 0:NE].unsqueeze(2).broadcast_to([NE, NE, P])))
                dve.wait_ge(r_in, 48)
                dve.tensor_copy(cond_rep[:].rearrange("p k (t b) -> p k t b", b=B),
                                cond[:].unsqueeze(2).broadcast_to([P, 2, P // B, B])).then_inc(rows_ready, 1)
                dve.wait_ge(logit_mm, 1)
                link(dve.tensor_copy(CL[:], PS[:, 1, 0:NE]))
                dve.tensor_tensor(SEL[:], PS[:, 0, 0:T * NE].rearrange("p (t e) -> p t e", e=NE),
                                  CL[:].unsqueeze(1).broadcast_to([P, T, NE]), ALU.add).then_inc(rows_ready, 1)
                dve.wait_ge(scored, 1)
                link(dve.tensor_tensor(SEL[:], SIG[:], bias[:].unsqueeze(1).broadcast_to([P, T, NE]), ALU.add))
                top_two(dve, link, SEL[:], BOTH[:], (T0[:], T1[:]), M[:, 0, :],
                        rank[:].unsqueeze(1).broadcast_to([P, T, NE]), [P, T, NE])
                link(dve.tensor_tensor(SIG[:], SIG[:], BOTH[:], ALU.mult))
                link(dve.tensor_reduce(M[:, 0, :], SIG[:], AX.X, ALU.add))
                link(dve.tensor_scalar(M[:, 1, :], M[:, 0, :], 1e-9, None, ALU.is_gt))
                link(dve.tensor_scalar(M[:, 0, :], M[:, 0, :], 1e-9, None, ALU.add))
                link(dve.reciprocal(M[:, 2, :], M[:, 0, :]))
                link(dve.tensor_tensor(M[:, 2, :], M[:, 2, :], M[:, 1, :], ALU.mult))
                link(dve.tensor_scalar(M[:, 1, :], M[:, 1, :], -0.5, 0.5, ALU.mult, ALU.add))
                link(dve.tensor_tensor(SIG[:], SIG[:], M[:, 2, :].unsqueeze(2).broadcast_to([P, T, NE]), ALU.mult))
                link(dve.tensor_tensor(BOTH[:], BOTH[:], M[:, 1, :].unsqueeze(2).broadcast_to([P, T, NE]), ALU.mult))
                dve.tensor_tensor(BOTH[:], BOTH[:], SIG[:], ALU.add).then_inc(gates_ready, 1)
                dve.sem_inc(added, 1)
                dve.wait_ge(gates_turned, 1)
                dve.tensor_copy(GT[:], PS[0:NE, 2:6, :].rearrange("p a b -> p (a b)")).then_inc(gates_copied, 1)
                dve.tensor_copy(XP[0][:], XT[:, :, 0:XT_COLS]).then_inc(x_split, 1)
                dve.wait_ge(x_split, 1)
                dve.tensor_tensor(XP[1][:], XT[:, :, 0:XT_COLS], XP[0][:].bitcast(F32), ALU.subtract).then_inc(x_split, 1)
                with dve.Fori(0, XT_COLS // 512) as i:
                    for u, (kind, e, m) in enumerate(units):
                        dve.wait_ge(activated, i * NU + u + 1)
                        if kind == "s":
                            dve.scalar_tensor_tensor(HB[:, u % 2, :], PS[:, PAIR + 2 * (u % 2) + 1, :], 1.0 / NS,
                                                     A1[:, u % 2, :], ALU.mult, ALU.mult).then_inc(h_full, 1)
                        else:
                            dve.wait_ge(gate_mm, i * NE + e + 1)
                            dve.tensor_tensor(HB[:, u % 2, :], PS[:, GATE + e % 2, :], A1[:, u % 2, :],
                                              ALU.mult).then_inc(h_full, 1)
                        if u >= 3:
                            dve.wait_ge(second_mm, i * NU + u - 2)
                        dve.wait_ge(h_full, i * NU + u + 1)
                        dve.tensor_copy(HP[0][:, u % 3, :], HB[:, u % 2, :]).then_inc(h_high, 1)
                        dve.wait_ge(h_high, i * NU + u + 1)
                        dve.tensor_tensor(HP[1][:, u % 3, :], HB[:, u % 2, :], HP[0][:, u % 3, :].bitcast(F32),
                                          ALU.subtract).then_inc(h_ready, 1)
                    dve.wait_ge(second_mm, (i + 1) * NU)
                    for f in range(2):
                        xs = XT[:, f, bass.ds(i * 512, 512)]
                        dve.scalar_tensor_tensor(xs, PS[:, OUT + f, :], 1.0 / (NS + TOP_K), xs,
                                                 ALU.mult, ALU.add).then_inc(added, 1)
                dve.wait_ge(added, 2 * (XT_COLS // 512) + 1)


def gated_experts(nc, gate_w, gate_b, time_w, time_b, ew1, ew2, sw1, sw2, b1, b2, cond_t, XT, ident, out):
    NE = ew1.shape[0]
    HT = FF // P
    L1_3 = S // 3
    with ExitStack() as ctx:
        def sb(name, shape, dt=F32):
            return ctx.enter_context(nc.sbuf_tensor(name, shape, dt))

        def sem(name):
            return ctx.enter_context(nc.semaphore(name))

        WN = 2 * FF + HT * D
        RAW = sb("e_weights_sb", [P, 2, WN])
        WP = [sb(f"e_weights_{n}", [P, 2, WN], F32R) for n in ("high", "low")]
        XP = [sb(f"x_part3_{n}", [P, 2, XT_COLS], F32R) for n in ("high", "low")]
        B1 = sb("e_b1", [P, NE + 1, HT])
        B2 = sb("e_b2", [P, NE + 1, 2])
        GW = sb("gate_w_sb", [P, 6, NE])
        TW = sb("time_w_sb", [P, 2, 2 * NE])
        GB = sb("gate_b_sb", [B, NE])
        TB = sb("time_b_sb", [B, 2 * NE])
        cond = sb("cond_g", [P, 2, B])
        SC = sb("silu_cond", [P, 2, B])
        SM = sb("range_sums", [P, 3, 2, B])
        GI = sb("gate_in", [P, 3, 2, B])
        LG = sb("gate_logits", [B, NE])
        MOD = sb("modulation", [B, 2 * NE])
        rank = sb("rank3", [B, NE])
        T0 = sb("g_t0", [B, NE])
        T1 = sb("g_t1", [B, NE])
        BOTH = sb("g_picked", [B, NE])
        WS = sb("g_spoiled", [B, NE])
        M = sb("g_m", [B, 4])
        BD = sb("block_diag", [B, B, NE])
        ones = sb("ones", [B, P])
        WB = sb("weights_all", [P, B, NE])
        A1 = sb("activated3", [P, 4, 512])
        HP = [sb(f"hidden3_{n}", [P, 4, 512], F32R) for n in ("high", "low")]
        Y = sb("weighted_out", [P, 2, 512])
        PS = ctx.enter_context(nc.psum_tensor("ps3", [P, 8, 512], F32))

        w_in = [sem("e_weights_0"), sem("e_weights_1")]
        b_in, g_in, silu_done = sem("e_biases"), sem("g_in"), sem("silu_done")
        step, gate_in, gate_mm, ready, exped, diag, spread = (
            sem("g_step"), sem("gate_in_s"), sem("gate_mm3"), sem("logits_ready"), sem("exped"), sem("diag"), sem("spread"))
        x_split, w_split = sem("x_split3"), sem("w_split3")
        first_mm, activated, h_ready, second_mm, weighted, summed, stored = (
            sem("first_mm3"), sem("activated_s"), sem("hidden_ready3"), sem("second_mm3"), sem("weighted"),
            sem("summed"), sem("stored"))

        bounds = (0, L1_3, 2 * L1_3, S)
        order = (NE,) + tuple(range(NE))
        thirds = {e: (0, 1, 2) for e in order}
        thirds[1], thirds[2] = (0, 2), (1, 2)
        chunks_before = [2 * sum(len(thirds[e]) for e in order[:n]) for n in range(NE + 2)]
        SPLITS = 16
        PIECE = WN // 2 // (SPLITS // 2)
        OUT, FIRST = 0, 4

        def cols(third, i):
            n = (bounds[third + 1] - bounds[third]) * B // 2
            return bass.ds(i * n + bounds[third] * B, n), n

        def w1(part, n, k, m):
            at = k * FF + m * P
            return WP[part][:, n % 2, at:at + P]

        def w2(part, n, m, f):
            at = 2 * FF + m * D + f * P
            return WP[part][:, n % 2, at:at + P]

        with nc.Block() as block:
            @block.sync
            def _(sp):
                sp.dma_start(GW[:], gate_w.rearrange("(k p) n -> p k n", p=P)).then_inc(g_in, 16)
                sp.dma_start(TW[:], time_w.rearrange("(k p) n -> p k n", p=P)).then_inc(g_in, 16)
                sp.dma_start(cond[:], cond_t.rearrange("(k p) b -> p k b", p=P)).then_inc(g_in, 16)
                sp.dma_start(GB[:], gate_b.rearrange("(a n) -> a n", a=1).broadcast_to([B, NE])).then_inc(g_in, 16)
                sp.dma_start(TB[:], time_b.rearrange("(a n) -> a n", a=1).broadcast_to([B, 2 * NE])).then_inc(g_in, 16)
                sp.dma_start(B1[:], b1).then_inc(b_in, 16)
                sp.dma_start(B2[:], b2).then_inc(b_in, 16)
                for n, e in enumerate(order):
                    if n >= 2:
                        sp.wait_ge(w_split, (n - 1) * 2 * SPLITS)
                    first, second = (ew1[e], ew2[e]) if e < NE else (sw1, sw2)
                    for src, a, z in ((first, 0, 2 * FF), (second, 2 * FF, WN)):
                        rows = src.rearrange("(k p) n -> p k n", p=P)
                        sp.dma_start(RAW[:, n % 2, a:z].rearrange("p (k n) -> p k n", k=rows.shape[1]), rows
                                     ).then_inc(w_in[n % 2], 16)
                with sp.Fori(0, 2) as i:
                    for q, third in enumerate(thirds[order[NE]]):
                        sp.wait_ge(summed, i * 2 * 3 + 2 * (chunks_before[NE] + q + 1) + 1)
                        at, _n = cols(third, i)
                        sp.dma_start(out.rearrange("(k p) n -> p k n", p=P)[:, :, at], XT[:, :, at]).then_inc(stored, 16)
                sp.wait_ge(stored, 16 * 6)

            @block.tensor
            def _(pe):
                pe.wait_ge(g_in, 80)
                pe.wait_ge(silu_done, 1)
                for k in range(2):
                    pe.matmul(PS[0:B, 0, 0:2 * NE], SC[:, k, :], TW[:, k, :], start=(k == 0), stop=(k == 1))
                pe.wait_ge(gate_in, 1)
                for k in range(6):
                    mm = pe.matmul(PS[0:B, 1, 0:NE], GI[:, k // 2, k % 2, :], GW[:, k, :], start=(k == 0), stop=(k == 5))
                mm.then_inc(gate_mm, 1)
                pe.wait_ge(diag, 1)
                pe.matmul(PS[:, 2, 0:B * NE], ones[:], BD[:].rearrange("p b e -> p (b e)"),
                          start=True, stop=True).then_inc(spread, 1)
                pe.wait_ge(x_split, 2)
                for n, e in enumerate(order):
                    units = [(q, third, m) for q, third in enumerate(thirds[e]) for m in range(HT)]
                    NU, NQ, CB = len(units), len(thirds[e]), chunks_before[n]
                    pe.wait_ge(w_split, (n + 1) * 2 * SPLITS)
                    with pe.Fori(0, 2) as i:
                        def second(u):
                            q, third, m = units[u]
                            _at, width = cols(third, i)
                            if m == 0:
                                pe.wait_ge(summed, i * 2 * NQ + 2 * (CB + max(q - 1, 0)) + 1)
                            pe.wait_ge(h_ready, i * NU + CB * HT + u + 1)
                            for f in range(2):
                                for wp, hp in PRODUCTS:
                                    mm = pe.matmul(PS[:, OUT + 2 * (q % 2) + f, 0:width], w2(wp, n, m, f), HP[hp][:, u % 4, 0:width],
                                                   start=(m == 0 and wp + hp == 0), stop=(m == HT - 1), skip_group_check=True)
                            mm.then_inc(second_mm, 1)

                        for u, (q, third, m) in enumerate(units):
                            at, width = cols(third, i)
                            if u >= 4:
                                pe.wait_ge(activated, i * NU + CB * HT + u - 3)
                            for k in range(2):
                                for wp, xp in PRODUCTS:
                                    mm = pe.matmul(PS[:, FIRST + u % 4, 0:width], w1(wp, n, k, m), XP[xp][:, k, at],
                                                   start=(k == 0 and wp + xp == 0), stop=(k == 1), skip_group_check=True)
                            mm.then_inc(first_mm, 1)
                            if u >= 2:
                                second(u - 2)
                        second(NU - 2)
                        second(NU - 1)

            @block.scalar
            def _(act):
                act.wait_ge(g_in, 80)
                act.activation(SC[:], cond[:], ACT.Silu).then_inc(silu_done, 1)
                act.wait_ge(ready, 1)
                act.activation(LG[:], LG[:], ACT.Exp, bias=M[:, 1:2], accum_out=M[:, 2:3]).then_inc(exped, 1)
                act.wait_ge(b_in, 32)
                for n, e in enumerate(order):
                    units = [(q, third, m) for q, third in enumerate(thirds[e]) for m in range(HT)]
                    NU, CB = len(units), chunks_before[n]
                    with act.Fori(0, 2) as i:
                        act.wait_ge(second_mm, i * NU + CB * HT + 1)
                        for u, (q, third, m) in enumerate(units):
                            _at, width = cols(third, i)
                            act.wait_ge(first_mm, i * NU + CB * HT + u + 1)
                            if u >= 4:
                                act.wait_ge(second_mm, i * NU + CB * HT + u - 3 + 1)
                            for dst in (HP[0], A1):
                                ins = act.activation(dst[:, u % 4, 0:width], PS[:, FIRST + u % 4, 0:width],
                                                     ACT.Gelu_apprx_tanh, bias=B1[:, e, m:m + 1])
                            ins.then_inc(activated, 1)

            @block.vector
            def _(dve):
                count = [0]

                def link(ins):
                    count[0] += 1
                    ins.then_inc(step, 1)
                    dve.wait_ge(step, count[0])

                for e in range(NE):
                    dve.memset(rank[:, e:e + 1], float(NE - e))
                dve.memset(ones[:], 1.0)
                x4 = XT[:, :, 0:XT_COLS].rearrange("p k (t b) -> p k b t", b=B)
                for r in range(3):
                    ins = dve.tensor_reduce(SM[:, r, :, :], x4[:, :, :, bounds[r]:bounds[r + 1]], AX.X, ALU.add)
                link(ins)
                both = float(S - L1_3)
                dve.tensor_tensor(GI[:, 1, :, :], SM[:, 0, :, :], SM[:, 2, :, :], ALU.add)
                dve.tensor_tensor(GI[:, 2, :, :], SM[:, 1, :, :], SM[:, 2, :, :], ALU.add)
                link(dve.tensor_tensor(GI[:, 0, :, :], SM[:, 0, :, :], SM[:, 1, :, :], ALU.add))
                link(dve.tensor_tensor(GI[:, 0, :, :], GI[:, 0, :, :], SM[:, 2, :, :], ALU.add))
                link(dve.tensor_scalar(GI[:, 0, :, :], GI[:, 0, :, :], 1.0 / S, None, ALU.mult))
                dve.tensor_scalar(GI[:, 1:3, :, :], GI[:, 1:3, :, :], 1.0 / both, None, ALU.mult).then_inc(gate_in, 1)
                dve.wait_ge(gate_mm, 1)
                dve.wait_ge(g_in, 80)
                link(dve.tensor_tensor(LG[:], PS[0:B, 1, 0:NE], GB[:], ALU.add))
                link(dve.tensor_tensor(MOD[:], PS[0:B, 0, 0:2 * NE], TB[:], ALU.add))
                link(dve.scalar_tensor_tensor(LG[:], MOD[:, 0:NE], 1.0, LG[:], ALU.add, ALU.mult))
                link(dve.tensor_tensor(LG[:], LG[:], MOD[:, NE:2 * NE], ALU.add))
                link(dve.tensor_reduce(M[:, 0:1], LG[:], AX.X, ALU.max))
                dve.tensor_scalar(M[:, 1:2], M[:, 0:1], -1.0, None, ALU.mult).then_inc(ready, 1)
                dve.wait_ge(exped, 1)
                link(dve.reciprocal(M[:, 3:4], M[:, 2:3]))
                link(dve.tensor_scalar(LG[:], LG[:], M[:, 3:4], None, ALU.mult))
                link(dve.tensor_copy(WS[:], LG[:]))
                rows = [v[:].unsqueeze(1) for v in (WS, BOTH, T0, T1, rank)]
                top_two(dve, link, rows[0], rows[1], rows[2:4], M[:, 0:1], rows[4], [B, 1, NE])
                link(dve.tensor_tensor(BOTH[:], BOTH[:], LG[:], ALU.mult))
                link(dve.tensor_reduce(M[:, 0:1], BOTH[:], AX.X, ALU.add))
                link(dve.tensor_scalar(M[:, 0:1], M[:, 0:1], 1e-8, None, ALU.add))
                link(dve.reciprocal(M[:, 3:4], M[:, 0:1]))
                link(dve.tensor_scalar(BOTH[:], BOTH[:], M[:, 3:4], None, ALU.mult))
                dve.tensor_tensor(BD[:], BOTH[:].unsqueeze(1).broadcast_to([B, B, NE]),
                                  ident[0:B, 0:B].unsqueeze(2).broadcast_to([B, B, NE]), ALU.mult).then_inc(diag, 1)
                dve.wait_ge(spread, 1)
                link(dve.tensor_copy(WB[:].rearrange("p b e -> p (b e)"), PS[:, 2, 0:B * NE]))
                dve.sem_inc(summed, 1)
                dve.sem_inc(second_mm, 1)
                dve.tensor_copy(XP[0][:], XT[:, :, 0:XT_COLS]).then_inc(x_split, 1)
                dve.wait_ge(x_split, 1)
                dve.tensor_tensor(XP[1][:], XT[:, :, 0:XT_COLS], XP[0][:].bitcast(F32), ALU.subtract).then_inc(x_split, 1)

                def split_weights(n, i, s, done):
                    at = bass.ds(i * (WN // 2) + s // 2 * PIECE, PIECE)
                    high, low = (w[:, n % 2, at] for w in WP)
                    if s == 0:
                        dve.wait_ge(w_in[n % 2], 32 * (n // 2 + 1))
                    if s % 2 == 0:
                        dve.tensor_copy(high, RAW[:, n % 2, at]).then_inc(w_split, 1)
                    else:
                        dve.wait_ge(w_split, done + s)
                        dve.tensor_tensor(low, RAW[:, n % 2, at], high.bitcast(F32), ALU.subtract).then_inc(w_split, 1)

                for i in range(2):
                    for s in range(SPLITS):
                        split_weights(0, i, s, i * SPLITS)
                dve.wait_ge(b_in, 32)
                for n, e in enumerate(order):
                    units = [(q, third, m) for q, third in enumerate(thirds[e]) for m in range(HT)]
                    NU, NQ, CB = len(units), len(thirds[e]), chunks_before[n]
                    with dve.Fori(0, 2) as i:
                        def add(q, third):
                            at, width = cols(third, i)
                            dve.wait_ge(second_mm, i * NU + CB * HT + HT * (q + 1) + 1)
                            for f in range(2):
                                o, xs = PS[:, OUT + 2 * (q % 2) + f, 0:width], XT[:, f, at]
                                if e == NE:
                                    dve.scalar_tensor_tensor(xs, o, B2[:, e, f:f + 1], xs, ALU.add, ALU.add).then_inc(summed, 1)
                                else:
                                    dve.scalar_tensor_tensor(
                                        Y[:, f, 0:width].rearrange("p (t b) -> p t b", b=B),
                                        o.rearrange("p (t b) -> p t b", b=B), B2[:, e, f:f + 1],
                                        WB[:, :, e].unsqueeze(1).broadcast_to([P, width // B, B]),
                                        ALU.add, ALU.mult).then_inc(weighted, 1)
                            if e < NE:
                                before = 2 * (CB - chunks_before[1] + q)
                                for f in range(2):
                                    xs = XT[:, f, at]
                                    dve.wait_ge(weighted, i * 2 * NQ + before + f + 1)
                                    dve.tensor_tensor(xs, xs, Y[:, f, 0:width], ALU.add).then_inc(summed, 1)

                        for u, (q, third, m) in enumerate(units):
                            _at, width = cols(third, i)
                            dve.wait_ge(activated, i * NU + CB * HT + u + 1)
                            dve.tensor_tensor(HP[1][:, u % 4, 0:width], A1[:, u % 4, 0:width],
                                              HP[0][:, u % 4, 0:width].bitcast(F32), ALU.subtract).then_inc(h_ready, 1)
                            if n < NE and u < SPLITS:
                                split_weights(n + 1, i, u, i * SPLITS + (n + 1) * 2 * SPLITS)
                            if q and m == 2:
                                add(q - 1, thirds[e][q - 1])
                        add(NQ - 1, thirds[e][NQ - 1])


def layers(nc, x, cond_t, l0, l1, l2, l3, eye, out):
    with ExitStack() as ctx:
        XT = ctx.enter_context(nc.sbuf_tensor("xt", [P, 2, XT_COLS + CH * B], F32))
        ident = ctx.enter_context(nc.sbuf_tensor("ident", [P, P], F32))
        ident_bf = ctx.enter_context(nc.sbuf_tensor("ident_bf", [P, P], BF16))
        eye_in, ident_ready = ctx.enter_context(nc.semaphore("eye_in")), ctx.enter_context(nc.semaphore("ident_ready"))
        with nc.Block() as block:
            @block.sync
            def _(sp):
                sp.dma_start(ident[:], eye).then_inc(eye_in, 16)

            @block.vector
            def _(dve):
                dve.memset(XT[:, :, XT_COLS:], 0.0)
                dve.wait_ge(eye_in, 16)
                dve.tensor_copy(ident_bf[:], ident[:]).then_inc(ident_ready, 1)
                dve.wait_ge(ident_ready, 1)

        hyperbolic_block(nc, x, cond_t, *l0, XT, ident, ident_bf)
        w_router, router_bias, w_experts = l2
        with ExitStack() as held:
            parts = [held.enter_context(nc.sbuf_tensor(f"l2_weights_{n}", [P, L2_COLS], F32R)) for n in ("high", "low")]
            gru(nc, *l1, cond_t, XT, ident_bf, w_experts, parts, ident)
            shared_and_routed(nc, w_router, router_bias, parts, cond_t, XT, ident)
        gated_experts(nc, *l3, cond_t, XT, ident, out)


def kernel(**inputs):
    from concourse import bacc
    from concourse.bass_utils import run_bass_kernel_spmd

    def own(name):
        return np.asarray(inputs[name])

    def joined(prefix, names):
        return np.concatenate([own(prefix + n) for n in names], axis=-1)

    def turned(name):
        return own(name).swapaxes(-1, -2)

    def row_tiles(w):
        return w.reshape(len(w), -1, P, w.shape[-1]).transpose(2, 0, 1, 3).reshape(P, -1)

    def features_first(prefix, routed, shared):
        both = np.concatenate([own(prefix + routed), own(prefix + shared)[None]])
        return both.reshape(len(both), -1, P).transpose(2, 0, 1)

    a, g, m, e = "L0_cond_", "L1_cond_", "L2_cond_", "L3_cond_"
    groups = {
        "x": [own("x")], "cond_t": [turned("cond_1024")],
        "l0": [joined(a, ("w_q", "w_k", "w_v")), joined(a, ("b_q", "b_k", "b_v"))]
              + [own(a + n) for n in ("w_o", "b_o", "w_f1", "b_f1", "w_f2", "b_f2", "w_ada", "b_ada")],
        "l1": [joined(g, ("W_z", "W_r", "W")), joined(g, ("U_z", "U_r", "U")), joined(g, ("C_z", "C_r", "C")),
               joined(g, ("b_z", "b_r", "b"))],
        "l2": [turned(m + "W_router"), own(m + "router_bias"),
               np.concatenate([row_tiles(turned(m + n)) for n in ("s_w1", "s_w3", "s_w2", "r_w1", "r_w2")], axis=1)],
        "l3": [own(e + n) for n in ("gate_w", "gate_b", "time_w", "time_b", "ew1", "ew2", "sw1", "sw2")]
              + [features_first(e, "eb1", "sb1"), features_first(e, "eb2", "sb2")],
        "eye": [np.eye(P, dtype=np.float32)],
    }
    nc = bacc.Bacc("TRN2", target_bir_lowering=False, num_devices=1)
    arrays, args = {}, {}
    for group, values in groups.items():
        args[group] = []
        for n, v in enumerate(values):
            name = f"in_{group}_{n}"
            arrays[name] = np.ascontiguousarray(v)
            args[group].append(nc.dram_tensor(name, arrays[name].shape, mybir.dt.from_np(arrays[name].dtype),
                                              kind="ExternalInput").ap())
    out = nc.dram_tensor("out_t", (D, XT_COLS), F32, kind="ExternalOutput").ap()
    layers(nc, args["x"][0], args["cond_t"][0], args["l0"], args["l1"], args["l2"], args["l3"], args["eye"][0], out)
    r = run_bass_kernel_spmd(nc, [arrays], core_ids=[0])
    return r.results[0]["out_t"].reshape(D, S, B).transpose(2, 1, 0)
```

```python
import math
from contextlib import ExitStack

import concourse.bass as bass
from concourse import mybir
import numpy as np

ALU = mybir.AluOpType
ACT = mybir.ActivationFunctionType
AX = mybir.AxisListType
F32 = mybir.dt.float32
F32R = mybir.dt.float32r
BF16 = mybir.dt.bfloat16
F16 = mybir.dt.float16
I32 = mybir.dt.int32

P = 128
B, S, D = 4, 512, 256
NT = S // P
H = 16
HD = D // H
FF = 1024
EPS = 1e-7
EPS2 = EPS * EPS
MAX_TANH = float(np.float32(1.0 - 1e-5))
ATANH_MAX = float(np.arctanh(np.float64(np.float32(1.0 - 1e-5))))


def beta(a, b):
    return math.exp(math.lgamma(a) + math.lgamma(b) - math.lgamma(a + b))


TO_HEADS = beta(HD / 2, 0.5) / beta(D / 2, 0.5)
SLOTS = 8
Q_SLOTS = ((0, 0, 1, 2), (0, 4, 1, 1), (1, 2, 1, 2), (1, 6, 1, 1), (2, 5, 2, 2))
K_SLOTS = ((0, 0, 2, 2), (0, 5, 1, 1), (1, 1, 2, 2), (1, 7, 1, 1), (2, 4, 2, 2))
L0_DVE_STEPS = 18
CH = 16
XT_COLS = B * S
TOP_K = 2
N_SHARED, N_ROUTED = 2, 8
HID_S, HID_R = 512, 256
PRODUCTS = ((0, 0), (0, 1), (1, 0))
L2_SHAPES = ((N_SHARED, 2, HID_S), (N_SHARED, 2, HID_S), (N_SHARED, HID_S // P, D), (N_ROUTED, 2, HID_R), (N_ROUTED, HID_R // P, D))
L2_COLS = sum(e * k * n for e, k, n in L2_SHAPES)


def parts_of(w, n):
    at = sum(e * k * c for e, k, c in L2_SHAPES[:n])
    e, k, c = L2_SHAPES[n]
    return w[:, at:at + e * k * c].rearrange("p (e k c) -> p e k c", e=e, k=k)




def vector_columns(dve, step, ready, done, at):
    count = {"step": 0, "ready": 0, "done": 0}

    def link(ins):
        count["step"] += 1
        ins.then_inc(step, 1)
        dve.wait_ge(step, at("step", count["step"]))

    def ask(ins):
        count["ready"] += 1
        ins.then_inc(ready, 1)
        dve.wait_ge(ready, at("ready", count["ready"]))

    def answered():
        count["done"] += 1
        dve.wait_ge(done, at("done", count["done"]))

    def newton(y, v, t):
        answered()
        link(dve.tensor_tensor(t, y, y, ALU.mult))
        link(dve.scalar_tensor_tensor(t, t, -0.5, v, ALU.mult, ALU.mult))
        link(dve.scalar_tensor_tensor(y, t, 1.5, y, ALU.add, ALU.mult))

    def clamp(ss, root, out, t):
        ask(dve.tensor_scalar(ss, ss, EPS2, None, ALU.max))
        newton(root, ss, t)
        link(dve.tensor_scalar(out, root, ATANH_MAX, 1.0, ALU.mult, ALU.min))

    return link, ask, answered, newton, clamp, count


def scalar_columns(act, step, ready, done, at):
    count = {"step": 0, "ready": 0}

    def arrive():
        count["ready"] += 1
        act.wait_ge(ready, at("ready", count["ready"]))

    def rsqrt(dst, src, tmp):
        arrive()
        count["step"] += 1
        act.activation(tmp, src, ACT.Ln).then_inc(step, 1)
        act.wait_ge(step, at("step", count["step"]))
        act.activation(dst, tmp, ACT.Exp, scale=-0.5).then_inc(done, 1)

    return arrive, rsqrt, count


def norm_columns(dve, columns, c, BS, MV):
    link, ask, answered, newton, _clamp, _count = columns
    mean, var = MV[:, 0, :], MV[:, 1, :]
    link(dve.tensor_tensor(mean, BS[:, :, 1], BS[:, :, 4], ALU.add))
    link(dve.tensor_scalar(mean, mean, 0.5, None, ALU.mult))
    link(dve.tensor_tensor(c(16), BS[:, :, 1], BS[:, :, 4], ALU.subtract))
    link(dve.tensor_tensor(c(16), c(16), c(16), ALU.mult))
    link(dve.tensor_tensor(var, BS[:, :, 2], BS[:, :, 5], ALU.add))
    link(dve.tensor_scalar(var, var, 1.0 / D, None, ALU.mult))
    link(dve.scalar_tensor_tensor(var, c(16), 0.25, var, ALU.mult, ALU.add))
    link(dve.tensor_tensor(c(21), mean, mean, ALU.mult))
    link(dve.tensor_tensor(c(21), c(21), var, ALU.add))
    link(dve.tensor_scalar(c(22), c(21), float(D), None, ALU.mult))
    ask(dve.tensor_scalar(c(0), c(22), EPS2, None, ALU.max))
    newton(c(1), c(0), c(16))
    link(dve.tensor_tensor(c(2), c(0), c(1), ALU.mult))
    ask(dve.tensor_scalar(c(2), c(2), MAX_TANH, None, ALU.min))
    link(dve.tensor_tensor(c(16), c(2), c(2), ALU.mult))
    link(dve.tensor_scalar(c(17), c(16), 1.0 / 15, None, ALU.mult))
    for odd in (13, 11, 9, 7, 5, 3):
        link(dve.scalar_tensor_tensor(c(17), c(17), 1.0 / odd, c(16), ALU.add, ALU.mult))
    link(dve.scalar_tensor_tensor(c(17), c(17), 1.0, c(2), ALU.add, ALU.mult))
    link(dve.tensor_scalar(c(18), c(2), 0.25, None, ALU.is_lt))
    answered()
    link(dve.tensor_tensor(c(3), c(3), c(4), ALU.subtract))
    link(dve.scalar_tensor_tensor(c(17), c(3), -0.5, c(17), ALU.mult, ALU.add))
    link(dve.tensor_tensor(c(17), c(17), c(18), ALU.mult))
    link(dve.scalar_tensor_tensor(c(17), c(3), 0.5, c(17), ALU.mult, ALU.add))
    link(dve.tensor_tensor(c(17), c(17), c(1), ALU.mult))
    link(dve.tensor_tensor(c(16), c(17), c(17), ALU.mult))
    link(dve.tensor_tensor(c(16), c(16), var, ALU.mult))
    ask(dve.tensor_scalar(c(5), c(16), 1e-6, None, ALU.add))
    newton(c(6), c(5), c(16))
    link(dve.tensor_tensor(c(18), c(17), c(6), ALU.mult))


def norm_scalars(act, arrive, rsqrt, done, c):
    rsqrt(c(1), c(0), c(20))
    arrive()
    act.activation(c(3), c(2), ACT.Ln, scale=1.0, bias=1.0)
    act.activation(c(4), c(2), ACT.Ln, scale=-1.0, bias=1.0).then_inc(done, 1)
    rsqrt(c(6), c(5), c(20))


def project_to_heads(nc, x, cond_t, w_qkv, b_qkv, w_ada, b_ada, ada, X, QKV, HF, C, ident):
    W = B * NT
    with ExitStack() as ctx:
        def sb(name, shape, dt=F32):
            return ctx.enter_context(nc.sbuf_tensor(name, shape, dt))

        def sem(name):
            return ctx.enter_context(nc.semaphore(name))

        Wqkv = sb("w_qkv_sb", [P, 2, 3 * D])
        W_ada = sb("w_ada_sb", [P, 2, 6 * D])
        bias_ada = sb("bias_ada", [P, 6 * D])
        bias_qkv = sb("bias_qkv", [P, 3 * D])
        cond = sb("cond_sb", [P, 2, B])
        U = sb("u", [P, NT, D])
        UT = sb("u_t", [P, NT, 2, P])
        SQ = sb("squares_qkv", [P, 2, 3 * D])
        cond_rep = sb("cond_rep", [P, 2, B, P])
        BS = sb("bn", [P, W, 6])
        MV = sb("mean_var", [P, 2, W])
        SSH = sb("head_ss", [P, W, 3 * H])
        HR = sb("head_rsqrt", [P, W, 3 * H])
        HT = sb("head_tmp", [P, W, 3 * H])
        LT = sb("log_tmp", [P, W, 3 * H])
        T3 = sb("qkv_cols", [P, 4, 3 * W])
        JKA = sb("junk_act", [P, D])
        PS = ctx.enter_context(nc.psum_tensor("ps_qkv", [P, 8, 512], F32))

        loads, cond_in = sem("loads"), sem("cond_in")
        cond_ready, ada_mm, ada_done = sem("cond_ready"), sem("ada_mm"), sem("ada_done")
        dve_step, act_step, cols_ready, cols_done = sem("dve_step"), sem("act_step"), sem("cols_ready"), sem("cols_done")
        centred, u_ready, u_turned, u_copied, u_ss = sem("centred"), sem("u_ready"), sem("u_turned"), sem("u_copied"), sem("u_ss")
        qkv_mm, raw_copied, qkv_out, qkv_sq, sq_summed = (
            sem("qkv_mm"), sem("raw_copied"), sem("qkv_out"), sem("qkv_sq"), sem("sq_summed"))
        LOADS = 16 * 4
        flat_qkv = QKV[:].rearrange("p n h d -> p n (h d)")

        def c(n):
            return C[:, n, :]

        def at(kind, n):
            return n

        def parts(j):
            return ((0, 512, 2 + 2 * (j % 2)), (512, 768, 3 + 2 * (j % 2)))

        with nc.Block() as block:
            @block.sync
            def _(sp):
                sp.dma_start(cond[:], cond_t.rearrange("(k p) b -> p k b", p=P)).then_inc(cond_in, 16)
                sp.dma_start(W_ada[:], w_ada.rearrange("(k p) n -> p k n", p=P)).then_inc(cond_in, 16)
                sp.dma_start(X[:], x.rearrange("b (j p) d -> p (b j) d", p=P)).then_inc(loads, 16)
                sp.dma_start(Wqkv[:], w_qkv.rearrange("(k p) n -> p k n", p=P)).then_inc(loads, 16)
                for dst, src in ((bias_qkv, b_qkv), (bias_ada, b_ada)):
                    n = src.shape[0]
                    sp.dma_start(dst[:], src.rearrange("(a n) -> a n", a=1).broadcast_to([P, n])).then_inc(loads, 16)

            @block.tensor
            def _(pe):
                pe.wait_ge(cond_in, 32)
                pe.wait_ge(cond_ready, 1)
                for b in range(B):
                    for n in range(3):
                        g = b * 3 + n
                        if g >= 8:
                            pe.wait_ge(ada_done, g - 7)
                        for k in range(2):
                            mm = pe.matmul(PS[:, g % 8, :], cond_rep[:, k, b, :], W_ada[:, k, n * 512:(n + 1) * 512],
                                           start=(k == 0), stop=(k == 1))
                        mm.then_inc(ada_mm, 1)
                pe.wait_ge(loads, LOADS)
                pe.wait_ge(ada_done, 12)
                with pe.Fori(0, B) as i:
                    for j in range(NT):
                        pe.wait_ge(u_ready, i * NT + j + 1)
                        if j >= 2:
                            pe.wait_ge(u_copied, i * NT + j - 1)
                        for k in range(2):
                            mm = pe.transpose(PS[:, j % 2, k * P:k * P + P], U[:, j, k * P:k * P + P], ident[:])
                        mm.then_inc(u_turned, 1)
                    for j in range(NT):
                        pe.wait_ge(u_copied, i * NT + j + 1)
                        pe.wait_ge(raw_copied, i * NT + max(j - 1, 0) + 1)
                        for a, z, bk in parts(j):
                            for k in range(2):
                                mm = pe.matmul(PS[:, bk, 0:z - a], UT[:, j, k, :], Wqkv[:, k, a:z],
                                               start=(k == 0), stop=(k == 1))
                        mm.then_inc(qkv_mm, 1)

            @block.scalar
            def _(act):
                act.preload_act_table_set("natural_log_exp_and_others")
                arrive, rsqrt, count = scalar_columns(act, act_step, cols_ready, cols_done, at)
                norm_scalars(act, arrive, rsqrt, cols_done, c)
                act.sem_inc(raw_copied, 1)
                with act.Fori(0, B) as i:
                    for j in range(NT):
                        act.wait_ge(u_ready, i * NT + j + 1)
                        if j:
                            act.wait_ge(u_ss, i * NT + j)
                        act.activation(JKA[:], U[:, j, :], ACT.Square, accum_out=C[:, 7, bass.ds(i * NT + j, 1)]).then_inc(u_ss, 1)
                        act.wait_ge(u_turned, i * NT + j + 1)
                        act.activation(UT[:, j, :, :].rearrange("p k t -> p (k t)"), PS[:, j % 2, 0:D], ACT.Copy).then_inc(u_copied, 1)
                    act.wait_ge(u_ss, (i + 1) * NT)
                    for j in range(NT):
                        act.wait_ge(qkv_mm, i * NT + j + 1)
                        for a, z, bk in parts(j):
                            ins = act.activation(flat_qkv[:, bass.ds(i * NT + j, 1), a:z], PS[:, bk:bk + 1, 0:z - a], ACT.Copy)
                        ins.then_inc(raw_copied, 1)
                rsqrt(c(8), c(7), c(20))
                with act.Fori(0, B) as i:
                    for j in range(NT):
                        act.wait_ge(qkv_out, i * NT + j + 1)
                        act.wait_ge(sq_summed, i * NT + max(j - 1, 0) + 1)
                        act.activation(SQ[:, j % 2:j % 2 + 1, :], flat_qkv[:, bass.ds(i * NT + j, 1), :], ACT.Square).then_inc(qkv_sq, 1)
                rsqrt(T3[:, 1, :], T3[:, 0, :], T3[:, 3, :])
                rsqrt(HR[:], SSH[:], LT[:])

            @block.vector
            def _(dve):
                dve.wait_ge(cond_in, 32)
                dve.tensor_copy(cond_rep[:], cond[:].unsqueeze(3).broadcast_to([P, 2, B, P])).then_inc(cond_ready, 1)
                dve.sem_inc(sq_summed, 1)
                dve.wait_ge(loads, LOADS)
                columns = vector_columns(dve, dve_step, cols_ready, cols_done, at)
                link, ask, answered, newton, clamp, count = columns
                for n in range(W):
                    ins = dve.bn_stats(BS[:, n, :], X[:, n, :])
                link(ins)

                def modulation(g):
                    b, n = g // 3, g % 3
                    dve.wait_ge(ada_mm, g + 1)
                    dve.tensor_tensor(ada[:, b, :, :].rearrange("p m d -> p (m d)")[:, n * 512:n * 512 + 512], PS[:, g % 8, :],
                                      bias_ada[:, n * 512:n * 512 + 512], ALU.add).then_inc(ada_done, 1)

                for g in range(4):
                    modulation(g)
                norm_columns(dve, columns, c, BS, MV)
                for g in range(4, 12):
                    modulation(g)
                dve.wait_ge(ada_done, 3 * B)
                for m in (1, 4):
                    dve.tensor_scalar(ada[:, :, m, :], ada[:, :, m, :], 1.0, None, ALU.add).then_inc(cond_ready, 1)
                dve.wait_ge(cond_ready, 3)
                with dve.Fori(0, B) as i:
                    for j in range(NT):
                        tile = bass.ds(i * NT + j, 1)
                        u = U[:, j:j + 1, :]
                        dve.scalar_tensor_tensor(u, X[:, tile, :], MV[:, 0, tile], ada[:, bass.ds(i, 1), 1, :],
                                                 ALU.subtract, ALU.mult).then_inc(centred, 1)
                    for j in range(NT):
                        tile = bass.ds(i * NT + j, 1)
                        u = U[:, j:j + 1, :]
                        dve.wait_ge(centred, i * NT + j + 1)
                        dve.scalar_tensor_tensor(u, u, C[:, 18, tile], ada[:, bass.ds(i, 1), 0, :],
                                                 ALU.mult, ALU.add).then_inc(u_ready, 1)
                    dve.wait_ge(u_turned, (i + 1) * NT)
                    dve.wait_ge(u_ss, (i + 1) * NT)
                clamp(c(7), c(8), c(19), c(16))

                def sum_squares(i, j):
                    dve.wait_ge(qkv_sq, i * NT + j + 1)
                    dve.tensor_reduce(SSH[:, bass.ds(i * NT + j, 1), :].rearrange("p a h -> p (a h)"),
                                      SQ[:, j % 2, :].rearrange("p (h d) -> p h d", d=HD), AX.X, ALU.add).then_inc(sq_summed, 1)

                with dve.Fori(0, B) as i:
                    for j in range(NT):
                        tile = bass.ds(i * NT + j, 1)
                        dve.wait_ge(raw_copied, i * NT + j + 2)
                        dve.scalar_tensor_tensor(flat_qkv[:, tile, :], flat_qkv[:, tile, :], C[:, 19, tile],
                                                 bias_qkv[:].unsqueeze(1), ALU.mult, ALU.add).then_inc(qkv_out, 1)
                        if j:
                            sum_squares(i, j - 1)
                    sum_squares(i, NT - 1)
                dve.wait_ge(sq_summed, W + 1)

                def by_head(t):
                    return t[:].rearrange("p n (t h) -> p (n t) h", h=H)

                link(dve.tensor_reduce(T3[:, 0, :], by_head(SSH), AX.X, ALU.add))
                ask(dve.tensor_scalar(T3[:, 0, :], T3[:, 0, :], EPS2, None, ALU.max))
                ask(dve.tensor_scalar(SSH[:], SSH[:], EPS2, None, ALU.max))
                newton(T3[:, 1, :], T3[:, 0, :], T3[:, 2, :])
                link(dve.tensor_scalar(T3[:, 1, :], T3[:, 1, :], ATANH_MAX, 1.0, ALU.mult, ALU.min))
                link(dve.tensor_scalar(T3[:, 1, :], T3[:, 1, :], TO_HEADS, None, ALU.mult))
                newton(HR[:], SSH[:], HT[:])
                link(dve.scalar_tensor_tensor(by_head(HF), by_head(HR), ATANH_MAX,
                                              T3[:, 1, :].unsqueeze(2).broadcast_to([P, 3 * W, H]), ALU.mult, ALU.min))


def attend(nc, w_o, b_o, ada, X, QKV, HF, C, XU, ident, ident_bf, squared):
    with ExitStack() as ctx:
        def sb(name, shape, dt=F32):
            return ctx.enter_context(nc.sbuf_tensor(name, shape, dt))

        def sem(name):
            return ctx.enter_context(nc.semaphore(name))

        Wo = sb("w_o_sb", [P, 2, D])
        bias_o = sb("bias_o", [P, D])
        UT = sb("attn_t", [P, NT, 2, P])
        QS, R1 = (sb(name, [P, 2 * H, HD])[:] for name in ("qk_scaled", "qk_rest"))
        JKA = sb("junk_attn", [P, D])
        JKV = sb("junk_dve_attn", [P, 2, D])
        PT = [sb(f"qk_parts_{n}", [P, 3, 2 * H, HD], BF16) for n in range(2)]
        ST = sb("qk_stack", [P, 2 * H, SLOTS, HD], BF16)
        QKT = sb("qk_t", [P, 2 * H, S], BF16)
        VP = sb("v_ones", [P, NT, H, 32])
        PR = sb("probs", [P, 4, 2, S])
        OT = sb("o_t", [P, 4, S])
        SQ = PR[:, 1, :, :].rearrange("p c t -> p (c t)").rearrange("p (j d) -> p j d", j=NT)
        OV = PR[:, 0, :, :].rearrange("p c t -> p (c t)").rearrange("p (j h d) -> p j h d", j=NT, h=H)    
        AT = sb("tangent", [P, NT, D])
        SSH = sb("o_ss", [P, NT, H])
        HR = sb("o_rsqrt", [P, NT, H])
        OF = sb("o_factor", [P, NT, H])
        HT = sb("o_tmp", [P, NT, H])
        LT = sb("o_log", [P, NT, H])
        RS = sb("row_recip", [P, NT, H])
        PS = ctx.enter_context(nc.psum_tensor("ps_attn", [P, 8, 512], F32))

        loads, v_cleared = sem("loads_o"), sem("v_cleared")
        cut_step = sem("cut_step")
        dve_step, act_step, cols_ready, cols_done = sem("dve_step_a"), sem("act_step_a"), sem("cols_ready_a"), sem("cols_done_a")
        stacked, stack_turned = sem("stacked"), sem("stack_turned")
        stack_copied_v, stack_copied_a = sem("stack_copied_v"), sem("stack_copied_a")
        scores_mm, probs_ready, pv_mm = sem("scores_mm"), sem("probs_ready"), sem("pv_mm")
        o_copied, o_turned, o_out, o_sq = sem("o_copied"), sem("o_turned"), sem("o_out"), sem("o_sq")
        attn_in, attn_turned, attn_copied = sem("attn_in"), sem("attn_turned"), sem("attn_copied")
        attn_mm, attn_out, gained, dotted = sem("attn_mm"), sem("attn_out"), sem("gained_a"), sem("dotted_a")

        def bank(n, a=0, z=512):
            return PS[:, n, a:z]

        def bank_bf(n):
            return PS[:, n, :].bitcast(BF16)

        def flat(ap):
            return ap.rearrange("p a b -> p (a b)")

        STEPS = {"step": L0_DVE_STEPS, "ready": 2, "done": 2}

        with nc.Block() as block:
            @block.sync
            def _(sp):
                sp.dma_start(Wo[:], w_o.rearrange("(k p) n -> p k n", p=P)).then_inc(loads, 16)
                sp.dma_start(bias_o[:], b_o.rearrange("(a n) -> a n", a=1).broadcast_to([P, D])).then_inc(loads, 16)

            @block.tensor
            def _(pe):
                pe.wait_ge(loads, 32)

                def turn_stack(i, j):
                    pe.wait_ge(stacked, i * NT * 10 + (j + 1) * 10)
                    for g in range(4):
                        n = j * 4 + g
                        if n >= 2:
                            pe.wait_ge((stack_copied_v, stack_copied_a)[n % 2], i * 8 + (n - 2) // 2 + 1)
                        for h in range(8):
                            mm = pe.transpose(bank_bf(6 + n % 2)[:, h * P:h * P + P],
                                              flat(ST[:, g * 8 + h, :, :]), ident_bf[:])
                        mm.then_inc(stack_turned, 1)

                def attention(i):
                    pe.wait_ge(stack_copied_v, i * 8 + 8)
                    pe.wait_ge(stack_copied_a, i * 8 + 8)

                    def scores(m):
                        n, e = m // 2, m % 2
                        hg, kt = n // 4, n % 4
                        if m >= 3:
                            pe.wait_ge(probs_ready, i * 32 + m - 2)
                        for c in range(2):
                            h = hg * 4 + e * 2 + c
                            mm = pe.matmul(bank(2 * (m % 3) + c), QKT[:, H + h, kt * P:kt * P + P], QKT[:, h, :],
                                           start=True, stop=True)
                        mm.then_inc(scores_mm, 1)

                    def weighted(m):
                        n, e = m // 2, m % 2
                        hg, kt = n // 4, n % 4
                        pe.wait_ge(probs_ready, i * 32 + m + 1)
                        if m % 8 == 0 and hg >= 2:
                            pe.wait_ge(o_copied, i * 4 + hg - 1)
                        for q in range(2 * e, 2 * e + 2):
                            mm = pe.matmul(PS[32 * q:32 * q + 32, 6 + hg % 2, :], VP[:, kt, hg * 4 + q, :],
                                           PR[:, m % 4, q % 2, :], start=(kt == 0), stop=(kt == 3),
                                           skip_group_check=True)
                        mm.then_inc(pv_mm, 1)

                    scores(0)
                    scores(1)
                    for m in range(32):
                        if m >= 1:
                            weighted(m - 1)
                        if m < 30:
                            scores(m + 2)
                    weighted(31)

                def finish(i, following):
                    pe.wait_ge(o_copied, i * 4 + 4)
                    for j in range(NT):
                        if j >= 2:
                            pe.wait_ge(o_out, i * NT + j - 1)
                        for g in range(4):
                            mm = pe.transpose(bank(j % 2, g * P, g * P + P), OT[:, g, j * P:j * P + P], ident[:])
                        mm.then_inc(o_turned, 1)
                    if following is not None:
                        for j in range(3):
                            turn_stack(following, j)
                    for j in range(NT):
                        pe.wait_ge(attn_in, i * NT + j + 1)
                        if j >= 2:
                            pe.wait_ge(attn_copied, i * NT + j - 1)
                        for k in range(2):
                            mm = pe.transpose(bank(2 + j % 2, k * P, k * P + P), AT[:, j, k * P:k * P + P], ident[:])
                        mm.then_inc(attn_turned, 1)
                    for j in range(NT):
                        pe.wait_ge(attn_copied, i * NT + j + 1)
                        if j >= 2:
                            pe.wait_ge(attn_out, i * NT + j - 1)
                        for k in range(2):
                            mm = pe.matmul(bank(4 + j % 2, 0, D), UT[:, j, k, :], Wo[:, k, :], start=(k == 0), stop=(k == 1))
                        mm.then_inc(attn_mm, 1)
                    if following is not None:
                        turn_stack(following, 3)

                for j in range(NT):
                    turn_stack(0, j)
                with pe.Fori(0, B - 1) as i:
                    attention(i)
                    finish(i, i + 1)
                attention(B - 1)
                finish(B - 1, None)

            def c(n):
                return C[:, n, 0:NT]

            @block.scalar
            def _(act):
                act.preload_act_table_set("natural_log_exp_and_others")
                act.sem_inc(squared, 1)

                def copy_stack(i, j):
                    for n in (4 * j + 1, 4 * j + 3):
                        act.wait_ge(stack_turned, i * 16 + n + 1)
                        g = n % 4
                        act.activation(QKT[:, g * 8:g * 8 + 8, j * P:j * P + P],
                                       bank_bf(7).rearrange("p (h t) -> p h t", t=P), ACT.Copy).then_inc(stack_copied_a, 1)

                def attention(i):
                    for m in range(32):
                        act.wait_ge(scores_mm, i * 32 + m + 1)
                        if m >= 4:
                            act.wait_ge(pv_mm, i * 32 + m - 3)
                        act.activation(PR[:, m % 4, :, :], PS[:, 2 * (m % 3):2 * (m % 3) + 2, :], ACT.Exp,
                                       scale=1.0 / math.sqrt(HD)).then_inc(probs_ready, 1)

                def finish(i, following):
                    arrive, rsqrt, count = scalar_columns(act, act_step, cols_ready, cols_done, lambda kind, n: i * 2 + n)
                    for j in range(NT):
                        act.wait_ge(o_out, i * NT + j + 1)
                        act.activation(SQ[:, j, :], flat(OV[:, j, :, :]), ACT.Square).then_inc(o_sq, 1)
                    if following is not None:
                        copy_stack(following, 0)
                    rsqrt(HR[:], SSH[:], LT[:])
                    if following is not None:
                        copy_stack(following, 1)
                    rsqrt(c(1), c(0), c(20))
                    if following is not None:
                        copy_stack(following, 2)
                    for j in range(NT):
                        act.wait_ge(attn_turned, i * NT + j + 1)
                        act.activation(flat(UT[:, j, :, :]), bank(2 + j % 2, 0, D), ACT.Copy).then_inc(attn_copied, 1)
                    for j in range(NT):
                        act.wait_ge(attn_out, i * NT + j + 1)
                        act.wait_ge(squared, i * NT + j + 1)
                        act.activation(JKA[:].unsqueeze(1), XU[:, bass.ds(i * NT + j, 1), :], ACT.Square,
                                       accum_out=C[:, 9, bass.ds(i * NT + j, 1)]).then_inc(squared, 1)
                    if following is not None:
                        copy_stack(following, 3)

                for j in range(NT):
                    copy_stack(0, j)
                with act.Fori(0, B - 1) as i:
                    attention(i)
                    finish(i, i + 1)
                attention(B - 1)
                finish(B - 1, None)

            @block.vector
            def _(dve):
                dve.memset(VP[:], 0.0).then_inc(v_cleared, 1)
                dve.wait_ge(v_cleared, 1)
                dve.memset(VP[:, :, :, HD:HD + 1], 1.0).then_inc(v_cleared, 1)
                dve.wait_ge(v_cleared, 2)
                dve.wait_ge(loads, 32)

                def tokens(i, j, a, z):
                    return QKV[:, bass.ds(i * NT + j, 1), a:z, :].rearrange("p a h d -> p (a h) d")

                def heads(i, j, a, z):
                    return HF[:, bass.ds(i * NT + j, 1), a:z].rearrange("p a h -> p (a h)").unsqueeze(2).broadcast_to([P, z - a, HD])

                def copy_stack(i, j):
                    for n in (4 * j, 4 * j + 2):
                        dve.wait_ge(stack_turned, i * 16 + n + 1)
                        g = n % 4
                        dve.tensor_copy(QKT[:, g * 8:g * 8 + 8, j * P:j * P + P],
                                        bank_bf(6).rearrange("p (h t) -> p h t", t=P)).then_inc(stack_copied_v, 1)

                def cut_parts(i, j):
                    def cut(n, ins):
                        ins.then_inc(cut_step, 1)
                        dve.wait_ge(cut_step, i * NT * 5 + j * 5 + n + 1)

                    p1, p2, p3 = (PT[j % 2][:, n, :, :] for n in range(3))
                    cut(0, dve.tensor_tensor(QS, tokens(i, j, 0, 2 * H), heads(i, j, 0, 2 * H), ALU.mult))
                    cut(1, dve.tensor_copy(p1, QS))
                    cut(2, dve.tensor_tensor(R1, QS, p1, ALU.subtract))
                    cut(3, dve.tensor_copy(p2, R1))
                    cut(4, dve.tensor_tensor(p3, R1, p2, ALU.subtract))

                def fill_stack(i, j, first=False):
                    if not first:
                        dve.wait_ge(stack_turned, i * 16 + j * 4)
                    for half, copies in ((0, Q_SLOTS), (1, K_SLOTS)):
                        hs = slice(half * H, half * H + H)
                        for part, first, slot_step, n in copies:
                            dst = ST[:, hs, first:first + slot_step * (n - 1) + 1:slot_step, :]
                            src = PT[j % 2][:, part, hs, :].unsqueeze(2).broadcast_to([P, H, n, HD])
                            dve.tensor_copy(dst, src).then_inc(stacked, 1)

                def scale_v(i, j):
                    dve.tensor_tensor(VP[:, j, :, 0:HD], tokens(i, j, 2 * H, 3 * H), heads(i, j, 2 * H, 3 * H), ALU.mult)

                def attention(i, following):
                    if following is not None:
                        cut_parts(following, 0)
                        fill_stack(following, 0)
                        cut_parts(following, 1)
                        cut_parts(following, 2)
                    for g in range(4):
                        dve.wait_ge(pv_mm, i * 32 + 8 * g + 8)
                        dve.tensor_copy(OT[:, g, :], bank(6 + g % 2)).then_inc(o_copied, 1)

                def finish(i, following):
                    link, ask, answered, newton, clamp, count = vector_columns(
                        dve, dve_step, cols_ready, cols_done, lambda kind, n: i * STEPS[kind] + n)

                    def sum_o(j):
                        dve.wait_ge(o_sq, i * NT + j + 1)
                        return dve.tensor_reduce(SSH[:, j, :], SQ[:, j, :].rearrange("p (h d) -> p h d", d=HD), AX.X, ALU.add)

                    for j in range(NT):
                        dve.wait_ge(o_turned, i * NT + j + 1)
                        o = bank(j % 2).rearrange("p (h d) -> p h d", d=32)
                        link(dve.reciprocal(RS[:, j, :].unsqueeze(2), o[:, :, HD:HD + 1]))
                        dve.tensor_tensor(OV[:, j, :, :], o[:, :, 0:HD], RS[:, j, :].unsqueeze(2).broadcast_to([P, H, HD]),
                                          ALU.mult).then_inc(o_out, 1)
                        if j:
                            sum_o(j - 1)
                    link(sum_o(NT - 1))
                    ask(dve.tensor_scalar(SSH[:], SSH[:], EPS2, None, ALU.max))
                    if following is not None:
                        for j in range(NT):
                            scale_v(following, j)
                        copy_stack(following, 0)
                        fill_stack(following, 1)
                        cut_parts(following, 3)
                    newton(HR[:], SSH[:], HT[:])
                    link(dve.tensor_scalar(OF[:], HR[:], ATANH_MAX, 1.0, ALU.mult, ALU.min))
                    link(dve.tensor_tensor(HT[:], OF[:], OF[:], ALU.mult))
                    link(dve.tensor_tensor(HT[:], HT[:], SSH[:], ALU.mult))
                    link(dve.tensor_reduce(c(0), HT[:], AX.X, ALU.add))
                    ask(dve.tensor_scalar(c(0), c(0), 1.0 / TO_HEADS ** 2, EPS2, ALU.mult, ALU.max))
                    if following is not None:
                        copy_stack(following, 1)
                        fill_stack(following, 2)
                    newton(c(1), c(0), c(16))
                    link(dve.tensor_scalar(c(2), c(1), ATANH_MAX, 1.0, ALU.mult, ALU.min))
                    link(dve.tensor_scalar(c(2), c(2), 1.0 / TO_HEADS, None, ALU.mult))
                    link(dve.tensor_tensor(OF[:], OF[:], c(2).unsqueeze(2).broadcast_to([P, NT, H]), ALU.mult))
                    for j in range(NT):
                        dve.tensor_tensor(AT[:, j, :].rearrange("p (h d) -> p h d", d=HD), OV[:, j, :, :],
                                          OF[:, j, :].unsqueeze(2).broadcast_to([P, H, HD]), ALU.mult).then_inc(attn_in, 1)
                    if following is not None:
                        copy_stack(following, 2)
                        fill_stack(following, 3)
                    for j in range(NT):
                        dve.wait_ge(attn_mm, i * NT + j + 1)
                        dve.tensor_tensor(XU[:, bass.ds(i * NT + j, 1), :], PS[:, 4 + j % 2:5 + j % 2, 0:D],
                                          bias_o[:].unsqueeze(1), ALU.add).then_inc(attn_out, 1)
                    if following is not None:
                        copy_stack(following, 3)
                    for j in range(NT):
                        tile = bass.ds(i * NT + j, 1)
                        dve.wait_ge(squared, i * NT + j + 2)
                        dve.tensor_tensor(XU[:, tile, :], XU[:, tile, :], ada[:, bass.ds(i, 1), 2, :], ALU.mult).then_inc(gained, 1)
                    for j in range(NT):
                        tile = bass.ds(i * NT + j, 1)
                        dve.wait_ge(gained, i * NT + j + 1)
                        for n, (other, column) in enumerate(((X, 23), (XU, 11))):
                            dve.scalar_tensor_tensor(JKV[:, n:n + 1, :], other[:, tile, :], 1.0, XU[:, tile, :], ALU.mult, ALU.mult,
                                                     accum_out=C[:, column, tile]).then_inc(dotted, 1)
                        dve.wait_ge(dotted, (i * NT + j + 1) * 2)
                    assert count == STEPS, count

                for j in range(NT):
                    cut_parts(0, j)
                    scale_v(0, j)
                    fill_stack(0, j, first=(j == 0))
                    copy_stack(0, j)
                with dve.Fori(0, B - 1) as i:
                    attention(i, i + 1)
                    finish(i, i + 1)
                attention(B - 1, None)
                finish(B - 1, None)


def feed_forward(nc, w_f1, b_f1, w_f2, b_f2, ada, X, C, XU, XT, ident, squared):
    W = B * NT
    with ExitStack() as ctx:
        def sb(name, shape, dt=F32):
            return ctx.enter_context(nc.sbuf_tensor(name, shape, dt))

        def sem(name):
            return ctx.enter_context(nc.semaphore(name))

        W1 = [sb(f"w_f1_{n}", [P, 2, FF], F32R) for n in ("high", "low")]
        W2 = [sb(f"w_f2_{n}", [P, FF // P, D], F32R) for n in ("high", "low")]
        bias_f1 = sb("bias_f1", [P, FF])
        bias_f2 = sb("bias_f2", [P, D])
        X1 = sb("x1", [P, W, D])
        X2 = sb("x2", [P, NT, D])
        U = XU
        US = sb("u_clamped", [P, NT, D])
        UT = [sb(f"u_ff_t_{n}", [P, NT, 2, P], F32R) for n in ("high", "low")]
        HB = sb("hidden", [P, NT, FF])
        HTR = [sb(f"hidden_t_{n}", [P, 2, FF], F32R) for n in ("high", "low")]
        FO = sb("ff_out", [P, W, D])
        raw = FO[:].rearrange("p n d -> p (n d)")
        F1, F2 = raw[:, 0:2 * FF].rearrange("p (k n) -> p k n", k=2), raw[:, 2 * FF:].rearrange("p (k n) -> p k n", n=D)
        BS = sb("bn_ff", [P, W, 6])
        MV = sb("mean_var_ff", [P, 2, W])
        JKA = sb("junk_act_ff", [P, FF])
        JKV = sb("junk_dve_ff", [P, NT, D])
        PS = ctx.enter_context(nc.psum_tensor("ps_ff", [P, 8, 512], F32))

        loads = sem("loads_ff")
        dve_step, act_step, cols_ready, cols_done = sem("dve_step_f"), sem("act_step_f"), sem("cols_ready_f"), sem("cols_done_f")
        gained, dotted, scaled, moved, counted = (
            sem("gained"), sem("dotted"), sem("scaled"), sem("moved"), sem("counted"))
        centred, u_ready = sem("centred_f"), sem("u_ready_f")
        us_ready, us_turned, us_high, us_low = sem("us_ready"), sem("us_turned"), sem("us_high"), sem("us_low")
        u_clamp = sem("u_clamp")
        w_high, w_low, h_high, h_low = sem("w_high_f"), sem("w_low_f"), sem("h_high_f"), sem("h_low_f")
        h_mm, h_out, h_turned, ff_mm, ff_copied, ff_out = (
            sem("h_mm"), sem("h_out"), sem("h_turned"), sem("ff_mm"), sem("ff_copied"), sem("ff_out_f"))
        x_out, x_turned, x_copied = sem("x_out"), sem("x_turned"), sem("x_copied")

        def c(n):
            return C[:, n, :]

        def at(kind, n):
            return n

        def bank(n, a=0, z=512):
            return PS[:, n, a:z]

        with nc.Block() as block:
            @block.sync
            def _(sp):
                for dst, src in ((F1, w_f1), (F2, w_f2)):
                    sp.dma_start(dst, src.rearrange("(k p) n -> p k n", p=P)).then_inc(loads, 16)
                for dst, src in ((bias_f1, b_f1), (bias_f2, b_f2)):
                    n = src.shape[0]
                    sp.dma_start(dst[:], src.rearrange("(a n) -> a n", a=1).broadcast_to([P, n])).then_inc(loads, 16)

            @block.tensor
            def _(pe):
                def turn(i, src, ready, copied, turned, b0):
                    for j in range(NT):
                        pe.wait_ge(ready, i * NT + j + 1)
                        if j >= 2:
                            pe.wait_ge(copied, i * NT + j - 1)
                        for k in range(2):
                            mm = pe.transpose(bank(b0 + j % 2, k * P, k * P + P), src[:, j, k * P:k * P + P], ident[:])
                        mm.then_inc(turned, 1)

                pe.wait_ge(w_low, 2)
                with pe.Fori(0, B) as i:
                    turn(i, US, us_ready, us_low, us_turned, 6)
                    pe.wait_ge(ff_copied, i * NT + 1)

                    def turn_hidden(j):
                        pe.wait_ge(h_out, i * NT * 2 + 2 * (j + 1))
                        if j:
                            pe.wait_ge(h_low, i * NT + j)
                        for n in range(8):
                            mm = pe.transpose(bank(4 + n // 4, n % 4 * P, n % 4 * P + P), HB[:, j, n * P:n * P + P], ident[:])
                        mm.then_inc(h_turned, 1)

                    for j in range(NT):
                        pe.wait_ge(us_low, i * NT + j + 1)
                        if j >= 2:
                            pe.wait_ge(h_out, i * NT * 2 + 2 * (j - 1))
                        for n in range(2):
                            for k in range(2):
                                for wp, up in PRODUCTS:
                                    mm = pe.matmul(bank(2 * (j % 2) + n), UT[up][:, j, k, :], W1[wp][:, k, n * 512:n * 512 + 512],
                                                   start=(k == 0 and wp + up == 0), stop=(k == 1), skip_group_check=True)
                        mm.then_inc(h_mm, 1)
                        if j == 2:
                            turn_hidden(0)
                    for j in range(NT):
                        if j < NT - 1:
                            turn_hidden(j + 1)
                        pe.wait_ge(h_low, i * NT + j + 1)
                        for n in range(8):
                            for wp, hp in PRODUCTS:
                                mm = pe.matmul(bank(j, 0, D), HTR[hp][:, j % 2, n * P:n * P + P], W2[wp][:, n, :],
                                               start=(n == 0 and wp + hp == 0), stop=(n == 7), skip_group_check=True)
                        mm.then_inc(ff_mm, 1)
                pe.wait_ge(ff_copied, W + 1)
                with pe.Fori(0, B) as i:
                    turn(i, X2, x_out, x_copied, x_turned, 0)
                    pe.wait_ge(x_copied, (i + 1) * NT)

            @block.scalar
            def _(act):
                act.preload_act_table_set("natural_log_exp_and_others")
                arrive, rsqrt, count = scalar_columns(act, act_step, cols_ready, cols_done, at)

                def squares(i, j, rows, column, before):
                    act.wait_ge(squared, i * NT + j + before + 1)
                    act.activation(JKA[:, 0:rows.shape[-1]], rows, ACT.Square,
                                   accum_out=C[:, column, bass.ds(i * NT + j, 1)]).then_inc(squared, 1)

                def tiles(src, i, j):
                    return src[:, bass.ds(i * NT + j, 1), :].rearrange("p a d -> p (a d)")

                def copy_turned(i, j):
                    act.wait_ge(x_turned, i * NT + j + 1)
                    act.activation(XT[:, :, 0:XT_COLS].rearrange("p k (t b) -> p k t b", b=B)[:, :, j * P:j * P + P, bass.ds(i, 1)],
                                   bank(j % 2, 0, D).rearrange("p (k t a) -> p k t a", k=2, a=1), ACT.Copy).then_inc(x_copied, 1)

                def mobius(r, A, ready, before):
                    if r:
                        with act.Fori(0, B) as i:
                            for j in range(NT):
                                act.wait_ge(ready, i * NT + j + 1)
                                squares(i, j, tiles(A, i, j), 9, before)
                    rsqrt(c(10), c(9), c(20))
                    if r:
                        with act.Fori(0, B) as i:
                            for j in range(NT):
                                act.wait_ge(gained, i * NT + j + 1)
                                squares(i, j, tiles(A, i, j), 11, before + W)
                    rsqrt(c(13), c(12), c(20))
                    arrive()
                    act.activation(c(15), c(14), ACT.Tanh).then_inc(cols_done, 1)
                    act.preload_act_table_set("natural_log_exp_and_others")
                    arrive()
                    with act.Fori(0, B) as i:
                        for j in range(NT):
                            tile = bass.ds(i * NT + j, 1)
                            act.activation(A[:, tile, :], A[:, tile, :], ACT.Copy, scale=C[:, 5, tile]).then_inc(scaled, 1)

                mobius(0, XU, None, 0)
                act.wait_ge(loads, 64)
                for high, w in ((W1[0], F1), (W2[0], F2)):
                    act.activation(high[:], w, ACT.Copy).then_inc(w_high, 1)
                norm_scalars(act, arrive, rsqrt, cols_done, c)
                with act.Fori(0, B) as i:
                    for j in range(NT):
                        act.wait_ge(u_ready, i * NT + j + 1)
                        squares(i, j, tiles(U, i, j), 7, W)
                rsqrt(c(8), c(7), c(20))
                act.wait_ge(u_clamp, 1)
                with act.Fori(0, B) as i:
                    for j in range(NT):
                        tile = bass.ds(i * NT + j, 1)
                        act.activation(US[:, j:j + 1, :], U[:, tile, :], ACT.Copy, scale=C[:, 19, tile]).then_inc(us_ready, 1)
                    for j in range(NT):
                        act.wait_ge(us_turned, i * NT + j + 1)
                        act.activation(UT[0][:, j, :, :].rearrange("p k t -> p (k t)"), bank(6 + j % 2, 0, D), ACT.Copy).then_inc(us_high, 1)
                    for j in range(NT):
                        act.wait_ge(h_out, i * NT * 2 + 2 * (j + 1))
                        squares(i, j, HB[:, j, :], 7, 2 * W)
                        act.wait_ge(h_turned, i * NT + j + 1)
                        if j >= 2:
                            act.wait_ge(ff_mm, i * NT + j - 1)
                        act.activation(HTR[0][:, j % 2, :], PS[:, 4:6, :].rearrange("p a b -> p (a b)"), ACT.Copy).then_inc(h_high, 1)
                rsqrt(c(8), c(7), c(20))
                mobius(1, FO, ff_out, 3 * W)
                with act.Fori(0, B) as i:
                    for j in range(NT):
                        copy_turned(i, j)

            @block.vector
            def _(dve):
                columns = vector_columns(dve, dve_step, cols_ready, cols_done, at)
                link, ask, answered, newton, clamp, count = columns
                dve.sem_inc(ff_copied, 1)

                def mobius(r, A, src, gain, squared_before):
                    dve.wait_ge(squared, squared_before + W + 1)
                    clamp(c(9), c(10), c(10), c(16))
                    if r == 0:
                        link(dve.tensor_tensor(c(17), c(10), c(10), ALU.mult))
                        link(dve.tensor_tensor(c(11), c(11), c(17), ALU.mult))
                        link(dve.tensor_tensor(c(16), c(23), c(10), ALU.mult))
                    else:
                        with dve.Fori(0, B) as i:
                            for j in range(NT):
                                tile = bass.ds(i * NT + j, 1)
                                dve.scalar_tensor_tensor(A[:, tile, :], A[:, tile, :], C[:, 10, tile], ada[:, bass.ds(i, 1), gain, :],
                                                         ALU.mult, ALU.mult).then_inc(gained, 1)
                            for j in range(NT):
                                tile = bass.ds(i * NT + j, 1)
                                dve.wait_ge(gained, i * NT + j + 1)
                                dve.scalar_tensor_tensor(JKV[:, j:j + 1, :], src[:, tile, :], 1.0, A[:, tile, :], ALU.mult, ALU.mult,
                                                         accum_out=C[:, 16, tile]).then_inc(dotted, 1)
                            dve.wait_ge(dotted, (i + 1) * NT)
                        dve.wait_ge(squared, squared_before + 2 * W + 1)
                    ask(dve.tensor_scalar(c(12), c(11), EPS2, None, ALU.max))
                    newton(c(13), c(12), c(17))
                    ask(dve.tensor_tensor(c(14), c(12), c(13), ALU.mult))
                    answered()
                    link(dve.tensor_tensor(c(17), c(15), c(13), ALU.mult))
                    link(dve.tensor_tensor(c(18), c(17), c(17), ALU.mult))
                    link(dve.tensor_tensor(c(18), c(18), c(11), ALU.mult))
                    link(dve.tensor_tensor(c(19), c(17), c(16), ALU.mult))
                    link(dve.tensor_scalar(c(19), c(19), 2.0, 1.0, ALU.mult, ALU.add))
                    link(dve.tensor_tensor(c(2), c(19), c(18), ALU.add))
                    link(dve.tensor_tensor(c(3), c(22), c(18), ALU.mult))
                    link(dve.tensor_tensor(c(3), c(3), c(19), ALU.add))
                    link(dve.tensor_scalar(c(3), c(3), EPS, None, ALU.max))
                    link(dve.reciprocal(c(3), c(3)))
                    link(dve.tensor_tensor(c(4), c(2), c(3), ALU.mult))
                    link(dve.tensor_scalar(c(5), c(22), -1.0, 1.0, ALU.mult, ALU.add))
                    link(dve.tensor_tensor(c(5), c(5), c(3), ALU.mult))
                    if r == 0:
                        link(dve.tensor_tensor(c(5), c(5), c(10), ALU.mult))
                    ask(dve.tensor_tensor(c(5), c(5), c(17), ALU.mult))

                def move(r, i, j, A, src, out):
                    tile = bass.ds(i * NT + j, 1)
                    dve.wait_ge(scaled, i * NT + j + r * W + 1)
                    dve.scalar_tensor_tensor(out(tile, j), src[:, tile, :], C[:, 4, tile], A[:, tile, :],
                                             ALU.mult, ALU.add).then_inc(moved, 1)

                mobius(0, XU, X, 2, 0)
                with dve.Fori(0, B) as i:
                    for j in range(NT):
                        move(0, i, j, XU, X, lambda tile, j: X1[:, tile, :])
                    for j in range(NT):
                        dve.wait_ge(moved, i * NT + j + 1)
                        dve.bn_stats(BS[:, bass.ds(i * NT + j, 1), :].rearrange("p a s -> p (a s)"),
                                     X1[:, bass.ds(i * NT + j, 1), :].rearrange("p a d -> p (a d)")).then_inc(counted, 1)
                dve.wait_ge(counted, W)
                norm_columns(dve, columns, c, BS, MV)
                with dve.Fori(0, B) as i:
                    for j in range(NT):
                        tile = bass.ds(i * NT + j, 1)
                        dve.scalar_tensor_tensor(U[:, tile, :], X1[:, tile, :], MV[:, 0, tile], ada[:, bass.ds(i, 1), 4, :],
                                                 ALU.subtract, ALU.mult).then_inc(centred, 1)
                    for j in range(NT):
                        tile = bass.ds(i * NT + j, 1)
                        dve.wait_ge(centred, i * NT + j + 1)
                        dve.scalar_tensor_tensor(U[:, tile, :], U[:, tile, :], C[:, 18, tile], ada[:, bass.ds(i, 1), 3, :],
                                                 ALU.mult, ALU.add).then_inc(u_ready, 1)
                dve.wait_ge(squared, 2 * W + 1)
                clamp(c(7), c(8), c(19), c(16))
                dve.sem_inc(u_clamp, 1)
                dve.wait_ge(loads, 64)
                with dve.Fori(0, B) as i:
                    for j in range(NT):
                        dve.wait_ge(us_high, i * NT + j + 1)
                        low = UT[1][:, j, :, :].rearrange("p k t -> p (k t)")
                        high = UT[0][:, j, :, :].rearrange("p k t -> p (k t)").bitcast(F32)
                        dve.tensor_tensor(low, bank(6 + j % 2, 0, D), high, ALU.subtract).then_inc(us_low, 1)

                    def add_bias(j):
                        dve.wait_ge(h_mm, i * NT + j + 1)
                        for n in range(2):
                            dve.tensor_tensor(HB[:, j, n * 512:n * 512 + 512], bank(2 * (j % 2) + n),
                                              bias_f1[:, n * 512:n * 512 + 512], ALU.add).then_inc(h_out, 1)

                    def copy_out(j):
                        dve.wait_ge(ff_mm, i * NT + j + 1)
                        dve.tensor_copy(FO[:, bass.ds(i * NT + j, 1), :], PS[:, j:j + 1, 0:D]).then_inc(ff_copied, 1)

                    for j in range(NT - 1):
                        add_bias(j)
                    for j in range(NT):
                        dve.wait_ge(h_high, i * NT + j + 1)
                        dve.tensor_tensor(HTR[1][:, j % 2, :], PS[:, 4:6, :].rearrange("p a b -> p (a b)"),
                                          HTR[0][:, j % 2, :].bitcast(F32), ALU.subtract).then_inc(h_low, 1)
                        if j == 0:
                            add_bias(NT - 1)
                        else:
                            copy_out(j - 1)
                    copy_out(NT - 1)
                    dve.wait_ge(squared, (i + 1) * NT + 2 * W + 1)
                clamp(c(7), c(8), c(19), c(16))
                dve.wait_ge(ff_copied, W + 1)
                with dve.Fori(0, B) as i:
                    for j in range(NT):
                        tile = bass.ds(i * NT + j, 1)
                        dve.scalar_tensor_tensor(FO[:, tile, :], FO[:, tile, :], C[:, 19, tile], bias_f2[:].unsqueeze(1),
                                                 ALU.mult, ALU.add).then_inc(ff_out, 1)
                mobius(1, FO, X1, 5, 3 * W)
                dve.memset(XT[:, :, XT_COLS:], 0.0)
                with dve.Fori(0, B) as i:
                    def add_input(j):
                        dve.wait_ge(moved, i * NT + j + W + 1)
                        dve.tensor_tensor(X2[:, j:j + 1, :], X2[:, j:j + 1, :], X[:, bass.ds(i * NT + j, 1), :], ALU.add).then_inc(x_out, 1)

                    for j in range(NT):
                        move(1, i, j, FO, X1, lambda tile, j: X2[:, j:j + 1, :])
                        if j:
                            add_input(j - 1)
                    add_input(NT - 1)
                    dve.wait_ge(x_turned, (i + 1) * NT)

            @block.gpsimd
            def _(pool):
                for n, (w, (high, low)) in enumerate(((F1, W1), (F2, W2))):
                    pool.wait_ge(w_high, n + 1)
                    pool.tensor_tensor(low[:], w, high[:].bitcast(F32), ALU.subtract).then_inc(w_low, 1)


def hyperbolic_block(nc, x, cond_t, w_qkv, b_qkv, w_o, b_o, w_f1, b_f1, w_f2, b_f2, w_ada, b_ada, XT, ident, ident_bf):
    with ExitStack() as held:
        def sb(name, shape):
            return held.enter_context(nc.sbuf_tensor(name, shape, F32))

        X = sb("x_tokens", [P, B * NT, D])
        ada = sb("ada", [P, B, 6, D])
        C = sb("cols", [P, 24, B * NT])
        squared = held.enter_context(nc.semaphore("squared"))
        XU = XT[:].rearrange("p k n -> p (k n)")[:, 0:B * NT * D].rearrange("p (n d) -> p n d", d=D)
        with nc.sbuf_tensor("qkv", [P, B * NT, 3 * H, HD], F32) as QKV, nc.sbuf_tensor("head_factor", [P, B * NT, 3 * H], F32) as HF:
            project_to_heads(nc, x, cond_t, w_qkv, b_qkv, w_ada, b_ada, ada, X, QKV, HF, C, ident)
            attend(nc, w_o, b_o, ada, X, QKV, HF, C, XU, ident, ident_bf, squared)
        feed_forward(nc, w_f1, b_f1, w_f2, b_f2, ada, X, C, XU, XT, ident, squared)


def gru(nc, w_x, u_h, c_v, b_v, cond_t, XT, ident_bf, w_next, next_parts, ident):
    NEXT = L2_COLS // (S // (2 * CH))
    with ExitStack() as ctx:
        def sb(name, shape, dt=F32):
            return ctx.enter_context(nc.sbuf_tensor(name, shape, dt))

        def sem(name):
            return ctx.enter_context(nc.semaphore(name))

        Wf = sb("w_x_sb", [P, 2, 3 * D])
        Wx = sb("w_x_parts", [P, 3, 2, 3 * D], BF16)
        XP = sb("x_parts", [P, 3, 2, CH * B], BF16)
        XR = sb("x_rest", [P, 2, CH * B])
        Uf = sb("u_h_sb", [P, 2, 3 * D])
        U = sb("u_parts", [P, 2, 2, 3 * D], F16)
        largest = sb("largest", [P, 3])
        row = sb("largest_row", [1, 2 * P])
        ones = sb("ones_row", [1, P])
        scales = sb("scales", [P, 4])
        Cv = sb("c_v_sb", [P, 2, 3 * D])
        cond = sb("cond_v", [P, 2, B])
        bias = sb("gru_bias", [B, 3 * D])
        V = sb("v_sum", [B, 3 * D])
        V1 = sb("v_parts", [B, 3, 3 * D], BF16)
        pick = sb("pick_batch", [B, CH, B], BF16)
        HS = sb("states", [P, 2 * CH + 1, 2 * B * 2])
        KP = sb("kept_parts", [P, 2, 2, B], F16)
        ZP = sb("fresh_parts", [P, 2, 2, B], F16)
        ZN = sb("fresh", [P, 2, B])
        ZS = sb("scan_factors", [P, 2 * B * 2])
        NK = sb("scan_terms", [P, 2 * B * 2])
        RP = sb("reset_parts", [P, 2, 2, B], F16)
        RH = sb("reset_state", [P, 2, B])
        G = sb("gates", [P, 2, 2, B])
        ZH = sb("z_state", [P, 2, B])
        WN = sb("next_weights", [P, 2, NEXT // 2])
        PS = ctx.enter_context(nc.psum_tensor("gate_sums", [P, 2, 3, 512], F32))

        w_in, c_in = sem("gru_weights"), sem("gru_c")
        u_in, u_scale, u_part, w_part = sem("u_weights_in"), sem("u_scale"), sem("u_part"), sem("w_part")
        largest_ready, largest_mm = sem("largest_ready"), sem("largest_mm")
        prep, v_mm, v_ready = sem("gru_prep"), sem("v_mm"), sem("v_ready")
        r_mm, z_mm, n_mm = sem("r_mm"), sem("z_mm"), sem("n_mm")
        r_ready, z_ready, n_ready = sem("r_ready"), sem("z_ready"), sem("n_ready")
        ra_ready, rh_ready, rb_ready = sem("ra_ready"), sem("rh_ready"), sem("rb_ready")
        zh_ready, zs_ready, keep_ready = sem("zh_ready"), sem("zs_ready"), sem("keep_ready")
        ka_ready, kb_ready, za_ready, zn_ready, zb_ready = (
            sem("ka_ready"), sem("kb_ready"), sem("za_ready"), sem("zn_ready"), sem("zb_ready"))
        h_ready = sem("h_ready")
        x_added, x_split = sem("x_added"), sem("x_split")
        next_in, next_split = [sem("next_in_0"), sem("next_in_1")], sem("next_split")
        N = 2 * CH
        SUMS, SMALL, LARGE = 2.0 ** 6, 2.0 ** 3, 2.0 ** 14
        EXPONENT = 0x7F800000

        def pairs(ap, n):
            return ap.rearrange("p (k b n) -> p k b n", b=B, n=2)[:, :, :, n]

        def gate(half, g):
            return PS[:, half, g, 0:CH * 2 * B].rearrange("p (t m b) -> p t m b", m=2, b=B)

        with nc.Block() as block:
            @block.sync
            def _(sp):
                sp.dma_start(Uf[:], u_h.rearrange("(k p) n -> p k n", p=P)).then_inc(u_in, 16)
                sp.dma_start(Cv[:], c_v.rearrange("(k p) n -> p k n", p=P)).then_inc(c_in, 16)
                sp.dma_start(cond[:], cond_t.rearrange("(k p) b -> p k b", p=P)).then_inc(c_in, 16)
                sp.dma_start(bias[:], b_v.rearrange("(a n) -> a n", a=1).broadcast_to([B, 3 * D])).then_inc(c_in, 16)
                sp.dma_start(Wf[:], w_x.rearrange("(k p) n -> p k n", p=P)).then_inc(w_in, 16)
                for half in range(2):
                    sp.dma_start(WN[:, half, :], w_next[:, half * NEXT // 2:(half + 1) * NEXT // 2]).then_inc(next_in[half], 16)
                with sp.Fori(0, S // N - 1) as i:
                    for half in range(2):
                        sp.wait_ge(next_split, i * 8 + half * 4 + 4)
                        sp.dma_start(WN[:, half, :], w_next[:, bass.ds(i * NEXT + NEXT + half * NEXT // 2, NEXT // 2)]
                                     ).then_inc(next_in[half], 16)

            @block.tensor
            def _(pe):
                pe.wait_ge(c_in, 48)
                for n, (a, z) in enumerate(((0, 512), (512, 768))):
                    for k in range(2):
                        mm = pe.matmul(PS[0:B, 0, n, 0:z - a], cond[:, k, :], Cv[:, k, a:z], start=(k == 0), stop=(k == 1))
                mm.then_inc(v_mm, 1)
                pe.wait_ge(largest_ready, 1)
                pe.transpose(PS[0:1, 0, 2, 0:P], largest[:, 2:3], ident[:]).then_inc(largest_mm, 1)
                pe.wait_ge(largest_ready, 2)
                pe.matmul(PS[:, 1, 0, 0:1], ones[:], row[:, P:P + 1], start=True, stop=True).then_inc(largest_mm, 1)
                pe.wait_ge(v_ready, 6)

                def project_condition(half, g):
                    for m in range(2):
                        for part in range(3):
                            pe.matmul(gate(half, g)[:, :, m, :], V1[:, part, g * D + m * P:g * D + m * P + P], pick[:],
                                      start=(m == 0 and part == 0), stop=False, skip_group_check=True)

                def project(half, g, m, k):
                    w = slice(g * D + m * P, g * D + m * P + P)
                    for wp, xp in ((0, 0), (0, 1), (1, 0), (1, 1), (0, 2), (2, 0)):
                        pe.matmul(gate(half, g)[:, :, m, :], Wx[:, wp, k, w], XP[:, xp, k, :].rearrange("p (t b) -> p t b", b=B),
                                  start=False, stop=False, skip_group_check=True)

                PIECES = [(g, m, k) for g in (1, 0, 2) for m in range(2) for k in range(2)]
                FIRST = CH - len(PIECES)
                for g in range(3):
                    project_condition(0, g)
                pe.wait_ge(x_split, 4)
                for piece in PIECES:
                    project(0, *piece)

                def share(out, g, value, last=False):
                    parts, part = value
                    for m in range(2):
                        w = slice(g * D + m * P, g * D + m * P + P)
                        for k in range(2):
                            for u in range(2 - part):
                                mm = pe.matmul(out[:, m, :], U[:, u, k, w], parts[:, part, k, :],
                                               start=False, stop=last, skip_group_check=True)
                    return mm

                with pe.Fori(0, S // N) as i:
                    for s in range(N):
                        half, t = s // CH, s % CH
                        at = i * N + s + 1
                        z_out, r_out, n_out = (gate(half, g)[:, t, :, :] for g in range(3))
                        pe.wait_ge(ka_ready, at)
                        share(r_out, 1, (KP, 0))
                        pe.wait_ge(za_ready, at)
                        share(r_out, 1, (ZP, 0))
                        pe.wait_ge(kb_ready, at)
                        share(r_out, 1, (KP, 1))
                        pe.wait_ge(zb_ready, at)
                        share(r_out, 1, (ZP, 1), True).then_inc(r_mm, 1)
                        for value in ((KP, 0), (ZP, 0), (KP, 1)):
                            share(z_out, 0, value)
                        share(z_out, 0, (ZP, 1), True).then_inc(z_mm, 1)
                        pe.wait_ge(ra_ready, at)
                        share(n_out, 2, (RP, 0))
                        pe.wait_ge(rb_ready, at)
                        share(n_out, 2, (RP, 1), True).then_inc(n_mm, 1)
                        if 1 <= t <= 3:
                            project_condition(1 - half, t - 1)
                        if t == FIRST:
                            pe.wait_ge(x_split, i * 8 + half * 4 + 8)
                        if t >= FIRST:
                            project(1 - half, *PIECES[t - FIRST])

            @block.scalar
            def _(act):
                act.preload_act_table_set("sigmoid_and_others")
                act.wait_ge(w_in, 16)
                act.activation(Wx[:, 0, :, :], Wf[:], ACT.Copy, scale=SUMS).then_inc(w_part, 1)
                act.wait_ge(u_scale, 1)
                act.activation(U[:, 0, :, :], Uf[:], ACT.Copy, scale=scales[:, 1:2]).then_inc(u_part, 1)
                act.wait_ge(w_part, 2)
                act.activation(Wx[:, 1, :, :], Wf[:], ACT.Copy).then_inc(w_part, 1)
                with act.Fori(0, S // N) as i:
                    for s in range(N):
                        half, t = s // CH, s % CH
                        act.wait_ge(r_mm, i * N + s + 1)
                        act.activation(G[:, 1, :, :], gate(half, 1)[:, t, :, :], ACT.Sigmoid, scale=1.0 / SUMS).then_inc(r_ready, 1)
                        act.wait_ge(z_mm, i * N + s + 1)
                        act.activation(G[:, 0, :, :], gate(half, 0)[:, t, :, :], ACT.Sigmoid, scale=1.0 / SUMS).then_inc(z_ready, 1)
                        act.wait_ge(n_mm, i * N + s + 1)
                        act.activation(pairs(NK[:], 0), gate(half, 2)[:, t, :, :], ACT.Tanh, scale=1.0 / SUMS).then_inc(n_ready, 1)

            @block.vector
            def _(dve):
                dve.memset(HS[:, 0, :], 0.0).then_inc(h_ready, 1)
                dve.memset(KP[:], 0.0).then_inc(ka_ready, 1)
                dve.memset(ZP[:], 0.0).then_inc(za_ready, 1)
                dve.memset(NK[:], 0.0)
                dve.memset(ZS[:], 0.0).then_inc(prep, 1)
                dve.sem_inc(kb_ready, 1)
                dve.sem_inc(zb_ready, 1)
                dve.tensor_copy(pick[:], ident_bf[0:B, 0:B].unsqueeze(1).broadcast_to([B, CH, B])).then_inc(v_ready, 1)
                dve.wait_ge(u_in, 16)
                count = [1]

                def link(ins):
                    count[0] += 1
                    ins.then_inc(prep, 1)
                    dve.wait_ge(prep, count[0])

                dve.tensor_reduce(largest[:, 0:1], Uf[:].rearrange("p k n -> p (k n)"), AX.X, ALU.max)
                link(dve.tensor_reduce(largest[:, 1:2], Uf[:].rearrange("p k n -> p (k n)"), AX.X, ALU.min))
                link(dve.tensor_scalar(largest[:, 1:2], largest[:, 1:2], -1.0, None, ALU.mult))
                dve.tensor_tensor(largest[:, 2:3], largest[:, 0:1], largest[:, 1:2], ALU.max).then_inc(largest_ready, 1)
                link(dve.memset(ones[:], 1.0))
                dve.wait_ge(largest_mm, 1)
                link(dve.tensor_reduce(row[:, P:P + 1], PS[0:1, 0, 2, 0:P], AX.X, ALU.max))
                dve.tensor_scalar(row[:, P:P + 1], row[:, P:P + 1], 2.0 ** -6, 2.0 ** 23, ALU.max, ALU.min
                                  ).then_inc(largest_ready, 1)
                dve.wait_ge(largest_mm, 2)
                power, factor_u, factor_h, undo = (scales[:, n:n + 1] for n in range(4))
                link(dve.tensor_copy(power, PS[:, 1, 0, 0:1]))
                link(dve.tensor_scalar(power.bitcast(I32), power.bitcast(I32), EXPONENT, None, ALU.bitwise_and))
                link(dve.reciprocal(factor_u, power))
                link(dve.tensor_scalar(factor_u, factor_u, 1.0 + 2.0 ** -10, None, ALU.mult))
                link(dve.tensor_scalar(factor_u.bitcast(I32), factor_u.bitcast(I32), EXPONENT, None, ALU.bitwise_and))
                link(dve.tensor_scalar(factor_u, factor_u, LARGE, SMALL, ALU.mult, ALU.min))
                dve.sem_inc(u_scale, 1)
                link(dve.tensor_scalar(factor_h, power, 1.0 / LARGE, 1.0 / SMALL, ALU.mult, ALU.max))
                link(dve.tensor_scalar(factor_h, factor_h, SUMS, None, ALU.mult))
                link(dve.tensor_scalar(undo, factor_u, 1.0 / SUMS, None, ALU.mult))
                dve.wait_ge(w_part, 1)
                dve.scalar_tensor_tensor(Wf[:], Wf[:], SUMS, Wx[:, 0, :, :], ALU.mult, ALU.subtract).then_inc(w_part, 1)
                dve.wait_ge(u_part, 1)
                dve.scalar_tensor_tensor(U[:, 1, :, :], Uf[:], factor_u, U[:, 0, :, :], ALU.mult, ALU.subtract).then_inc(v_ready, 1)
                dve.wait_ge(v_mm, 1)
                dve.tensor_tensor(V[:, 0:512], PS[0:B, 0, 0, :], bias[:, 0:512], ALU.add)
                link(dve.tensor_tensor(V[:, 512:768], PS[0:B, 0, 1, 0:256], bias[:, 512:768], ALU.add))
                link(dve.tensor_scalar(V[:], V[:], SUMS, None, ALU.mult))
                dve.tensor_copy(V1[:, 0, :], V[:]).then_inc(v_ready, 1)
                dve.wait_ge(v_ready, 3)
                link(dve.tensor_tensor(V[:], V[:], V1[:, 0, :], ALU.subtract))
                dve.tensor_copy(V1[:, 1, :], V[:]).then_inc(v_ready, 1)
                dve.wait_ge(v_ready, 4)
                dve.tensor_tensor(V1[:, 2, :], V[:], V1[:, 1, :], ALU.subtract).then_inc(v_ready, 1)

                dve.wait_ge(w_part, 3)
                dve.tensor_tensor(Wx[:, 2, :, :], Wf[:], Wx[:, 1, :, :], ALU.subtract).then_inc(v_ready, 1)

                def split_x(n, at, done):
                    xs = XT[:, :, bass.ds(at, CH * B)]
                    if n:
                        dve.wait_ge(x_split, done + n)
                    if n == 0:
                        ins = dve.tensor_copy(XP[:, 0, :, :], xs)
                    elif n == 1:
                        ins = dve.tensor_tensor(XR[:], xs, XP[:, 0, :, :], ALU.subtract)
                    elif n == 2:
                        ins = dve.tensor_copy(XP[:, 1, :, :], XR[:])
                    else:
                        ins = dve.tensor_tensor(XP[:, 2, :, :], XR[:], XP[:, 1, :, :], ALU.subtract)
                    ins.then_inc(x_split, 1)

                for n in range(4):
                    split_x(n, 0, 0)

                def split_next(n):
                    half, piece, low = n // 4, n // 2 % 2, n % 2
                    a = piece * NEXT // 4
                    src = WN[:, half, a:a + NEXT // 4]
                    high, rest = (w[:, bass.ds(i * NEXT + half * NEXT // 2 + a, NEXT // 4)] for w in next_parts)
                    if low:
                        dve.wait_ge(next_split, i * 8 + n)
                        dve.tensor_tensor(rest, src, high.bitcast(F32), ALU.subtract).then_inc(next_split, 1)
                    else:
                        if piece == 0:
                            dve.wait_ge(next_in[half], i * 16 + 16)
                        dve.tensor_copy(high, src).then_inc(next_split, 1)

                with dve.Fori(0, S // N) as i:
                    for s in range(N):
                        at = i * N + s + 1
                        old, new = pairs(HS[:, s, :], 1), HS[:, s + 1, :]
                        dve.wait_ge(r_ready, at)
                        dve.wait_ge(h_ready, at)
                        dve.tensor_tensor(RP[:, 0, :, :], G[:, 1, :, :], old, ALU.mult).then_inc(ra_ready, 1)
                        dve.tensor_tensor(RH[:], G[:, 1, :, :], old, ALU.mult).then_inc(rh_ready, 1)
                        dve.wait_ge(rh_ready, at)
                        dve.tensor_tensor(RP[:, 1, :, :], RH[:], RP[:, 0, :, :], ALU.subtract).then_inc(rb_ready, 1)
                        dve.wait_ge(z_ready, at)
                        dve.tensor_tensor(ZH[:], G[:, 0, :, :], old, ALU.mult).then_inc(zh_ready, 1)
                        dve.tensor_scalar(pairs(ZS[:], 1), G[:, 0, :, :], factor_h, None, ALU.mult).then_inc(zs_ready, 1)
                        dve.wait_ge(zh_ready, at)
                        dve.tensor_tensor(KP[:, 0, :, :], old, ZH[:], ALU.subtract).then_inc(ka_ready, 1)
                        dve.wait_ge(zs_ready, at)
                        dve.tensor_tensor(pairs(NK[:], 1), old, ZH[:], ALU.subtract).then_inc(keep_ready, 1)
                        dve.wait_ge(n_ready, at)
                        dve.tensor_tensor(ZP[:, 0, :, :], pairs(ZS[:], 1), pairs(NK[:], 0), ALU.mult).then_inc(za_ready, 1)
                        dve.tensor_tensor(ZN[:], pairs(ZS[:], 1), pairs(NK[:], 0), ALU.mult).then_inc(zn_ready, 1)
                        dve.wait_ge(keep_ready, at)
                        dve.tensor_tensor(KP[:, 1, :, :], pairs(NK[:], 1), KP[:, 0, :, :], ALU.subtract).then_inc(kb_ready, 1)
                        dve.wait_ge(zn_ready, at)
                        dve.tensor_tensor(ZP[:, 1, :, :], ZN[:], ZP[:, 0, :, :], ALU.subtract).then_inc(zb_ready, 1)
                        dve.tensor_tensor_scan(new, ZS[:], NK[:], 0.0, ALU.mult, ALU.add).then_inc(h_ready, 1)
                        if s % CH < 4:
                            split_x(s % CH, (i * N + (s // CH + 1) * CH) * B, i * 8 + s // CH * 4 + 4)
                        elif s % CH % 2 == 0 and s % CH < 12:
                            split_next(s // CH * 4 + (s % CH - 4) // 2)
                    dve.wait_ge(h_ready, (i + 1) * N + 1)
                    dve.tensor_copy(HS[:, 0, :], HS[:, N, :]).then_inc(x_added, 1)
                    xs = XT[:, :, bass.ds(i * N * B, N * B)]
                    for k in range(2):
                        states = HS[:, 1:N + 1, :].rearrange("p t (k b n) -> p k t b n", b=B, n=2)[:, k, :, :, 1]
                        dve.scalar_tensor_tensor(xs[:, k, :].rearrange("p (t b) -> p t b", b=B), states, undo,
                                                 xs[:, k, :].rearrange("p (t b) -> p t b", b=B),
                                                 ALU.mult, ALU.add).then_inc(x_added, 1)
                    dve.wait_ge(x_added, i * 3 + 3)
                dve.wait_ge(next_split, S // N * 8)


def top_two(dve, link, scores, picked, t, m, rank, shape):
    def over(v):
        return v.unsqueeze(len(shape) - 1).broadcast_to(shape)

    one = t[1]
    for n in range(2):
        link(dve.tensor_reduce(m, scores, AX.X, ALU.max))
        link(dve.tensor_tensor(t[0], scores, over(m), ALU.is_equal))
        link(dve.tensor_tensor(t[0], t[0], rank, ALU.mult))
        link(dve.tensor_reduce(m, t[0], AX.X, ALU.max))
        link(dve.tensor_tensor(one, t[0], over(m), ALU.is_equal))
        if n == 0:
            link(dve.tensor_copy(picked, one))
            link(dve.scalar_tensor_tensor(scores, one, -1e30, scores, ALU.mult, ALU.add))
        else:
            link(dve.tensor_tensor(picked, picked, one, ALU.add))


def shared_and_routed(nc, w_router, router_bias, W, cond_t, XT, ident):
    NS, NE, HS_T, HR_T = N_SHARED, N_ROUTED, HID_S // P, HID_R // P
    SW1, SW3, SW2, RW1, RW2 = ([parts_of(w, n) for w in W] for n in range(5))
    T = XT_COLS // P
    with ExitStack() as ctx:
        def sb(name, shape, dt=F32):
            return ctx.enter_context(nc.sbuf_tensor(name, shape, dt))

        def sem(name):
            return ctx.enter_context(nc.semaphore(name))

        XP = [sb(f"x_part_{n}", [P, 2, XT_COLS], F32R) for n in range(2)]
        WR = sb("w_router_sb", [P, 4, NE])
        cond = sb("cond_r", [P, 2, B])
        cond_rep = sb("cond_cols", [P, 2, P])
        bias = sb("router_bias_sb", [P, NE])
        rank = sb("rank", [P, NE])
        SIG = sb("router_scores", [P, T, NE])
        SEL = sb("selection", [P, T, NE])
        BOTH = sb("picked_two", [P, T, NE])
        T0 = sb("router_t0", [P, T, NE])
        T1 = sb("router_t1", [P, T, NE])
        M = sb("router_m", [P, 3, T])
        CL = sb("cond_logits", [P, NE])
        GT = sb("gates_t", [NE, XT_COLS])
        pick = sb("pick_expert", [NE, NE, P])
        A1 = sb("activated", [P, 2, 512])
        HB = sb("hidden_2", [P, 2, 512])
        HP = [sb(f"hidden_part_{n}", [P, 3, 512], F32R) for n in range(2)]
        PS = ctx.enter_context(nc.psum_tensor("ps2", [P, 8, 512], F32))
        OUT, PAIR, GATE = 0, 2, 6

        r_in, x_split, h_full, h_high = sem("router_in"), sem("x_split_2"), sem("h_full"), sem("h_high")
        step, rows_ready, logit_mm, scored = sem("router_step"), sem("rows_ready"), sem("logit_mm"), sem("scored")
        gates_ready, gates_turned, gates_copied = sem("gates_ready"), sem("gates_turned"), sem("gates_copied")
        first_mm, gate_mm, activated, h_ready, second_mm, added = (
            sem("first_mm"), sem("gate_mm"), sem("activated"), sem("hidden_ready"), sem("second_mm"), sem("added"))

        units = [("s", e, m) for e in range(NS) for m in range(HS_T)] + [("r", e, m) for e in range(NE) for m in range(HR_T)]
        NU = len(units)

        with nc.Block() as block:
            @block.sync
            def _(sp):
                sp.dma_start(WR[:], w_router.rearrange("(k p) n -> p k n", p=P)).then_inc(r_in, 16)
                sp.dma_start(cond[:], cond_t.rearrange("(k p) b -> p k b", p=P)).then_inc(r_in, 16)
                sp.dma_start(bias[:], router_bias.rearrange("(a n) -> a n", a=1).broadcast_to([P, NE])).then_inc(r_in, 16)

            @block.tensor
            def _(pe):
                pe.wait_ge(r_in, 48)
                pe.wait_ge(rows_ready, 1)
                for k in range(2):
                    pe.matmul(PS[:, 1, 0:NE], cond_rep[:, k, :], WR[:, 2 + k, :], start=(k == 0), stop=(k == 1))
                for t in range(T):
                    for k in range(2):
                        mm = pe.matmul(PS[:, 0, t * NE:t * NE + NE], XT[:, k, t * P:t * P + P], WR[:, k, :],
                                       start=(k == 0), stop=(k == 1), skip_group_check=True)
                mm.then_inc(logit_mm, 1)
                pe.wait_ge(gates_ready, 1)
                for t in range(T):
                    mm = pe.transpose(PS[0:NE, 2 + t // 4, t % 4 * P:t % 4 * P + P], BOTH[:, t, :], ident[:])
                mm.then_inc(gates_turned, 1)
                pe.wait_ge(gates_copied, 1)
                pe.wait_ge(x_split, 2)
                with pe.Fori(0, XT_COLS // 512) as i:
                    def second(u):
                        kind, e, m = units[u]
                        w = SW2 if kind == "s" else RW2
                        pe.wait_ge(h_ready, i * NU + u + 1)
                        for f in range(2):
                            for wp, hp in PRODUCTS:
                                mm = pe.matmul(PS[:, OUT + f, :], w[wp][:, e, m, f * P:f * P + P], HP[hp][:, u % 3, :],
                                               start=(u == 0 and wp + hp == 0), stop=(u == NU - 1), skip_group_check=True)
                        mm.then_inc(second_mm, 1)

                    for u, (kind, e, m) in enumerate(units):
                        if u >= 2:
                            pe.wait_ge(h_full, i * NU + u - 1)
                        pair = PAIR + 2 * (u % 2)
                        for n, w in enumerate((SW1, SW3) if kind == "s" else (RW1,)):
                            for k in range(2):
                                for wp, xp in PRODUCTS:
                                    mm = pe.matmul(PS[:, pair + n, :], w[wp][:, e, k, m * P:m * P + P],
                                                   XP[xp][:, k, bass.ds(i * 512, 512)], start=(k == 0 and wp + xp == 0),
                                                   stop=(k == 1), skip_group_check=True)
                        mm.then_inc(first_mm, 1)
                        if kind == "r" and m == 0:
                            pe.matmul(PS[:, GATE + e % 2, :], pick[:, e, :], GT[:, bass.ds(i * 512, 512)],
                                      start=True, stop=True).then_inc(gate_mm, 1)
                        if u == 1:
                            pe.wait_ge(added, 2 * i + 1)
                        if u:
                            second(u - 1)
                    second(NU - 1)

            @block.scalar
            def _(act):
                act.wait_ge(logit_mm, 1)
                act.wait_ge(rows_ready, 2)
                act.activation(SIG[:], SEL[:], ACT.Sigmoid).then_inc(scored, 1)
                with act.Fori(0, XT_COLS // 512) as i:
                    for u, (kind, e, m) in enumerate(units):
                        act.wait_ge(first_mm, i * NU + u + 1)
                        if u >= 2:
                            act.wait_ge(h_full, i * NU + u - 1)
                        act.activation(A1[:, u % 2, :], PS[:, PAIR + 2 * (u % 2), :],
                                       ACT.Silu if kind == "s" else ACT.Gelu).then_inc(activated, 1)

            @block.vector
            def _(dve):
                count = [0]

                def link(ins):
                    count[0] += 1
                    ins.then_inc(step, 1)
                    dve.wait_ge(step, count[0])

                for e in range(NE):
                    dve.memset(rank[:, e:e + 1], float(NE - e))
                link(dve.tensor_copy(pick[:], ident[0:NE, 0:NE].unsqueeze(2).broadcast_to([NE, NE, P])))
                dve.wait_ge(r_in, 48)
                dve.tensor_copy(cond_rep[:].rearrange("p k (t b) -> p k t b", b=B),
                                cond[:].unsqueeze(2).broadcast_to([P, 2, P // B, B])).then_inc(rows_ready, 1)
                dve.tensor_copy(XP[0][:], XT[:, :, 0:XT_COLS]).then_inc(x_split, 1)
                dve.wait_ge(x_split, 1)
                dve.tensor_tensor(XP[1][:], XT[:, :, 0:XT_COLS], XP[0][:].bitcast(F32), ALU.subtract).then_inc(x_split, 1)
                dve.wait_ge(logit_mm, 1)
                link(dve.tensor_copy(CL[:], PS[:, 1, 0:NE]))
                dve.tensor_tensor(SEL[:], PS[:, 0, 0:T * NE].rearrange("p (t e) -> p t e", e=NE),
                                  CL[:].unsqueeze(1).broadcast_to([P, T, NE]), ALU.add).then_inc(rows_ready, 1)
                dve.wait_ge(scored, 1)
                link(dve.tensor_tensor(SEL[:], SIG[:], bias[:].unsqueeze(1).broadcast_to([P, T, NE]), ALU.add))
                top_two(dve, link, SEL[:], BOTH[:], (T0[:], T1[:]), M[:, 0, :],
                        rank[:].unsqueeze(1).broadcast_to([P, T, NE]), [P, T, NE])
                link(dve.tensor_tensor(SIG[:], SIG[:], BOTH[:], ALU.mult))
                link(dve.tensor_reduce(M[:, 0, :], SIG[:], AX.X, ALU.add))
                link(dve.tensor_scalar(M[:, 1, :], M[:, 0, :], 1e-9, None, ALU.is_gt))
                link(dve.tensor_scalar(M[:, 0, :], M[:, 0, :], 1e-9, None, ALU.add))
                link(dve.reciprocal(M[:, 2, :], M[:, 0, :]))
                link(dve.tensor_tensor(M[:, 2, :], M[:, 2, :], M[:, 1, :], ALU.mult))
                link(dve.tensor_scalar(M[:, 1, :], M[:, 1, :], -0.5, 0.5, ALU.mult, ALU.add))
                link(dve.tensor_tensor(SIG[:], SIG[:], M[:, 2, :].unsqueeze(2).broadcast_to([P, T, NE]), ALU.mult))
                link(dve.tensor_tensor(BOTH[:], BOTH[:], M[:, 1, :].unsqueeze(2).broadcast_to([P, T, NE]), ALU.mult))
                dve.tensor_tensor(BOTH[:], BOTH[:], SIG[:], ALU.add).then_inc(gates_ready, 1)
                dve.sem_inc(added, 1)
                dve.wait_ge(gates_turned, 1)
                dve.tensor_copy(GT[:], PS[0:NE, 2:6, :].rearrange("p a b -> p (a b)")).then_inc(gates_copied, 1)
                with dve.Fori(0, XT_COLS // 512) as i:
                    for u, (kind, e, m) in enumerate(units):
                        dve.wait_ge(activated, i * NU + u + 1)
                        if kind == "s":
                            dve.scalar_tensor_tensor(HB[:, u % 2, :], PS[:, PAIR + 2 * (u % 2) + 1, :], 1.0 / NS,
                                                     A1[:, u % 2, :], ALU.mult, ALU.mult).then_inc(h_full, 1)
                        else:
                            dve.wait_ge(gate_mm, i * NE + e + 1)
                            dve.tensor_tensor(HB[:, u % 2, :], PS[:, GATE + e % 2, :], A1[:, u % 2, :],
                                              ALU.mult).then_inc(h_full, 1)
                        if u >= 3:
                            dve.wait_ge(second_mm, i * NU + u - 2)
                        dve.wait_ge(h_full, i * NU + u + 1)
                        dve.tensor_copy(HP[0][:, u % 3, :], HB[:, u % 2, :]).then_inc(h_high, 1)
                        dve.wait_ge(h_high, i * NU + u + 1)
                        dve.tensor_tensor(HP[1][:, u % 3, :], HB[:, u % 2, :], HP[0][:, u % 3, :].bitcast(F32),
                                          ALU.subtract).then_inc(h_ready, 1)
                    dve.wait_ge(second_mm, (i + 1) * NU)
                    for f in range(2):
                        xs = XT[:, f, bass.ds(i * 512, 512)]
                        dve.scalar_tensor_tensor(xs, PS[:, OUT + f, :], 1.0 / (NS + TOP_K), xs,
                                                 ALU.mult, ALU.add).then_inc(added, 1)
                dve.wait_ge(added, 2 * (XT_COLS // 512) + 1)


def gated_experts(nc, gate_w, gate_b, time_w, time_b, ew1, ew2, sw1, sw2, b1, b2, cond_t, XT, ident, out):
    NE = ew1.shape[0]
    HT = FF // P
    L1_3 = S // 3
    with ExitStack() as ctx:
        def sb(name, shape, dt=F32):
            return ctx.enter_context(nc.sbuf_tensor(name, shape, dt))

        def sem(name):
            return ctx.enter_context(nc.semaphore(name))

        WN = 2 * FF + HT * D
        RAW = sb("e_weights_sb", [P, 2, WN])
        WP = [sb(f"e_weights_{n}", [P, 2, WN], F32R) for n in ("high", "low")]
        XP = [sb(f"x_part3_{n}", [P, 2, XT_COLS], F32R) for n in ("high", "low")]
        B1 = sb("e_b1", [P, NE + 1, HT])
        B2 = sb("e_b2", [P, NE + 1, 2])
        GW = sb("gate_w_sb", [P, 6, NE])
        TW = sb("time_w_sb", [P, 2, 2 * NE])
        GB = sb("gate_b_sb", [B, NE])
        TB = sb("time_b_sb", [B, 2 * NE])
        cond = sb("cond_g", [P, 2, B])
        SC = sb("silu_cond", [P, 2, B])
        SM = sb("range_sums", [P, 3, 2, B])
        GI = sb("gate_in", [P, 3, 2, B])
        LG = sb("gate_logits", [B, NE])
        MOD = sb("modulation", [B, 2 * NE])
        rank = sb("rank3", [B, NE])
        T0 = sb("g_t0", [B, NE])
        T1 = sb("g_t1", [B, NE])
        BOTH = sb("g_picked", [B, NE])
        WS = sb("g_spoiled", [B, NE])
        M = sb("g_m", [B, 4])
        BD = sb("block_diag", [B, B, NE])
        ones = sb("ones", [B, P])
        WB = sb("weights_all", [P, B, NE])
        A1 = sb("activated3", [P, 4, 512])
        HP = [sb(f"hidden3_{n}", [P, 4, 512], F32R) for n in ("high", "low")]
        Y = sb("weighted_out", [P, 2, 512])
        PS = ctx.enter_context(nc.psum_tensor("ps3", [P, 8, 512], F32))

        w_in = [sem("e_weights_0"), sem("e_weights_1")]
        b_in, g_in, silu_done = sem("e_biases"), sem("g_in"), sem("silu_done")
        step, gate_in, gate_mm, ready, exped, diag, spread = (
            sem("g_step"), sem("gate_in_s"), sem("gate_mm3"), sem("logits_ready"), sem("exped"), sem("diag"), sem("spread"))
        x_split, w_high, w_split = sem("x_split3"), sem("w_high"), sem("w_split3")
        first_mm, activated, h_ready, second_mm, weighted, summed, stored = (
            sem("first_mm3"), sem("activated_s"), sem("hidden_ready3"), sem("second_mm3"), sem("weighted"),
            sem("summed"), sem("stored"))

        bounds = (0, L1_3, 2 * L1_3, S)
        order = (NE,) + tuple(range(NE))
        thirds = {e: (0, 1, 2) for e in order}
        thirds[1], thirds[2] = (0, 2), (1, 2)
        chunks_before = [2 * sum(len(thirds[e]) for e in order[:n]) for n in range(NE + 2)]
        SPLITS = 16
        PIECE = WN // 2 // (SPLITS // 2)
        OUT, FIRST = 0, 4

        def cols(third, i):
            n = (bounds[third + 1] - bounds[third]) * B // 2
            return bass.ds(i * n + bounds[third] * B, n), n

        def w1(part, n, k, m):
            at = k * FF + m * P
            return WP[part][:, n % 2, at:at + P]

        def w2(part, n, m, f):
            at = 2 * FF + m * D + f * P
            return WP[part][:, n % 2, at:at + P]

        with nc.Block() as block:
            @block.sync
            def _(sp):
                sp.dma_start(GW[:], gate_w.rearrange("(k p) n -> p k n", p=P)).then_inc(g_in, 16)
                sp.dma_start(TW[:], time_w.rearrange("(k p) n -> p k n", p=P)).then_inc(g_in, 16)
                sp.dma_start(cond[:], cond_t.rearrange("(k p) b -> p k b", p=P)).then_inc(g_in, 16)
                sp.dma_start(GB[:], gate_b.rearrange("(a n) -> a n", a=1).broadcast_to([B, NE])).then_inc(g_in, 16)
                sp.dma_start(TB[:], time_b.rearrange("(a n) -> a n", a=1).broadcast_to([B, 2 * NE])).then_inc(g_in, 16)
                sp.dma_start(B1[:], b1).then_inc(b_in, 16)
                sp.dma_start(B2[:], b2).then_inc(b_in, 16)
                for n, e in enumerate(order):
                    if n >= 2:
                        sp.wait_ge(w_split, (n - 2) * 2 * SPLITS + 1)
                    first, second = (ew1[e], ew2[e]) if e < NE else (sw1, sw2)
                    for src, a, z in ((first, 0, 2 * FF), (second, 2 * FF, WN)):
                        rows = src.rearrange("(k p) n -> p k n", p=P)
                        sp.dma_start(RAW[:, n % 2, a:z].rearrange("p (k n) -> p k n", k=rows.shape[1]), rows
                                     ).then_inc(w_in[n % 2], 16)
                with sp.Fori(0, 2) as i:
                    for q, third in enumerate(thirds[order[NE]]):
                        sp.wait_ge(summed, i * 2 * 3 + 2 * (chunks_before[NE] + q + 1) + 1)
                        at, _n = cols(third, i)
                        sp.dma_start(out.rearrange("(k p) n -> p k n", p=P)[:, :, at], XT[:, :, at]).then_inc(stored, 16)
                sp.wait_ge(stored, 16 * 6)

            @block.tensor
            def _(pe):
                pe.wait_ge(g_in, 80)
                pe.wait_ge(silu_done, 1)
                for k in range(2):
                    pe.matmul(PS[0:B, 0, 0:2 * NE], SC[:, k, :], TW[:, k, :], start=(k == 0), stop=(k == 1))
                pe.wait_ge(gate_in, 1)
                for k in range(6):
                    mm = pe.matmul(PS[0:B, 1, 0:NE], GI[:, k // 2, k % 2, :], GW[:, k, :], start=(k == 0), stop=(k == 5))
                mm.then_inc(gate_mm, 1)
                pe.wait_ge(diag, 1)
                pe.matmul(PS[:, 2, 0:B * NE], ones[:], BD[:].rearrange("p b e -> p (b e)"),
                          start=True, stop=True).then_inc(spread, 1)
                pe.wait_ge(x_split, 2)
                for n, e in enumerate(order):
                    units = [(q, third, m) for q, third in enumerate(thirds[e]) for m in range(HT)]
                    NU, NQ, CB = len(units), len(thirds[e]), chunks_before[n]
                    pe.wait_ge(w_split, n * 2 * SPLITS + 1)
                    with pe.Fori(0, 2) as i:
                        def second(u):
                            q, third, m = units[u]
                            _at, width = cols(third, i)
                            if m == 0:
                                pe.wait_ge(summed, i * 2 * NQ + 2 * (CB + max(q - 1, 0)) + 1)
                            pe.wait_ge(h_ready, i * NU + CB * HT + u + 1)
                            for f in range(2):
                                for wp, hp in PRODUCTS:
                                    mm = pe.matmul(PS[:, OUT + 2 * (q % 2) + f, 0:width], w2(wp, n, m, f), HP[hp][:, u % 4, 0:width],
                                                   start=(m == 0 and wp + hp == 0), stop=(m == HT - 1), skip_group_check=True)
                            mm.then_inc(second_mm, 1)

                        for u, (q, third, m) in enumerate(units):
                            at, width = cols(third, i)
                            if u >= 4:
                                pe.wait_ge(activated, i * NU + CB * HT + u - 3)
                            for k in range(2):
                                for wp, xp in PRODUCTS:
                                    mm = pe.matmul(PS[:, FIRST + u % 4, 0:width], w1(wp, n, k, m), XP[xp][:, k, at],
                                                   start=(k == 0 and wp + xp == 0), stop=(k == 1), skip_group_check=True)
                            mm.then_inc(first_mm, 1)
                            if u >= 2:
                                second(u - 2)
                        second(NU - 2)
                        second(NU - 1)

            @block.scalar
            def _(act):
                act.wait_ge(g_in, 80)
                act.activation(SC[:], cond[:], ACT.Silu).then_inc(silu_done, 1)
                act.activation(XP[0][:], XT[:, :, 0:XT_COLS], ACT.Copy).then_inc(x_split, 1)
                act.wait_ge(w_in[0], 32)
                act.activation(WP[0][:, 0, :], RAW[:, 0, :], ACT.Copy).then_inc(w_high, 1)
                act.wait_ge(ready, 1)
                act.activation(LG[:], LG[:], ACT.Exp, bias=M[:, 1:2], accum_out=M[:, 2:3]).then_inc(exped, 1)
                act.wait_ge(b_in, 32)
                for n, e in enumerate(order):
                    units = [(q, third, m) for q, third in enumerate(thirds[e]) for m in range(HT)]
                    NU, CB = len(units), chunks_before[n]
                    with act.Fori(0, 2) as i:
                        act.wait_ge(second_mm, i * NU + CB * HT + 1)
                        for u, (q, third, m) in enumerate(units):
                            _at, width = cols(third, i)
                            act.wait_ge(first_mm, i * NU + CB * HT + u + 1)
                            if u >= 4:
                                act.wait_ge(second_mm, i * NU + CB * HT + u - 3 + 1)
                            for dst in (HP[0], A1):
                                ins = act.activation(dst[:, u % 4, 0:width], PS[:, FIRST + u % 4, 0:width],
                                                     ACT.Gelu_apprx_tanh, bias=B1[:, e, m:m + 1])
                            ins.then_inc(activated, 1)

            @block.vector
            def _(dve):
                count = [0]

                def link(ins):
                    count[0] += 1
                    ins.then_inc(step, 1)
                    dve.wait_ge(step, count[0])

                for e in range(NE):
                    dve.memset(rank[:, e:e + 1], float(NE - e))
                dve.memset(ones[:], 1.0)
                x4 = XT[:, :, 0:XT_COLS].rearrange("p k (t b) -> p k b t", b=B)
                for r in range(3):
                    ins = dve.tensor_reduce(SM[:, r, :, :], x4[:, :, :, bounds[r]:bounds[r + 1]], AX.X, ALU.add)
                link(ins)
                both = float(S - L1_3)
                dve.tensor_tensor(GI[:, 1, :, :], SM[:, 0, :, :], SM[:, 2, :, :], ALU.add)
                dve.tensor_tensor(GI[:, 2, :, :], SM[:, 1, :, :], SM[:, 2, :, :], ALU.add)
                link(dve.tensor_tensor(GI[:, 0, :, :], SM[:, 0, :, :], SM[:, 1, :, :], ALU.add))
                link(dve.tensor_tensor(GI[:, 0, :, :], GI[:, 0, :, :], SM[:, 2, :, :], ALU.add))
                link(dve.tensor_scalar(GI[:, 0, :, :], GI[:, 0, :, :], 1.0 / S, None, ALU.mult))
                dve.tensor_scalar(GI[:, 1:3, :, :], GI[:, 1:3, :, :], 1.0 / both, None, ALU.mult).then_inc(gate_in, 1)
                dve.wait_ge(gate_mm, 1)
                dve.wait_ge(g_in, 80)
                link(dve.tensor_tensor(LG[:], PS[0:B, 1, 0:NE], GB[:], ALU.add))
                link(dve.tensor_tensor(MOD[:], PS[0:B, 0, 0:2 * NE], TB[:], ALU.add))
                link(dve.scalar_tensor_tensor(LG[:], MOD[:, 0:NE], 1.0, LG[:], ALU.add, ALU.mult))
                link(dve.tensor_tensor(LG[:], LG[:], MOD[:, NE:2 * NE], ALU.add))
                link(dve.tensor_reduce(M[:, 0:1], LG[:], AX.X, ALU.max))
                dve.tensor_scalar(M[:, 1:2], M[:, 0:1], -1.0, None, ALU.mult).then_inc(ready, 1)
                dve.wait_ge(exped, 1)
                link(dve.reciprocal(M[:, 3:4], M[:, 2:3]))
                link(dve.tensor_scalar(LG[:], LG[:], M[:, 3:4], None, ALU.mult))
                link(dve.tensor_copy(WS[:], LG[:]))
                rows = [v[:].unsqueeze(1) for v in (WS, BOTH, T0, T1, rank)]
                top_two(dve, link, rows[0], rows[1], rows[2:4], M[:, 0:1], rows[4], [B, 1, NE])
                link(dve.tensor_tensor(BOTH[:], BOTH[:], LG[:], ALU.mult))
                link(dve.tensor_reduce(M[:, 0:1], BOTH[:], AX.X, ALU.add))
                link(dve.tensor_scalar(M[:, 0:1], M[:, 0:1], 1e-8, None, ALU.add))
                link(dve.reciprocal(M[:, 3:4], M[:, 0:1]))
                link(dve.tensor_scalar(BOTH[:], BOTH[:], M[:, 3:4], None, ALU.mult))
                dve.tensor_tensor(BD[:], BOTH[:].unsqueeze(1).broadcast_to([B, B, NE]),
                                  ident[0:B, 0:B].unsqueeze(2).broadcast_to([B, B, NE]), ALU.mult).then_inc(diag, 1)
                dve.wait_ge(spread, 1)
                link(dve.tensor_copy(WB[:].rearrange("p b e -> p (b e)"), PS[:, 2, 0:B * NE]))
                dve.sem_inc(summed, 1)
                dve.sem_inc(second_mm, 1)
                dve.wait_ge(x_split, 1)
                dve.tensor_tensor(XP[1][:], XT[:, :, 0:XT_COLS], XP[0][:].bitcast(F32), ALU.subtract).then_inc(x_split, 1)

                def split_weights(n, i, s, done):
                    at = bass.ds(i * (WN // 2) + s // 2 * PIECE, PIECE)
                    high, low = (w[:, n % 2, at] for w in WP)
                    if s == 0:
                        dve.wait_ge(w_in[n % 2], 32 * (n // 2 + 1))
                    if s % 2 == 0:
                        dve.tensor_copy(high, RAW[:, n % 2, at]).then_inc(w_split, 1)
                    else:
                        dve.wait_ge(w_split, done + s)
                        dve.tensor_tensor(low, RAW[:, n % 2, at], high.bitcast(F32), ALU.subtract).then_inc(w_split, 1)

                dve.wait_ge(w_high, 1)
                dve.tensor_tensor(WP[1][:, 0, :], RAW[:, 0, :], WP[0][:, 0, :].bitcast(F32), ALU.subtract).then_inc(w_split, 1)
                dve.wait_ge(b_in, 32)
                for n, e in enumerate(order):
                    units = [(q, third, m) for q, third in enumerate(thirds[e]) for m in range(HT)]
                    NU, NQ, CB = len(units), len(thirds[e]), chunks_before[n]
                    with dve.Fori(0, 2) as i:
                        def add(q, third):
                            at, width = cols(third, i)
                            dve.wait_ge(second_mm, i * NU + CB * HT + HT * (q + 1) + 1)
                            for f in range(2):
                                o, xs = PS[:, OUT + 2 * (q % 2) + f, 0:width], XT[:, f, at]
                                if e == NE:
                                    dve.scalar_tensor_tensor(xs, o, B2[:, e, f:f + 1], xs, ALU.add, ALU.add).then_inc(summed, 1)
                                else:
                                    dve.scalar_tensor_tensor(
                                        Y[:, f, 0:width].rearrange("p (t b) -> p t b", b=B),
                                        o.rearrange("p (t b) -> p t b", b=B), B2[:, e, f:f + 1],
                                        WB[:, :, e].unsqueeze(1).broadcast_to([P, width // B, B]),
                                        ALU.add, ALU.mult).then_inc(weighted, 1)
                            if e < NE:
                                before = 2 * (CB - chunks_before[1] + q)
                                for f in range(2):
                                    xs = XT[:, f, at]
                                    dve.wait_ge(weighted, i * 2 * NQ + before + f + 1)
                                    dve.tensor_tensor(xs, xs, Y[:, f, 0:width], ALU.add).then_inc(summed, 1)

                        for u, (q, third, m) in enumerate(units):
                            _at, width = cols(third, i)
                            dve.wait_ge(activated, i * NU + CB * HT + u + 1)
                            dve.tensor_tensor(HP[1][:, u % 4, 0:width], A1[:, u % 4, 0:width],
                                              HP[0][:, u % 4, 0:width].bitcast(F32), ALU.subtract).then_inc(h_ready, 1)
                            if n < NE and u < SPLITS:
                                split_weights(n + 1, i, u, i * SPLITS + n * 2 * SPLITS + 1)
                            if q and m == 2:
                                add(q - 1, thirds[e][q - 1])
                        add(NQ - 1, thirds[e][NQ - 1])


def layers(nc, x, cond_t, l0, l1, l2, l3, eye, out):
    with ExitStack() as ctx:
        XT = ctx.enter_context(nc.sbuf_tensor("xt", [P, 2, XT_COLS + CH * B], F32))
        ident = ctx.enter_context(nc.sbuf_tensor("ident", [P, P], F32))
        ident_bf = ctx.enter_context(nc.sbuf_tensor("ident_bf", [P, P], BF16))
        eye_in, ident_ready = ctx.enter_context(nc.semaphore("eye_in")), ctx.enter_context(nc.semaphore("ident_ready"))
        with nc.Block() as block:
            @block.sync
            def _(sp):
                sp.dma_start(ident[:], eye).then_inc(eye_in, 16)

            @block.vector
            def _(dve):
                dve.wait_ge(eye_in, 16)
                dve.tensor_copy(ident_bf[:], ident[:]).then_inc(ident_ready, 1)
                dve.wait_ge(ident_ready, 1)

        hyperbolic_block(nc, x, cond_t, *l0, XT, ident, ident_bf)
        w_router, router_bias, w_experts = l2
        with ExitStack() as held:
            parts = [held.enter_context(nc.sbuf_tensor(f"l2_weights_{n}", [P, L2_COLS], F32R)) for n in ("high", "low")]
            gru(nc, *l1, cond_t, XT, ident_bf, w_experts, parts, ident)
            shared_and_routed(nc, w_router, router_bias, parts, cond_t, XT, ident)
        gated_experts(nc, *l3, cond_t, XT, ident, out)


def kernel(**inputs):
    from concourse import bacc
    from concourse.bass_utils import run_bass_kernel_spmd

    def own(name):
        return np.asarray(inputs[name])

    def joined(prefix, names):
        return np.concatenate([own(prefix + n) for n in names], axis=-1)

    def turned(name):
        return own(name).swapaxes(-1, -2)

    def row_tiles(w):
        return w.reshape(len(w), -1, P, w.shape[-1]).transpose(2, 0, 1, 3).reshape(P, -1)

    def features_first(prefix, routed, shared):
        both = np.concatenate([own(prefix + routed), own(prefix + shared)[None]])
        return both.reshape(len(both), -1, P).transpose(2, 0, 1)

    a, g, m, e = "L0_cond_", "L1_cond_", "L2_cond_", "L3_cond_"
    groups = {
        "x": [own("x")], "cond_t": [turned("cond_1024")],
        "l0": [joined(a, ("w_q", "w_k", "w_v")), joined(a, ("b_q", "b_k", "b_v"))]
              + [own(a + n) for n in ("w_o", "b_o", "w_f1", "b_f1", "w_f2", "b_f2", "w_ada", "b_ada")],
        "l1": [joined(g, ("W_z", "W_r", "W")), joined(g, ("U_z", "U_r", "U")), joined(g, ("C_z", "C_r", "C")),
               joined(g, ("b_z", "b_r", "b"))],
        "l2": [turned(m + "W_router"), own(m + "router_bias"),
               np.concatenate([row_tiles(turned(m + n)) for n in ("s_w1", "s_w3", "s_w2", "r_w1", "r_w2")], axis=1)],
        "l3": [own(e + n) for n in ("gate_w", "gate_b", "time_w", "time_b", "ew1", "ew2", "sw1", "sw2")]
              + [features_first(e, "eb1", "sb1"), features_first(e, "eb2", "sb2")],
        "eye": [np.eye(P, dtype=np.float32)],
    }
    nc = bacc.Bacc("TRN2", target_bir_lowering=False, num_devices=1)
    arrays, args = {}, {}
    for group, values in groups.items():
        args[group] = []
        for n, v in enumerate(values):
            name = f"in_{group}_{n}"
            arrays[name] = np.ascontiguousarray(v)
            args[group].append(nc.dram_tensor(name, arrays[name].shape, mybir.dt.from_np(arrays[name].dtype),
                                              kind="ExternalInput").ap())
    out = nc.dram_tensor("out_t", (D, XT_COLS), F32, kind="ExternalOutput").ap()
    layers(nc, args["x"][0], args["cond_t"][0], args["l0"], args["l1"], args["l2"], args["l3"], args["eye"][0], out)
    r = run_bass_kernel_spmd(nc, [arrays], core_ids=[0])
    return r.results[0]["out_t"].reshape(D, S, B).transpose(2, 1, 0)
```
